# Optimizing a Trainium2 kernel written in Bass

```python
import numpy as np
import jax
import jax.numpy as jnp

def _softmax(x, axis=-1):
    return jax.nn.softmax(x, axis=axis)

def _gelu(x):
    return jax.nn.gelu(x, approximate=True)

def _silu(x):
    return jax.nn.silu(x)

def _sigmoid(x):
    return jax.nn.sigmoid(x)

def _layernorm(x, axis=-1, eps=1e-05):
    m = jnp.mean(x, axis=axis, keepdims=True)
    v = jnp.var(x, axis=axis, keepdims=True)
    return (x - m) / jnp.sqrt(v + eps)

def _scatter_add(tgt, idx, src, axis=0):
    return tgt.at[idx].add(src)

def _segment_sum(src, seg, n):
    return jax.ops.segment_sum(src, seg, n)
kernel_name = 'mk_lm_tower_d1_tok_ids1024_r4_3b31d1'

def setup_inputs(seed: int=0):
    np.random.seed(seed)
    _w = jnp.asarray

    def _rec_inputs():
        import jax
        import jax.numpy as jnp
        _rk = jax.random.key(seed)
        x = jax.random.randint(jax.random.fold_in(_rk, 1), (8, 512), 0, 12564, jnp.int32)
        return x
    x = _rec_inputs()

    def _L0_tok_setup():
        import jax, jax.numpy as jnp
        import numpy as np
        INPUT_SIZE = 512
        EMBED_SIZE = 256
        VOCAB_SIZE = 50257
        BATCH_SIZE = 8

        def positional_encoding(seq_len, d, n=10000.0):
            pos = jnp.arange(seq_len, dtype=jnp.float32)[:, None]
            i = jnp.arange(d // 2, dtype=jnp.float32)[None, :]
            den = jnp.power(n, 2.0 * i / d)
            ang = pos / den
            P = jnp.zeros((seq_len, d), dtype=jnp.float32)
            P = P.at[:, 0::2].set(jnp.sin(ang))
            P = P.at[:, 1::2].set(jnp.cos(ang))
            return P
        key = jax.random.key(seed)
        k1, k2 = jax.random.split(key)
        x = jax.random.randint(k1, (BATCH_SIZE, INPUT_SIZE), 0, VOCAB_SIZE, dtype=jnp.int64 if jax.config.jax_enable_x64 else jnp.int32)
        W = jax.random.normal(k2, (VOCAB_SIZE, EMBED_SIZE), dtype=jnp.float32)
        return {'x': x, 'W': W}
    _L0_tok_all = _L0_tok_setup()
    _L0_tok_in = {k: v for k, v in _L0_tok_all.items() if k in ('W',)}
    del _L0_tok_all

    def _L0_attn_setup():
        import jax, jax.numpy as jnp
        import numpy as np
        D_MODEL = 256
        N_HEADS = 16
        D_K = D_MODEL // N_HEADS

        def _rope_cache(T, dtype):
            half = D_K // 2
            freq = 1.0 / 10000.0 ** (2.0 * jnp.arange(half, dtype=dtype) / D_K)
            angles = jnp.arange(T, dtype=dtype)[:, None] * freq[None, :]
            return (jnp.cos(angles), jnp.sin(angles))

        def _apply_rope(x, cos, sin):
            half = x.shape[-1] // 2
            x1, x2 = (x[..., :half], x[..., half:])
            return jnp.concatenate([x1 * cos - x2 * sin, x1 * sin + x2 * cos], axis=-1)
        key = jax.random.key(seed)
        ks = jax.random.split(key, 9)
        s = 0.02
        return {'x': jax.random.normal(ks[0], (4, 512, D_MODEL), dtype=jnp.float32), 'WQ_w': jax.random.normal(ks[1], (D_MODEL, D_MODEL), dtype=jnp.float32) * s, 'WQ_b': jax.random.normal(ks[2], (D_MODEL,), dtype=jnp.float32) * s, 'WK_w': jax.random.normal(ks[3], (D_MODEL, D_MODEL), dtype=jnp.float32) * s, 'WK_b': jax.random.normal(ks[4], (D_MODEL,), dtype=jnp.float32) * s, 'WV_w': jax.random.normal(ks[5], (D_MODEL, D_MODEL), dtype=jnp.float32) * s, 'WV_b': jax.random.normal(ks[6], (D_MODEL,), dtype=jnp.float32) * s, 'Wo_w': jax.random.normal(ks[7], (D_MODEL, D_MODEL), dtype=jnp.float32) * s, 'Wo_b': jax.random.normal(ks[8], (D_MODEL,), dtype=jnp.float32) * s}
    _L0_attn_all = _L0_attn_setup()
    _L0_attn_in = {k: v for k, v in _L0_attn_all.items() if k in ('WQ_w', 'WQ_b', 'WK_w', 'WK_b', 'WV_w', 'WV_b', 'Wo_w', 'Wo_b')}
    del _L0_attn_all

    def _L0_ffn_setup():
        import jax, jax.numpy as jnp
        import numpy as np
        D = 256
        F = 256
        E = 8
        K = 2
        B, T = (2, 512)

        def _moe_forward(x, router_w, w1, w2, shared_gate_up, shared_down, shared_gate_w):
            b, t, d = x.shape
            xf = x.reshape(-1, d)
            n = xf.shape[0]
            logits = xf @ router_w
            probs = jax.nn.softmax(logits, axis=-1)
            topw, topi = jax.lax.top_k(probs, K)
            combine = jnp.zeros((n, E), dtype=probs.dtype).at[jnp.arange(n)[:, None], topi].add(topw)
            h = jax.nn.silu(jnp.einsum('nd,edf->nef', xf, w1))
            ye = jnp.einsum('nef,efd->ned', h, w2)
            routed = jnp.einsum('ne,ned->nd', combine, ye)
            gu = xf @ shared_gate_up
            gate, up = (gu[:, :F], gu[:, F:])
            shared = jax.nn.silu(gate) * up @ shared_down
            shared = jax.nn.sigmoid(xf @ shared_gate_w) * shared
            return (routed + shared).reshape(b, t, d)
        key = jax.random.key(seed)
        ks = jax.random.split(key, 7)
        std = 0.02
        x = jax.random.normal(ks[0], (B, T, D), dtype=jnp.float32)
        router_w = jax.random.normal(ks[1], (D, E), dtype=jnp.float32) * std
        w1 = jax.random.normal(ks[2], (E, D, F), dtype=jnp.float32) * std
        w2 = jax.random.normal(ks[3], (E, F, D), dtype=jnp.float32) * std
        shared_gate_up = jax.random.normal(ks[4], (D, 2 * F), dtype=jnp.float32) * std
        shared_down = jax.random.normal(ks[5], (F, D), dtype=jnp.float32) * std
        shared_gate_w = jax.random.normal(ks[6], (D, 1), dtype=jnp.float32) * std
        return {'x': x, 'router_w': router_w, 'w1': w1, 'w2': w2, 'shared_gate_up': shared_gate_up, 'shared_down': shared_down, 'shared_gate_w': shared_gate_w}
    _L0_ffn_all = _L0_ffn_setup()
    _L0_ffn_in = {k: v for k, v in _L0_ffn_all.items() if k in ('router_w', 'w1', 'w2', 'shared_gate_up', 'shared_down', 'shared_gate_w')}
    del _L0_ffn_all
    return {'x': x, 'L0_tok_W': _L0_tok_in['W'], 'L0_attn_WQ_w': _L0_attn_in['WQ_w'], 'L0_attn_WQ_b': _L0_attn_in['WQ_b'], 'L0_attn_WK_w': _L0_attn_in['WK_w'], 'L0_attn_WK_b': _L0_attn_in['WK_b'], 'L0_attn_WV_w': _L0_attn_in['WV_w'], 'L0_attn_WV_b': _L0_attn_in['WV_b'], 'L0_attn_Wo_w': _L0_attn_in['Wo_w'], 'L0_attn_Wo_b': _L0_attn_in['Wo_b'], 'L0_ffn_router_w': _L0_ffn_in['router_w'], 'L0_ffn_w1': _L0_ffn_in['w1'], 'L0_ffn_w2': _L0_ffn_in['w2'], 'L0_ffn_shared_gate_up': _L0_ffn_in['shared_gate_up'], 'L0_ffn_shared_down': _L0_ffn_in['shared_down'], 'L0_ffn_shared_gate_w': _L0_ffn_in['shared_gate_w']}

def reference(x, L0_tok_W, L0_attn_WQ_w, L0_attn_WQ_b, L0_attn_WK_w, L0_attn_WK_b, L0_attn_WV_w, L0_attn_WV_b, L0_attn_Wo_w, L0_attn_Wo_b, L0_ffn_router_w, L0_ffn_w1, L0_ffn_w2, L0_ffn_shared_gate_up, L0_ffn_shared_down, L0_ffn_shared_gate_w):
    import jax
    import jax.numpy as jnp

    def _L0_tok_ref(x, W):
        import jax, jax.numpy as jnp
        import numpy as np
        INPUT_SIZE = 512
        EMBED_SIZE = 256
        VOCAB_SIZE = 50257
        BATCH_SIZE = 8

        def positional_encoding(seq_len, d, n=10000.0):
            pos = jnp.arange(seq_len, dtype=jnp.float32)[:, None]
            i = jnp.arange(d // 2, dtype=jnp.float32)[None, :]
            den = jnp.power(n, 2.0 * i / d)
            ang = pos / den
            P = jnp.zeros((seq_len, d), dtype=jnp.float32)
            P = P.at[:, 0::2].set(jnp.sin(ang))
            P = P.at[:, 1::2].set(jnp.cos(ang))
            return P
        emb = W[x]
        pe = positional_encoding(INPUT_SIZE, EMBED_SIZE)
        return emb + pe[None, :, :]

    def _L0_attn_ref(x, WQ_w, WQ_b, WK_w, WK_b, WV_w, WV_b, Wo_w, Wo_b):
        import jax, jax.numpy as jnp
        import numpy as np
        D_MODEL = 256
        N_HEADS = 16
        D_K = D_MODEL // N_HEADS

        def _rope_cache(T, dtype):
            half = D_K // 2
            freq = 1.0 / 10000.0 ** (2.0 * jnp.arange(half, dtype=dtype) / D_K)
            angles = jnp.arange(T, dtype=dtype)[:, None] * freq[None, :]
            return (jnp.cos(angles), jnp.sin(angles))

        def _apply_rope(x, cos, sin):
            half = x.shape[-1] // 2
            x1, x2 = (x[..., :half], x[..., half:])
            return jnp.concatenate([x1 * cos - x2 * sin, x1 * sin + x2 * cos], axis=-1)
        B, T, D = x.shape

        def proj(w, b):
            y = jnp.einsum('btd,ed->bte', x, w) + b
            return y.reshape(B, T, N_HEADS, D_K).transpose(0, 2, 1, 3)
        q = proj(WQ_w, WQ_b)
        k = proj(WK_w, WK_b)
        v = proj(WV_w, WV_b)
        cos, sin = _rope_cache(T, x.dtype)
        q = _apply_rope(q, cos, sin)
        k = _apply_rope(k, cos, sin)
        scores = jnp.einsum('bhqd,bhkd->bhqk', q, k) / jnp.sqrt(jnp.asarray(D_K, x.dtype))
        causal = jnp.tril(jnp.ones((T, T), dtype=bool))
        scores = jnp.where(causal[None, None, :, :], scores, -jnp.inf)
        attn = jax.nn.softmax(scores, axis=-1)
        out = jnp.einsum('bhqk,bhkd->bhqd', attn, v)
        out = out.transpose(0, 2, 1, 3).reshape(B, T, D)
        return jnp.einsum('btd,ed->bte', out, Wo_w) + Wo_b

    def _L0_ffn_ref(x, router_w, w1, w2, shared_gate_up, shared_down, shared_gate_w):
        import jax, jax.numpy as jnp
        import numpy as np
        D = 256
        F = 256
        E = 8
        K = 2
        B, T = (2, 512)

        def _moe_forward(x, router_w, w1, w2, shared_gate_up, shared_down, shared_gate_w):
            b, t, d = x.shape
            xf = x.reshape(-1, d)
            n = xf.shape[0]
            logits = xf @ router_w
            probs = jax.nn.softmax(logits, axis=-1)
            topw, topi = jax.lax.top_k(probs, K)
            combine = jnp.zeros((n, E), dtype=probs.dtype).at[jnp.arange(n)[:, None], topi].add(topw)
            h = jax.nn.silu(jnp.einsum('nd,edf->nef', xf, w1))
            ye = jnp.einsum('nef,efd->ned', h, w2)
            routed = jnp.einsum('ne,ned->nd', combine, ye)
            gu = xf @ shared_gate_up
            gate, up = (gu[:, :F], gu[:, F:])
            shared = jax.nn.silu(gate) * up @ shared_down
            shared = jax.nn.sigmoid(xf @ shared_gate_w) * shared
            return (routed + shared).reshape(b, t, d)
        return _moe_forward(x, router_w, w1, w2, shared_gate_up, shared_down, shared_gate_w)
    h = _L0_tok_ref(x, L0_tok_W)
    h = h + _L0_attn_ref(_layernorm(h, axis=-1), L0_attn_WQ_w, L0_attn_WQ_b, L0_attn_WK_w, L0_attn_WK_b, L0_attn_WV_w, L0_attn_WV_b, L0_attn_Wo_w, L0_attn_Wo_b)
    h = h + _L0_ffn_ref(_layernorm(h, axis=-1), L0_ffn_router_w, L0_ffn_w1, L0_ffn_w2, L0_ffn_shared_gate_up, L0_ffn_shared_down, L0_ffn_shared_gate_w)
    return h

_drawn_inputs = setup_inputs


def setup_inputs(seed=0):
    import zlib

    import numpy as np

    out = dict(_drawn_inputs(seed))
    spreads = {}
    factors = {'L0_attn_WQ_w': 8.0,
     'L0_attn_WQ_b': 30.336,
     'L0_attn_WK_w': 8.0,
     'L0_attn_WK_b': 39.192,
     'L0_attn_WV_b': 8.0,
     'L0_attn_Wo_b': 3.603,
     'L0_ffn_router_w': 5.966,
     'L0_ffn_w1': 5.178,
     'L0_ffn_w2': 5.152,
     'L0_ffn_shared_gate_up': 7.54,
     'L0_ffn_shared_down': 7.578,
     'L0_ffn_shared_gate_w': 8.0}
    for name, (base, spread) in spreads.items():
        noise = np.random.default_rng([zlib.crc32(name.encode()), seed]).standard_normal(out[name].shape)
        drawn = base * np.exp(spread * noise) if base else spread * noise
        out[name] = jnp.asarray(drawn.astype(out[name].dtype))
    for name, factor in factors.items():
        out[name] = (out[name] * factor).astype(out[name].dtype)
    return out
```

```python
from contextlib import ExitStack

import concourse.bass as bass
from concourse import mybir

F32 = mybir.dt.float32
F32R = mybir.dt.float32r
BF16 = mybir.dt.bfloat16
I32 = mybir.dt.int32
U32 = mybir.dt.uint32
ALU = mybir.AluOpType
ACT = mybir.ActivationFunctionType
AX = mybir.AxisListType

P = 128
NB, T, D = 8, 512, 256
H, DK = 16, 16
E, F = 8, 256
TB, DC = T // P, D // P
HH = 4
HG = H // HH
CH = E + 1
STEPS = 12
LOOP_FIRST = 2
HALF = DK // 2
TERMS_Q = (0, 0, 1, 0, 2, 1)
TERMS_K = (0, 1, 0, 2, 0, 1)
NT = len(TERMS_Q)
KS = NT * DK
KM = KS + 3
LOADS = 2 * NT * 16
EPS = 1e-5
NEG = -3.0e38
SCALE = 1.0 / DK ** 0.5
MAX_FILLS = ((3,), (2,), (0, 1))
NF = HH * len(MAX_FILLS)
ROUND_KEYS = ((0,), (1,), (2, 3))
NR = len(ROUND_KEYS)
MOE_LAST = 4 * CH + 1


def max_fills(i):
    if i >= 8:
        return []
    return [3 * (i // 2) + 2] if i % 2 else [3 * (i // 2), 3 * (i // 2) + 1]


def moe_step(s, i):
    return (-2, STEPS * 3 + i - 3) if s == 0 else (-1, STEPS * (s - 1) + i - 3)


def bank_h_uses():
    uses = []
    for s in range(4):
        for i in range(STEPS):
            d, m = moe_step(s, i)
            if s == 1 and i == 1:
                uses.append(("router", -1, 0))
            if i == 3:
                uses.append(("heads", -1 if s == 0 else 0, (s - 1) % 4))
            if s == 1 and i == 4:
                uses.append(("weights", -1, 0))
            if m == 2:
                uses.append(("spread", d, 0))
            if s and m >= 0 and m % 4 == 3 and m // 4 + 1 < CH:
                uses.append(("spread", d, m // 4 + 1))
            if i == 9:
                uses.append(("maxima", 1 if s == 3 else 0, (s + 1) % 4))
    return uses


class Round:

    def __init__(self, t, fixed=None):
        self.t = t
        n = t if fixed is None else fixed
        self.n = n
        self.nxt = 0 <= n + 1 < NB
        self.att = 0 <= n < NB
        self.epi = 0 <= n - 1 < NB
        self.tail = 0 <= n - 2 < NB
        self.has = {1: self.nxt, 0: self.att, -1: self.epi, -2: self.tail}

    def count(self, per, d, k):
        if isinstance(self.t, int):
            return min(max((self.t + d) * per + k, 0), NB * per)
        assert (LOOP_FIRST + d) * per + k > 0
        return self.t * per + (d * per + k)

    def held(self, eng, per, d, k):
        value = self.count(per, d, k)
        return value if isinstance(value, int) else eng.snap(eng.to_reg(value))


def lm_block_kernel(nc, x, table, pe, cos, sin2, wqkv, bqkv, wo, bo, wr, w1, w2, wgu, wdn, out, loop):
    ctx = ExitStack()
    with ctx:
        def sb(name, shape, dt=F32):
            return ctx.enter_context(nc.sbuf_tensor(name, shape, dt))

        def bank(name, n=1):
            return ctx.enter_context(nc.psum_tensor(name, [P, n, 512], F32))

        def sem(name):
            return ctx.enter_context(nc.semaphore(name))

        parts_dram = nc.dram_tensor("qk_parts", (3, 4, P, T), BF16, kind="Internal").ap()
        base_dram = nc.dram_tensor("pe_plus_bias", (T, D), F32, kind="Internal").ap()

        ident = sb("ident", [P, P])
        identb = sb("identb", [P, P], BF16)
        causal = sb("causal", [P, T], BF16)
        cos_sb = sb("cos_sb", [P, TB, HALF])
        sin_sb = sb("sin_sb", [P, TB, DK])
        bias = sb("bias", [P, 3 * D])
        spread = sb("spread", [P, CH, P], BF16)
        iota8 = sb("iota8", [P, E])
        minus_half = sb("minus_half", [P, TB])
        wqkv_h, wqkv_l = sb("wqkv_h", [P, DC, 3 * D], F32R), sb("wqkv_l", [P, DC, 3 * D], F32R)
        wo_h, wo_l = sb("wo_h", [P, DC, D], F32R), sb("wo_l", [P, DC, D], F32R)
        wr_h, wr_l = sb("wr_h", [P, DC, E + 2], F32R), sb("wr_l", [P, DC, E + 2], F32R)
        w1_h, w1_l = sb("w1_h", [P, DC, E, F], F32R), sb("w1_l", [P, DC, E, F], F32R)
        w2_h, w2_l = sb("w2_h", [P, DC, E, D], F32R), sb("w2_l", [P, DC, E, D], F32R)
        wgu_h, wgu_l = sb("wgu_h", [P, DC, 2 * F], F32R), sb("wgu_l", [P, DC, 2 * F], F32R)
        wdn_h, wdn_l = sb("wdn_h", [P, DC, D], F32R), sb("wdn_l", [P, DC, D], F32R)
        idx, idx_res = sb("idx", [P, TB], I32), sb("idx_res", [P, TB], I32)
        h_in = sb("h_in", [P, TB, D])
        res = sb("res", [P, TB, D])
        h1 = sb("h1", [P, TB, D])
        o_tok = sb("o_tok", [P, TB, D])
        v_new = sb("v_new", [P, TB, D])
        v_aug = sb("v_aug", [P, TB, H, DK + 1])
        stats = sb("stats", [P, TB, 6])
        mv = sb("mv", [P, TB, 2])
        var_eps = sb("var_eps", [P, TB])
        rstd = sb("rstd", [P, TB])
        a_h, a_l = sb("a_h", [P, DC, T], F32R), sb("a_l", [P, DC, T], F32R)
        x2_h, x2_l = sb("x2_h", [P, DC, T], F32R), sb("x2_l", [P, DC, T], F32R)
        hid = sb("hid", [P, 2, T])
        cb = sb("cb", [P, 2, T])
        parts = sb("parts", [P, 3, 4, 2 * P], BF16)
        q_terms = sb("q_terms", [P, HG, HH, T], BF16)
        k_terms = sb("k_terms", [P, HG, HH, T], BF16)
        probs0 = sb("probs0", [P, HH, T])
        probs1 = sb("probs1", [P, HH, 3 * P])
        heads_t = sb("heads_t", [P, T])
        rec = sb("rec", [P, TB, HH])
        scrap = sb("scrap", [P, T], BF16)
        row_max = sb("row_max", [P, TB, HH])
        max_rest = sb("max_rest", [P, TB, HH])
        max_parts = sb("max_parts", [P, TB, 3, HH], BF16)
        max_rows = sb("max_rows", [3 * HH, T], BF16)
        nmax = sb("nmax", [P, TB])
        logit = sb("logit", [P, TB, CH])
        ex = sb("ex", [P, TB, CH])
        esum = sb("esum", [P, TB])
        erec = sb("erec", [P, TB])
        pr = sb("pr", [P, TB, E])
        top8 = sb("top8", [P, TB, 8])
        top_i = sb("top_i", [P, TB, 8], U32)
        top_f = sb("top_f", [P, TB, 2])
        pick = sb("pick", [P, TB, E])
        pick2 = sb("pick2", [P, TB, E])
        den = sb("den", [P, TB])
        cw = sb("cw", [P, TB, CH])
        cw_rest = sb("cw_rest", [P, TB, CH])
        cw_parts = sb("cw_parts", [P, TB, P], BF16)
        cw_rows = sb("cw_rows", [P, T], BF16)

        bank_m = bank("bank_m")
        bank_s = bank("bank_s")
        bank_o = bank("bank_o")
        bank_h = bank("bank_h")
        bank_fg = bank("bank_fg", 2)
        bank_y = bank("bank_y", 2)
        bank_h_bf = bank_h[:, 0, :].bitcast(BF16)

        go = sem("go")
        s_ld = sem("s_ld"); s_cd = sem("s_cd"); s_cp = sem("s_cp"); s_cv = sem("s_cv"); s_cq = sem("s_cq")
        s_wd = [sem("s_wd0"), sem("s_wd1")]
        s_we = [sem("s_we0"), sem("s_we1")]
        s_wh = sem("s_wh"); s_wl = sem("s_wl"); s_ea = sem("s_ea"); s_base = sem("s_base")
        s_tab = sem("s_tab"); s_idx = sem("s_idx"); s_gat = sem("s_gat")
        s_tabr = sem("s_tabr"); s_idxr = sem("s_idxr"); s_gatr = sem("s_gatr")
        s_n1 = sem("s_n1"); s_n1p = sem("s_n1p"); s_n2 = sem("s_n2"); s_n2p = sem("s_n2p")
        s_xt = sem("s_xt"); s_xh = sem("s_xh"); s_xl = sem("s_xl")
        s_qkv = sem("s_qkv"); s_qk = sem("s_qk"); s_vn = sem("s_vn"); s_v = sem("s_v")
        s_rc = sem("s_rc"); s_rs = sem("s_rs"); s_rot = sem("s_rot")
        s_qt = sem("s_qt"); s_ph = sem("s_ph"); s_pr = sem("s_pr"); s_pm = sem("s_pm"); s_pl = sem("s_pl")
        s_pw = sem("s_pw"); s_terms = [sem(f"s_terms{g}") for g in range(HG)]
        s_mf = sem("s_mf"); s_mr = sem("s_mr"); s_mc = sem("s_mc"); s_mt = sem("s_mt"); s_me = sem("s_me")
        s_mrow = [sem(f"s_mrow{g}") for g in range(HG)]
        s_sf = sem("s_sf"); s_exp = sem("s_exp"); s_mask = sem("s_mask"); s_pv = sem("s_pv")
        s_oe = sem("s_oe"); s_ot = sem("s_ot"); s_or = sem("s_or"); s_on = sem("s_on")
        s_ott = sem("s_ott"); s_oh = sem("s_oh"); s_ol = sem("s_ol"); s_op = sem("s_op"); s_h1 = sem("s_h1")
        s_x2t = sem("s_x2t"); s_x2h = sem("s_x2h"); s_x2l = sem("s_x2l")
        s_rt = sem("s_rt"); s_lg = sem("s_lg"); s_ex = sem("s_ex"); s_cw = sem("s_cw"); s_ct = sem("s_ct")
        s_ce = sem("s_ce"); s_sp = sem("s_sp"); s_cb = sem("s_cb")
        s_up = sem("s_up"); s_th = sem("s_th"); s_gx = sem("s_gx"); s_gs = sem("s_gs"); s_g = sem("s_g"); s_gh = sem("s_gh")
        s_gl = sem("s_gl"); s_dn = sem("s_dn")
        s_ye = sem("s_ye"); s_yt = sem("s_yt"); s_fin = sem("s_fin"); s_out = sem("s_out")

        H_FREE = {"router": (s_cw, CW_READ), "heads": (s_on, None), "weights": (s_ce, None),
                  "spread": (s_cb, None), "maxima": (s_me, None)}
        H_PER = {"router": CW_OPS, "heads": HG, "weights": 1, "spread": CH, "maxima": HG}
        USES = bank_h_uses()

        def bank_h_free(r, use):
            at = USES.index(use)
            back = 0
            while True:
                at -= 1
                if at < 0:
                    at += len(USES)
                    back += 1
                kind, d, k = USES[at]
                n = r.n - back + d
                if r.n - back < -1:
                    return go, 1
                if 0 <= n < NB:
                    s, fixed = H_FREE[kind]
                    return (s, r.count(H_PER[kind], d - back, fixed if fixed is not None else k + 1))

        def rounds(eng, body):
            for n in range(-1, LOOP_FIRST):
                body(Round(n))
            if loop:
                with eng.Fori(LOOP_FIRST, NB - 1) as t:
                    body(Round(t, fixed=3))
            else:
                for n in range(2, NB - 1):
                    body(Round(n))
            for n in (NB - 1, NB, NB + 1):
                body(Round(n))

        def seq(ap, r, d):
            if isinstance(r.t, int):
                return ap[r.t + d:r.t + d + 1]
            return ap[bass.ds(r.t + d, 1)]

        def weight_pieces():
            cut = []
            def rows(w):
                return w.rearrange("(c p) n -> p c n", p=P)
            for c in range(DC):
                cut.append((rows(wqkv)[:, c, 0:512], wqkv_h[:, c, 0:512], wqkv_l[:, c, 0:512], 512))
            cut.append((rows(wqkv)[:, :, 512:768], wqkv_h[:, :, 512:768], wqkv_l[:, :, 512:768], 512))
            cut.append((rows(wo), wo_h[:], wo_l[:], 512))
            cut.append((rows(wr), wr_h[:], wr_l[:], DC * (E + 2)))
            for c in range(DC):
                cut.append((rows(wgu)[:, c, :], wgu_h[:, c, :], wgu_l[:, c, :], 512))
            cut.append((rows(wdn), wdn_h[:], wdn_l[:], 512))
            for e in range(E):
                cut.append((rows(w1[e]), w1_h[:, :, e, :], w1_l[:, :, e, :], 512))
                cut.append((rows(w2[e]), w2_h[:, :, e, :], w2_l[:, :, e, :], 512))
            return cut

        def stage(n, width):
            flat = h1[:].rearrange("p k d -> p (k d)")[:, 512 * (n % 2):512 * (n % 2) + width]
            return flat if width == 512 and weight_shape(n) == 1 else flat.rearrange("p (c n) -> p c n", c=DC)

        def weight_shape(n):
            return 1 if len(weight_pieces()[n][1].shape) == 2 else 2

        block = ctx.enter_context(nc.Block())

        @block.sync
        def _(sp):
            sp.dma_start(cos_sb[:], cos.rearrange("(k p) c -> p k c", p=P)).then_inc(s_ld, 16)
            sp.dma_start(sin_sb[:], sin2.rearrange("(k p) c -> p k c", p=P)).then_inc(s_ld, 16)
            sp.dma_start(bias[:], bqkv.rearrange("(a n) -> a n", a=1).broadcast_to([P, 3 * D])).then_inc(s_ld, 16)
            sp.dma_start(res[:], pe.rearrange("(k p) d -> p k d", p=P)).then_inc(s_cd, 16)
            sp.dma_start(v_new[:, 0, :], bo.rearrange("(a n) -> a n", a=1).broadcast_to([P, D])).then_inc(s_cd, 16)
            pieces = weight_pieces()
            for n, (src, _, _, width) in enumerate(pieces[:FIRST_PIECES]):
                if n >= 2:
                    sp.wait_ge(s_wl, n - 1)
                sp.dma_start(stage(n, width), src).then_inc(s_wd[n % 2], 16)
            sp.wait_ge(s_base, 1)
            sp.dma_start(base_dram.rearrange("(k p) d -> p k d", p=P), res[:]).then_inc(s_cd, 16)
            sp.wait_ge(s_cd, 48)

            def body(r):
                if r.nxt:
                    x_read, x2_read = r.held(sp, 1, 1, 0), r.held(sp, 1, -2, 1)
                    sp.wait_ge(s_xt, x_read)
                    sp.wait_ge(s_x2t, x2_read)
                    sp.dma_start(h_in[:], pe.rearrange("(k p) d -> p k d", p=P)).then_inc(s_tab, 16)
                    sp.wait_ge(s_gat, r.count(64, 1, 0))
                    sp.dma_start(idx[:], seq(x, r, 1).rearrange("a p k -> (a p) k")).then_inc(s_idx, 16)
                if r.att:
                    load_terms(r, 0, 3)
                if r.tail:
                    sp.wait_ge(s_fin, r.count(1, -2, 1))
                    sp.dma_start(seq(out, r, -2).rearrange("a (k p) d -> p (a k) d", p=P), o_tok[:]).then_inc(s_out, 16)
                if r.nxt:
                    for half in range(2):
                        sp.wait_ge(s_pl, r.count(TB, 1, 2 * half + 2))
                        sp.wait_ge(s_pm, r.count(TB, 1, 2 * half + 2))
                        sp.wait_ge(s_ph, r.count(TB, 1, 2 * half + 2))
                        sp.wait_ge(s_terms[3], r.count(LOADS, 0, LOADS))
                        sp.dma_start(parts_dram[:, :, :, half * 2 * P:(half + 1) * 2 * P].rearrange("a c p t -> p (a c) t"),
                                     parts[:].rearrange("p a c t -> p (a c) t")).then_inc(s_pw, 16)
                    load_terms(r, 1, 0)
                    load_terms(r, 1, 1)
                if r.att:
                    sp.wait_ge(s_h1, r.count(1, 0, 0))
                    sp.dma_start(res[:], base_dram.rearrange("(k p) d -> p k d", p=P)).then_inc(s_tabr, 16)
                    sp.wait_ge(s_gatr, r.count(64, 0, 0))
                    sp.dma_start(idx_res[:], seq(x, r, 0).rearrange("a p k -> (a p) k")).then_inc(s_idxr, 16)
                if r.nxt:
                    load_terms(r, 1, 2)

            def load_terms(r, d, g):
                stored, scored = r.held(sp, 32, d, 32), r.held(sp, HG * STEPS, d - 1, STEPS * (g + 1))
                sp.wait_ge(s_pw, stored)
                sp.wait_ge(s_sf, scored)
                rows = slice((g % 2) * 64, (g % 2) * 64 + 64)
                for j in range(NT):
                    for c, terms, dst in ((0, TERMS_Q, q_terms), (2, TERMS_K, k_terms)):
                        sp.dma_start(dst[DK * j:DK * (j + 1), g, :, :],
                                     parts_dram[terms[j], c + g // 2, rows, :].rearrange("(h i) t -> i h t", i=DK))\
                            .then_inc(s_terms[g], 16)

            rounds(sp, body)
            sp.wait_ge(s_out, 16 * NB)

        @block.tensor
        def _(pe_eng):
            t_eng = pe_eng

            def product(dst, lh, ll, rh, rl, first, last):
                t_eng.matmul(dst, lh, rh, start=first, stop=False, skip_group_check=True)
                t_eng.matmul(dst, lh, rl, start=False, stop=False, skip_group_check=True)
                return t_eng.matmul(dst, ll, rh, start=False, stop=last, skip_group_check=True)

            def plain_scores(r, d, g, f):
                head = f // len(MAX_FILLS)
                n = HG * NF
                t_eng.wait_ge(s_terms[g], r.count(LOADS, d, LOADS))
                t_eng.wait_ge(s_mr, r.count(n, d, NF * g + f))
                off = 0
                for qb in MAX_FILLS[f % len(MAX_FILLS)]:
                    last = t_eng.matmul(bank_m[:, 0, off:off + (qb + 1) * P], q_terms[0:KS, g, head, qb * P:(qb + 1) * P],
                                        k_terms[0:KS, g, head, 0:(qb + 1) * P], start=True, stop=True)
                    off += (qb + 1) * P
                last.then_inc(s_mf, 1)

            def scores(r, g, i):
                t_eng.wait_ge(s_mrow[g], r.count(48, 0, 48))
                t_eng.wait_ge(s_exp, r.count(HG * STEPS, 0, STEPS * g + i))
                off = 0
                for kb in ROUND_KEYS[i // HH]:
                    n = T - kb * P
                    last = t_eng.matmul(bank_s[:, 0, off:off + n], k_terms[0:KM, g, i % HH, kb * P:(kb + 1) * P],
                                        q_terms[0:KM, g, i % HH, kb * P:T], start=True, stop=True)
                    off += n
                last.then_inc(s_sf, 1)

            def probs_v(r, d, g, rd):
                t_eng.wait_ge(s_mask, r.count(HG * NR, d, NR * g + rd + 1))
                t_eng.wait_ge(s_exp, r.count(HG * STEPS, d, STEPS * g + HH * rd + HH))
                t_eng.wait_ge(s_v, r.count(1, d, 1))
                if rd == 0:
                    t_eng.wait_ge(s_oe, r.count(HG, d, g))
                buf = probs1 if rd == 1 else probs0
                off = 0
                for kb in ROUND_KEYS[rd]:
                    n = T - kb * P
                    for hh in range(HH):
                        last = t_eng.matmul(bank_o[32 * hh:32 * hh + DK + 1, 0, kb * P:T], v_aug[:, kb, HH * g + hh, :],
                                            buf[:, hh, off:off + n], start=(kb == 0), stop=(kb == TB - 1),
                                            skip_group_check=True)
                    off += n
                last.then_inc(s_pv, 1)

            def turn(dst, src, last_sem):
                for c in range(DC):
                    for k in range(TB):
                        last = t_eng.transpose(dst[:, c, k * P:(k + 1) * P], src[:, k, c * P:(c + 1) * P], ident[:])
                last.then_inc(last_sem, 1)

            def qkv(r, k):
                n = TB
                t_eng.wait_ge(s_xh, r.count(2, 1, 2))
                t_eng.wait_ge(s_xl, r.count(2, 1, 2))
                if r.n < 0:
                    t_eng.wait_ge(s_wl, 3)
                t_eng.wait_ge(s_h1, r.count(1, -1, 1))
                t_eng.wait_ge(s_gx, r.count(2 * CH, -2, 2 * CH))
                t_eng.wait_ge(s_qk, r.count(n, 1, k))
                t_eng.wait_ge(s_vn, r.count(n, 1, k))
                for b, cols in ((0, slice(0, 512)), (1, slice(512, 768))):
                    dst = bank_fg[:, b, 0:cols.stop - cols.start]
                    for c in range(DC):
                        rows = slice(k * P, (k + 1) * P)
                        last = product(dst, a_h[:, c, rows], a_l[:, c, rows], wqkv_h[:, c, cols], wqkv_l[:, c, cols],
                                       c == 0, c == DC - 1)
                last.then_inc(s_qkv, 1)

            def turn_qk(r, k):
                if k >= 2:
                    t_eng.wait_ge(s_pr, r.count(TB, 1, k - 1))
                    t_eng.wait_ge(s_ph, r.count(TB, 1, k - 1))
                else:
                    t_eng.wait_ge(s_x2h, r.count(2, -1, 2))
                    t_eng.wait_ge(s_x2l, r.count(2, -1, 2))
                    t_eng.wait_ge(s_xh, r.count(2, 1, 2))
                    t_eng.wait_ge(s_xl, r.count(2, 1, 2))
                t_eng.wait_ge(s_rot, r.count(TB, 1, k + 1))
                for c in range(4):
                    last = t_eng.transpose(bank_y[:, k % 2, c * P:(c + 1) * P], cb[:, 0, c * P:(c + 1) * P], ident[:])
                last.then_inc(s_qt, 1)

            def experts(r, d, m):
                c, k = m // 4, m % 4
                half = k // 2
                if k % 2 == 0 and c < CH:
                    i = 2 * c + half
                    free = i if c == 0 or (c == 1 and half == 0) else i - 1
                    t_eng.wait_ge(s_gx, r.count(2 * CH, d, free))
                    if c == 0 and half == 0:
                        t_eng.wait_ge(s_x2h, r.count(2, d, 2))
                        t_eng.wait_ge(s_x2l, r.count(2, d, 2))
                        t_eng.wait_ge(s_qk, r.count(TB, d + 2, TB))
                        t_eng.wait_ge(s_vn, r.count(TB, d + 2, TB))
                        t_eng.wait_ge(s_h1, r.count(1, d, 1))
                        if r.n <= 1:
                            t_eng.wait_ge(s_wl, len(weight_pieces()))
                    cols = slice(half * P, half * P + P)
                    for dc in range(DC):
                        if c == 0:
                            product(bank_fg[:, 0, :], wgu_h[:, dc, cols], wgu_l[:, dc, cols], x2_h[:, dc, :], x2_l[:, dc, :],
                                    dc == 0, dc == DC - 1)
                            up = slice(F + half * P, F + half * P + P)
                            last = product(bank_fg[:, 1, :], wgu_h[:, dc, up], wgu_l[:, dc, up], x2_h[:, dc, :], x2_l[:, dc, :],
                                           dc == 0, dc == DC - 1)
                        else:
                            last = product(bank_fg[:, half, :], w1_h[:, dc, c - 1, cols], w1_l[:, dc, c - 1, cols],
                                           x2_h[:, dc, :], x2_l[:, dc, :], dc == 0, dc == DC - 1)
                    last.then_inc(s_up, 1)
                if k % 2 == 1:
                    cc, half = (c - 1, 1) if k == 1 else (c, 0)
                    if 0 <= cc < CH:
                        i = 2 * cc + half
                        t_eng.wait_ge(s_gl, r.count(2 * CH, d, i + 1))
                        if i == 0:
                            t_eng.wait_ge(s_pr, r.count(TB, d + 2, TB))
                            t_eng.wait_ge(s_ph, r.count(TB, d + 2, TB))
                        for dd in range(DC):
                            cols = slice(dd * P, dd * P + P)
                            wh, wl = (wdn_h[:, half, cols], wdn_l[:, half, cols]) if cc == 0 else \
                                     (w2_h[:, half, cc - 1, cols], w2_l[:, half, cc - 1, cols])
                            last = product(bank_y[:, dd, :], wh, wl, a_h[:, half, :], a_l[:, half, :],
                                           i == 0, i == 2 * CH - 1)
                        last.then_inc(s_dn, 1)
                if m == 2:
                    spread_weights(r, d, 0)
                if k == 3 and c + 1 < CH:
                    spread_weights(r, d, c + 1)

            def spread_weights(r, d, c):
                t_eng.wait_ge(s_ce, r.count(1, d, 1))
                t_eng.wait_ge(*bank_h_free(r, ("spread", d, c)))
                t_eng.matmul(bank_h[:, 0, :], spread[:, (c + CH - 1) % CH, :], cw_rows[:], start=True, stop=True)\
                    .then_inc(s_sp, 1)

            def body(r):
                for s in range(4):
                    for i in range(STEPS):
                        d, m = moe_step(s, i)
                        plain_d = 1 if s == 3 else 0
                        fills = max_fills(i) if r.has[plain_d] else []
                        for f in fills[:1]:
                            plain_scores(r, plain_d, (s + 1) % HG, f)
                        if r.has[d] and 0 <= m <= MOE_LAST:
                            experts(r, d, m)
                        if i == 0 and r.has[-1 if s == 0 else 0]:
                            probs_v(r, -1 if s == 0 else 0, (s - 1) % HG, 2)
                        if r.att and i in (5, 9):
                            probs_v(r, 0, s, (i - 5) // 4)
                        if r.att:
                            scores(r, s, i)
                        for f in fills[1:]:
                            plain_scores(r, plain_d, (s + 1) % HG, f)
                        if i == 3 and r.has[-1 if s == 0 else 0]:
                            hd, g = (-1, 3) if s == 0 else (0, s - 1)
                            t_eng.wait_ge(s_oe, r.count(HG, hd, g + 1))
                            t_eng.wait_ge(*bank_h_free(r, ("heads", hd, g)))
                            for k in range(TB):
                                last = t_eng.transpose(bank_h[:, 0, k * P:(k + 1) * P], heads_t[:, k * P:(k + 1) * P], ident[:])
                            last.then_inc(s_ot, 1)
                        if i == 9 and r.has[plain_d]:
                            g = (s + 1) % HG
                            t_eng.wait_ge(s_mc, r.count(4 * HG, plain_d, 4 * g + 4))
                            t_eng.wait_ge(*bank_h_free(r, ("maxima", plain_d, g)))
                            for k in range(TB):
                                last = t_eng.transpose(bank_h_bf[0:3 * HH, k * P:(k + 1) * P],
                                                       max_parts[:, k, :, :].rearrange("p a h -> p (a h)"), identb[:])
                            last.then_inc(s_mt, 1)
                        if s == 0 and i == 5 and r.epi:
                            t_eng.wait_ge(s_on, r.count(HG, -1, HG))
                            t_eng.wait_ge(s_gx, r.count(2 * CH, -2, 2 * CH))
                            t_eng.wait_ge(s_qk, r.count(TB, 0, TB))
                            t_eng.wait_ge(s_vn, r.count(TB, 0, TB))
                            turn(bank_fg, o_tok, s_ott)
                        if s == 0 and i == 6 and r.tail:
                            t_eng.wait_ge(s_ye, r.count(1, -2, 1))
                            for k in range(TB):
                                for dd in range(DC):
                                    off = (k % 2) * D + dd * P
                                    last = t_eng.transpose(bank_y[:, k // 2, off:off + P], hid[:, dd, k * P:(k + 1) * P], ident[:])
                            last.then_inc(s_yt, 1)
                        if s == 0 and i == 7 and r.epi:
                            t_eng.wait_ge(s_oh, r.count(2, -1, 2))
                            t_eng.wait_ge(s_ol, r.count(2, -1, 2))
                            if r.n <= 1:
                                t_eng.wait_ge(s_wl, 4)
                            for k in range(TB):
                                for c in range(DC):
                                    rows = slice(k * P, (k + 1) * P)
                                    last = product(bank_fg[:, k // 2, (k % 2) * D:(k % 2 + 1) * D], a_h[:, c, rows], a_l[:, c, rows],
                                                   wo_h[:, c, :], wo_l[:, c, :], c == 0, c == DC - 1)
                            last.then_inc(s_op, 1)
                        if s == 0 and i == 8 and r.nxt:
                            t_eng.wait_ge(s_n1, r.count(N_OPS, 1, N_OPS))
                            t_eng.wait_ge(s_fin, r.count(1, -2, 1))
                            t_eng.wait_ge(s_pr, r.count(TB, 0, TB))
                            t_eng.wait_ge(s_ph, r.count(TB, 0, TB))
                            t_eng.wait_ge(s_x2h, r.count(2, -2, 2))
                            turn(bank_y, h_in, s_xt)
                        if s == 0 and i == 10 and r.nxt:
                            qkv(r, 0)
                        if s == 0 and i == 11 and r.epi:
                            t_eng.wait_ge(s_n2, r.count(N_OPS, -1, N_OPS))
                            t_eng.wait_ge(s_xh, r.count(2, 1, 2))
                            t_eng.wait_ge(s_xl, r.count(2, 1, 2))
                            t_eng.wait_ge(s_fin, r.count(1, -2, 1))
                            t_eng.wait_ge(s_pr, r.count(TB, 0, TB))
                            t_eng.wait_ge(s_ph, r.count(TB, 0, TB))
                            turn(bank_y, h_in, s_x2t)
                        if s == 1 and i < TB and r.nxt:
                            turn_qk(r, i)
                            if i + 1 < TB:
                                qkv(r, i + 1)
                        if s == 1 and i == 1 and r.epi:
                            t_eng.wait_ge(s_x2h, r.count(2, -1, 2))
                            t_eng.wait_ge(s_x2l, r.count(2, -1, 2))
                            if r.n <= 1:
                                t_eng.wait_ge(s_wl, 5)
                            t_eng.wait_ge(*bank_h_free(r, ("router", -1, 0)))
                            for k in range(TB):
                                for c in range(DC):
                                    rows = slice(k * P, (k + 1) * P)
                                    last = product(bank_h[:, 0, k * (E + 2):(k + 1) * (E + 2)], x2_h[:, c, rows], x2_l[:, c, rows],
                                                   wr_h[:, c, :], wr_l[:, c, :], c == 0, c == DC - 1)
                            last.then_inc(s_rt, 1)
                        if s == 1 and i == 4 and r.epi:
                            t_eng.wait_ge(s_cw, r.count(CW_OPS, -1, CW_OPS))
                            t_eng.wait_ge(*bank_h_free(r, ("weights", -1, 0)))
                            for k in range(TB):
                                last = t_eng.transpose(bank_h_bf[:, k * P:(k + 1) * P], cw_parts[:, k, :], identb[:])
                            last.then_inc(s_ct, 1)

            t_eng.wait_ge(go, 1)
            rounds(t_eng, body)

        @block.scalar
        def _(act):
            def split_weight(n):
                _, hi, _, width = weight_pieces()[n]
                if n < FIRST_PIECES:
                    act.wait_ge(s_wd[n % 2], 16 * (n // 2 + 1))
                else:
                    act.wait_ge(s_we[n % 2], 16 * ((n - FIRST_PIECES) // 2 + 1))
                nc.scalar.activation(hi, stage(n, width), ACT.Copy).then_inc(s_wh, 1)

            for n in range(FIRST_PIECES):
                split_weight(n)

            def experts(r, d, m):
                c, k = m // 4, m % 4
                i = 2 * c + k // 2
                if k % 2 == 1 and c < CH:
                    act.wait_ge(s_up, r.count(2 * CH, d, i + 1))
                    act.wait_ge(s_gl, r.count(2 * CH, d, i - 1))
                    if i < 2:
                        act.wait_ge(s_gl, r.count(2 * CH, d - 1, 2 * CH))
                    if i < 2:
                        act.wait_ge(s_rot, r.count(TB, d + 2, TB))
                    if i < 2:
                        act.wait_ge(s_yt, r.count(1, d - 1, 1))
                    nc.scalar.activation(hid[:, k // 2, :], bank_fg[:, 0 if c == 0 else k // 2, :], ACT.Tanh, scale=0.5)\
                        .then_inc(s_th, 1)

            def experts_high(r, d, m):
                c, k = m // 4, m % 4
                cc, half = (c, 0) if k == 2 else (c - 1, 1)
                if k % 2 == 0 and 0 <= cc < CH:
                    i = 2 * cc + half
                    act.wait_ge(s_g, r.count(2 * CH, d, i + 1))
                    act.wait_ge(s_dn, r.count(2 * CH, d, i - 1))
                    if i < 2:
                        act.wait_ge(s_qkv, r.count(TB, d + 2, TB))
                    if i < 2:
                        act.wait_ge(s_op, r.count(1, d, 1))
                    nc.scalar.activation(a_h[:, half, :], hid[:, half, :], ACT.Copy).then_inc(s_gh, 1)

            def weights_out(r, d, c):
                act.wait_ge(s_sp, r.count(CH, d, c + 1))
                if c >= 2:
                    act.wait_ge(s_g, r.count(2 * CH, d, 2 * (c - 1)))
                if c < 2:
                    act.wait_ge(s_qt, r.count(TB, d + 2, TB))
                if c < 2:
                    act.wait_ge(s_pl, r.count(TB, d + 2, TB))
                if c < 2:
                    act.wait_ge(s_g, r.count(2 * CH, d - 1, 2 * CH))
                nc.scalar.activation(cb[:, c % 2, :], bank_h[:, 0, :], ACT.Copy).then_inc(s_cb, 1)

            def high(src, dst, sem_out):
                for c in range(DC):
                    nc.scalar.activation(dst[:, c, :], src[:, c, :], ACT.Copy).then_inc(sem_out, 1)

            def body(r):
                for s in range(4):
                    for i in range(STEPS):
                        d, m = moe_step(s, i)
                        moe = r.has[d] and 0 <= m <= MOE_LAST
                        if moe:
                            experts(r, d, m)
                        if r.att:
                            buf, rd = (probs1 if i // HH == 1 else probs0), i // HH
                            g3 = NR * s
                            free = {0: g3, 1: g3 - 1, 2: g3 + 1}[rd]
                            act.wait_ge(s_sf, r.count(HG * STEPS, 0, STEPS * s + i + 1))
                            act.wait_ge(s_pv, r.count(HG * NR, 0, free))
                            n = T if rd == 0 else 3 * P
                            nc.scalar.activation(buf[:, i % HH, 0:n], bank_s[:, 0, 0:n], ACT.Exp, scale=SCALE).then_inc(s_exp, 1)
                        if moe:
                            if m == 2:
                                weights_out(r, d, 0)
                            experts_high(r, d, m)
                            if m % 4 == 3 and m // 4 + 1 < CH:
                                weights_out(r, d, m // 4 + 1)
                        hd, hg = (-1, 3) if s == 0 else (0, s - 1)
                        if i == 0 and r.has[hd]:
                            act.wait_ge(s_pv, r.count(HG * NR, hd, NR * (hg + 1)))
                            act.wait_ge(s_ot, r.count(HG, hd, hg))
                            nc.scalar.activation(heads_t[:], bank_o[:, 0, :], ACT.Copy).then_inc(s_oe, 1)
                        pd = 1 if s == 3 else 0
                        if i == 9 and r.has[pd]:
                            g = (s + 1) % HG
                            act.wait_ge(s_mt, r.count(HG, pd, g + 1))
                            act.wait_ge(s_mrow[(g - 1) % HG], r.count(48, pd - (g == 0), 48))
                            nc.scalar.activation(max_rows[:], bank_h_bf[0:3 * HH, 0:T], ACT.Copy).then_inc(s_me, 1)
                            act.wait_ge(s_me, r.count(HG, pd, g + 1))
                            act.wait_ge(s_sf, r.count(HG * STEPS, pd - 1, STEPS * (g + 1)))
                            for a in range(3):
                                act.dma_start(q_terms[KS + a:KS + a + 1, g, :, :], max_rows[HH * a:HH * (a + 1), :])\
                                    .then_inc(s_mrow[g], 16)
                        if s == 0 and i == 5 and r.tail:
                            act.wait_ge(s_dn, r.count(2 * CH, -2, 2 * CH))
                            for dd in range(DC):
                                y = nc.scalar.activation(hid[:, dd, :], bank_y[:, dd, :], ACT.Copy)
                            y.then_inc(s_ye, 1)
                        if s == 0 and i == 5 and r.epi:
                            act.wait_ge(s_ott, r.count(1, -1, 1))
                            act.wait_ge(s_dn, r.count(2 * CH, -2, 2 * CH))
                            act.wait_ge(s_qkv, r.count(TB, 0, TB))
                            high(bank_fg, a_h, s_oh)
                        if s == 0 and i == 8 and r.nxt:
                            act.wait_ge(s_xt, r.count(1, 1, 1))
                            act.wait_ge(s_op, r.count(1, -1, 1))
                            act.wait_ge(s_qkv, r.count(TB, 0, TB))
                            high(bank_y, a_h, s_xh)
                        if s == 0 and i == 11 and r.epi:
                            act.wait_ge(s_x2t, r.count(1, -1, 1))
                            act.wait_ge(s_up, r.count(2 * CH, -2, 2 * CH))
                            act.wait_ge(s_rt, r.count(1, -2, 1))
                            high(bank_y, x2_h, s_x2h)
                        if s == 1 and i == 2 and r.epi:
                            act.wait_ge(s_lg, r.count(3, -1, 3))
                            act.wait_ge(s_cw, r.count(CW_OPS, -2, CW_OPS))
                            nc.scalar.activation(ex[:], logit[:], ACT.Exp).then_inc(s_ex, 1)
                        if s == 1 and i == 4 and r.epi:
                            act.wait_ge(s_ct, r.count(1, -1, 1))
                            act.wait_ge(s_sp, r.count(CH, -2, CH))
                            nc.scalar.activation(cw_rows[:], bank_h_bf[:, 0:T], ACT.Copy).then_inc(s_ce, 1)
                        if s == 1 and i < TB and r.nxt:
                            k = i
                            cols = slice((k % 2) * P, (k % 2 + 1) * P)
                            act.wait_ge(s_qt, r.count(TB, 1, k + 1))
                            if k % 2 == 0:
                                act.wait_ge(s_pw, r.count(32, 1, 16 * (k // 2)))
                            nc.scalar.activation(parts[:, 0, :, cols], bank_y[:, k % 2, :].rearrange("p (c t) -> p c t", c=4),
                                                 ACT.Copy).then_inc(s_ph, 1)
                            act.wait_ge(s_pr, r.count(TB, 1, k + 1))
                            nc.scalar.activation(parts[:, 1, :, cols], cb[:, 1, :].rearrange("p (c t) -> p c t", c=4),
                                                 ACT.Copy).then_inc(s_pm, 1)
                        n = FIRST_PIECES + STEPS * (s - 1) + i
                        if r.n == 0 and FIRST_PIECES <= n + 1 < len(weight_pieces()):
                            src, _, _, width = weight_pieces()[n + 1]
                            act.wait_ge(s_wl, n)
                            act.dma_start(stage(n + 1, width), src).then_inc(s_we[(n + 1) % 2], 16)
                        if r.n == 0 and FIRST_PIECES <= n < len(weight_pieces()):
                            split_weight(n)

            act.wait_ge(go, 1)
            rounds(act, body)

        @block.vector
        def _(dve):
            v = nc.vector
            v.memset(causal[:], 0.0).then_inc(s_cv, 1)
            v.memset(v_aug[:], 1.0).then_inc(s_cv, 1)
            v.memset(cw_parts[:], 0.0).then_inc(s_cv, 1)
            v.memset(bank_o[:, 0, :], 0.0).then_inc(s_cv, 1)
            v.memset(k_terms[KS:P, :, :, :].rearrange("p g h t -> p (g h t)"), 1.0).then_inc(s_cv, 1)
            dve.wait_ge(s_cp, 6)
            v.tensor_copy(identb[:], ident[:]).then_inc(s_cv, 1)
            dve.wait_ge(s_cv, 6)
            dve.wait_ge(s_ld, 48)
            v.memset(minus_half[:], -0.5).then_inc(go, 1)
            dve.wait_ge(s_cd, 32)
            v.tensor_tensor(res[:], res[:], v_new[:, 0:1, :].broadcast_to([P, TB, D]), ALU.add).then_inc(s_base, 1)

            def low_weight(n):
                _, hi, lo, width = weight_pieces()[n]
                dve.wait_ge(s_wh, n + 1)
                v.tensor_tensor(lo, stage(n, width), hi.bitcast(F32), ALU.subtract).then_inc(s_wl, 1)

            for n in range(FIRST_PIECES):
                low_weight(n)

            def statistics(r, d, src, chain):
                for k in range(TB):
                    last = v.bn_stats(stats[:, k, :], src[:, k, :])
                last.then_inc(chain, 1)
                summed = r.held(dve, N_OPS, d, 1)
                dve.wait_ge(go, 1)
                dve.wait_ge(chain, summed)
                for k in range(TB):
                    last = v.bn_aggr(mv[:, k, :], stats[:, k, :])
                last.then_inc(chain, 1)
                dve.wait_ge(chain, r.count(N_OPS, d, 2))
                v.tensor_scalar(var_eps[:], mv[:, :, 1], EPS, None, ALU.add).then_inc(chain, 1)

            def normalise(src, chain):
                for k in range(TB):
                    last = v.tensor_scalar(h_in[:, k, :], src[:, k, :], mv[:, k, 0:1], rstd[:, k:k + 1], ALU.subtract, ALU.mult)
                last.then_inc(chain, 1)

            def low(r, d, src, hi, lo, filled, sem_out):
                for c in range(DC):
                    dve.wait_ge(filled, r.count(2, d, c + 1))
                    v.tensor_tensor(lo[:, c, :], src[:, c, :], hi[:, c, :].bitcast(F32), ALU.subtract).then_inc(sem_out, 1)

            def maxima(r, d, g, f):
                filled = r.held(dve, HG * NF, d, NF * g + f + 1)
                dve.wait_ge(go, 1)
                dve.wait_ge(s_mf, filled)
                off = 0
                for qb in MAX_FILLS[f % len(MAX_FILLS)]:
                    n = (qb + 1) * P
                    last = v.tensor_tensor_reduce(scrap[:, off:off + n], bank_m[:, 0, off:off + n], causal[:, T - n:T], 1.0, NEG,
                                                  ALU.add, ALU.max, row_max[:, qb, f // len(MAX_FILLS):f // len(MAX_FILLS) + 1])
                    off += n
                last.then_inc(s_mr, 1)

            def experts(r, d, m):
                c, k = m // 4, m % 4
                if k % 2 == 1 and c < CH:
                    half, i = k // 2, 2 * c + k // 2
                    dve.wait_ge(s_th, r.count(2 * CH, d, i + 1))
                    op = v.scalar_tensor_tensor(out=hid[:, half, :], in0=hid[:, half, :], scalar=1.0,
                                                in1=bank_fg[:, 0 if c == 0 else half, :], op0=ALU.add, op1=ALU.mult)
                    if c == 0:
                        op.then_inc(s_gs, 1)
                        dve.wait_ge(s_gs, r.count(2, d, half + 1))
                        op = v.tensor_tensor(hid[:, half, :], hid[:, half, :], bank_fg[:, 1, :], ALU.mult)
                    op.then_inc(s_gx, 1)

            def route(r):
                base = -1
                done = [0]

                def link(op):
                    done[0] += 1
                    op.then_inc(s_cw, 1)

                def linked():
                    dve.wait_ge(s_cw, r.count(CW_OPS, base, done[0]))

                def linked_alone():
                    so_far = r.held(dve, CW_OPS, base, done[0])
                    dve.wait_ge(go, 1)
                    dve.wait_ge(s_cw, so_far)

                lg = bank_h[:, 0, 0:TB * (E + 2)].rearrange("p (k e) -> p k e", k=TB)
                dve.wait_ge(s_rt, r.count(1, -1, 1))
                v.tensor_reduce(nmax[:], lg[:, :, 0:E], AX.X, ALU.max).then_inc(s_lg, 1)
                dve.wait_ge(s_lg, r.count(3, -1, 1))
                dve.wait_ge(s_ex, r.count(1, -2, 1))
                v.tensor_tensor(logit[:, :, 0:E], lg[:, :, 0:E], nmax[:, :].unsqueeze(2).broadcast_to([P, TB, E]), ALU.subtract)\
                    .then_inc(s_lg, 1)
                v.tensor_scalar(logit[:, :, E:CH], lg[:, :, E:CH], -1.0, None, ALU.mult).then_inc(s_lg, 1)
                dve.wait_ge(s_ex, r.count(1, -1, 1))
                dve.wait_ge(s_lg, r.count(3, -1, 3))
                link(v.tensor_reduce(esum[:], ex[:, :, 0:E], AX.X, ALU.add))
                linked()
                link(v.reciprocal(erec[:], esum[:]))
                linked()
                link(v.tensor_tensor(pr[:], ex[:, :, 0:E], erec[:, :].unsqueeze(2).broadcast_to([P, TB, E]), ALU.mult))
                linked_alone()
                for k in range(TB):
                    op = v.max(top8[:, k, :], pr[:, k, :])
                link(op)
                linked_alone()
                for k in range(TB):
                    op = v.max_index(top_i[:, k, :], top8[:, k, :], pr[:, k, :])
                link(op)
                linked()
                link(v.tensor_copy(top_f[:], top_i[:, :, 0:2]))
                linked()
                for dst, j in ((pick, 0), (pick2, 1)):
                    link(v.tensor_tensor(dst[:], iota8[:, :].unsqueeze(1).broadcast_to([P, TB, E]),
                                         top_f[:, :, j:j + 1].broadcast_to([P, TB, E]), ALU.is_equal))
                linked()
                link(v.tensor_tensor(pick[:], pick[:], pick2[:], ALU.add))
                linked()
                link(v.scalar_tensor_tensor(out=cw[:, :, 0:E], in0=pick[:], scalar=0.5, in1=pr[:], op0=ALU.mult, op1=ALU.mult))
                link(v.tensor_scalar(den[:], ex[:, :, E], 1.0, None, ALU.add))
                linked()
                link(v.reciprocal(den[:], den[:]))
                linked()
                link(v.tensor_scalar(cw[:, :, E], den[:], 0.5, None, ALU.mult))
                linked()
                dve.wait_ge(s_ct, r.count(1, -2, 1))
                link(v.tensor_copy(cw_parts[:, :, 0:CH], cw[:]))
                linked()
                link(v.tensor_tensor(cw_rest[:], cw[:], cw_parts[:, :, 0:CH], ALU.subtract))
                linked()
                link(v.tensor_copy(cw_parts[:, :, CH:2 * CH], cw_rest[:]))
                linked()
                link(v.tensor_tensor(cw_parts[:, :, 2 * CH:3 * CH], cw_rest[:], cw_parts[:, :, CH:2 * CH], ALU.subtract))
                assert done[0] == CW_OPS

            def body(r):
                for s in range(4):
                    for i in range(STEPS):
                        d, m = moe_step(s, i)
                        pd, pg = (1 if s == 3 else 0), (s + 1) % HG
                        fills = max_fills(i) if r.has[pd] else []
                        for f in fills[:1]:
                            maxima(r, pd, pg, f)
                        if r.has[d] and 0 <= m <= MOE_LAST:
                            experts(r, d, m)
                        for f in fills[1:]:
                            maxima(r, pd, pg, f)
                        if i == 8 and r.has[pd]:
                            n = 4 * HG
                            dve.wait_ge(s_mr, r.count(HG * NF, pd, NF * (pg + 1)))
                            dve.wait_ge(s_mt, r.count(HG, pd, pg))
                            v.tensor_scalar(max_parts[:, :, 0, :], row_max[:], -1.0, None, ALU.mult).then_inc(s_mc, 1)
                            dve.wait_ge(s_mc, r.count(n, pd, 4 * pg + 1))
                            v.scalar_tensor_tensor(out=max_rest[:], in0=row_max[:], scalar=-1.0, in1=max_parts[:, :, 0, :],
                                                   op0=ALU.mult, op1=ALU.subtract).then_inc(s_mc, 1)
                            dve.wait_ge(s_mc, r.count(n, pd, 4 * pg + 2))
                            v.tensor_copy(max_parts[:, :, 1, :], max_rest[:]).then_inc(s_mc, 1)
                            dve.wait_ge(s_mc, r.count(n, pd, 4 * pg + 3))
                            v.tensor_tensor(max_parts[:, :, 2, :], max_rest[:], max_parts[:, :, 1, :], ALU.subtract).then_inc(s_mc, 1)
                        hd, hg = (-1, 3) if s == 0 else (0, s - 1)
                        if i == 3 and r.has[hd]:
                            ht = bank_h[:, 0, :].rearrange("p (k h w) -> p k h w", k=TB, h=HH)
                            dve.wait_ge(s_ot, r.count(HG, hd, hg + 1))
                            v.reciprocal(rec[:], ht[:, :, :, DK]).then_inc(s_or, 1)
                            dve.wait_ge(s_or, r.count(HG, hd, hg + 1))
                            dve.wait_ge(s_ott, r.count(1, hd, 0))
                            if s == 1:
                                dve.wait_ge(s_out, r.count(16, -2, 16))
                            v.tensor_tensor(o_tok[:, :, hg * HH * DK:(hg + 1) * HH * DK].rearrange("p k (h w) -> p k h w", h=HH),
                                            ht[:, :, :, 0:DK], rec[:].unsqueeze(3).broadcast_to([P, TB, HH, DK]), ALU.mult)\
                                .then_inc(s_on, 1)
                        if s == 0 and i == 4 and r.nxt:
                            dve.wait_ge(s_gat, r.count(64, 1, 64))
                            statistics(r, 1, h_in, s_n1)
                            dve.wait_ge(s_n1p, r.count(1, 1, 1))
                            normalise(h_in, s_n1)
                        if s == 0 and i == 5 and r.epi:
                            low(r, -1, bank_fg, a_h, a_l, s_oh, s_ol)
                        if s == 0 and i == 6 and r.tail:
                            dve.wait_ge(s_yt, r.count(1, -2, 1))
                            dve.wait_ge(s_ott, r.count(1, -1, 1))
                            dve.wait_ge(s_h1, r.count(1, -2, 1))
                            if not r.epi:
                                dve.wait_ge(s_out, r.count(16, -2, 0))
                            for half in range(2):
                                op = v.tensor_tensor(o_tok[:, 2 * half:2 * half + 2, :], bank_y[:, half, :].rearrange("p (k d) -> p k d", k=2),
                                                     h1[:, 2 * half:2 * half + 2, :], ALU.add)
                            op.then_inc(s_fin, 1)
                        if s == 0 and i == 7 and r.epi:
                            dve.wait_ge(s_op, r.count(1, -1, 1))
                            dve.wait_ge(s_gatr, r.count(64, -1, 64))
                            dve.wait_ge(s_fin, r.count(1, -2, 1))
                            if r.n <= 1:
                                dve.wait_ge(s_wl, len(weight_pieces()))
                            for half in range(2):
                                op = v.tensor_tensor(h1[:, 2 * half:2 * half + 2, :], bank_fg[:, half, :].rearrange("p (k d) -> p k d", k=2),
                                                     res[:, 2 * half:2 * half + 2, :], ALU.add)
                            op.then_inc(s_h1, 1)
                        if s == 0 and i == 8 and r.nxt:
                            low(r, 1, bank_y, a_h, a_l, s_xh, s_xl)
                        if s == 0 and i == 8 and r.epi:
                            dve.wait_ge(s_h1, r.count(1, -1, 1))
                            statistics(r, -1, h1, s_n2)
                            dve.wait_ge(s_n2p, r.count(1, -1, 1))
                            dve.wait_ge(s_xt, r.count(1, 1, 1))
                            normalise(h1, s_n2)
                        if s == 0 and i == 11 and r.epi:
                            low(r, -1, bank_y, x2_h, x2_l, s_x2h, s_x2l)
                        if s == 0 and i == 10 and r.nxt:
                            rotate(r, 0)
                        if s == 1 and i < TB and r.nxt:
                            k = i
                            cols = slice((k % 2) * P, (k % 2 + 1) * P)
                            dve.wait_ge(s_ph, r.count(TB, 1, k + 1))
                            dve.wait_ge(s_pl, r.count(TB, 1, k))
                            v.tensor_tensor(cb[:, 1, :].rearrange("p (c t) -> p c t", c=4),
                                            bank_y[:, k % 2, :].rearrange("p (c t) -> p c t", c=4), parts[:, 0, :, cols],
                                            ALU.subtract).then_inc(s_pr, 1)
                            dve.wait_ge(s_pm, r.count(TB, 1, k + 1))
                            dve.wait_ge(s_pr, r.count(TB, 1, k + 1))
                            v.tensor_tensor(parts[:, 2, :, cols], cb[:, 1, :].rearrange("p (c t) -> p c t", c=4),
                                            parts[:, 1, :, cols], ALU.subtract).then_inc(s_pl, 1)
                            if k + 1 < TB:
                                rotate(r, k + 1)
                        if s == 1 and i == 1 and r.epi:
                            route(r)
                        if r.n == 0 and s >= 1:
                            n = FIRST_PIECES + STEPS * (s - 1) + i
                            if n < len(weight_pieces()):
                                low_weight(n)

            def rotate(r, k):
                dve.wait_ge(s_qkv, r.count(TB, 1, k + 1))
                dve.wait_ge(s_yt, r.count(1, -2, 1))
                dve.wait_ge(s_rot, r.count(TB, 1, k))
                dve.wait_ge(s_gl, r.count(2 * CH, -2, 2 * CH))
                v.tensor_tensor(hid[:, 0, :], bank_fg[:, 0, :], bias[:, 0:2 * D], ALU.add).then_inc(s_qk, 1)
                dve.wait_ge(s_v, r.count(1, 1, 0))
                if r.n < 0:
                    dve.wait_ge(s_base, 1)
                v.tensor_tensor(v_new[:, k, :], bank_fg[:, 1, 0:D], bias[:, 2 * D:3 * D], ALU.add).then_inc(s_vn, 1)
                dve.wait_ge(s_qk, r.count(TB, 1, k + 1))
                x = hid[:, 0, :].rearrange("p (h a w) -> p h a w", a=2, w=HALF)
                y = hid[:, 1, :].rearrange("p (h a w) -> p h a w", a=2, w=HALF)
                for a in range(2):
                    sn = sin_sb[:, k:k + 1, a * HALF:(a + 1) * HALF].broadcast_to([P, 2 * H, HALF])
                    op = v.tensor_tensor(y[:, :, a, :], x[:, :, 1 - a, :], sn, ALU.mult)
                op.then_inc(s_rs, 1)
                dve.wait_ge(s_rs, r.count(TB, 1, k + 1))
                dve.wait_ge(s_rc, r.count(TB, 1, k + 1))
                v.tensor_tensor(cb[:, 0, :], cb[:, 0, :], hid[:, 1, :], ALU.add).then_inc(s_rot, 1)

            rounds(dve, body)

        @block.gpsimd
        def _(pool):
            g = nc.gpsimd
            g.memset(ident[:], 0.0).then_inc(s_cq, 1)
            g.memset(spread[:], 0.0).then_inc(s_cq, 1)
            pool.wait_ge(s_cq, 2)
            g.affine_select(out=ident[:], in_=ident[:], compare_op=ALU.not_equal, fill=1.0, base=0,
                            pattern=[[-1, P]], channel_multiplier=1).then_inc(s_cp, 1)
            for a in range(3):
                g.affine_select(out=spread[:], in_=spread[:], compare_op=ALU.not_equal, fill=1.0, base=-CH * a,
                                pattern=[[-1, CH], [0, P]], channel_multiplier=1).then_inc(s_cp, 1)
                pool.wait_ge(s_cp, a + 2)
            g.iota(iota8[:], pattern=[[1, E]], base=0, channel_multiplier=0,
                   allow_small_or_imprecise_dtypes=True).then_inc(s_cp, 1)
            pool.wait_ge(s_cv, 1)
            last = causal[:, T - P:T]
            g.affine_select(out=last, in_=last, compare_op=ALU.is_ge, fill=NEG, base=0,
                            pattern=[[-1, P]], channel_multiplier=1).then_inc(s_cp, 1)
            pool.wait_ge(go, 1)

            def gather(r, d, dst, tab, ids, row_ids, done):
                here = r.held(pool, 16, d, 16)
                pool.wait_ge(go, 1)
                pool.wait_ge(tab, here)
                pool.wait_ge(ids, here)
                for k in range(TB):
                    g.indirect_dma_start(out=dst[:, k, :], out_offset=None, in_=table,
                                         in_offset=bass.IndirectOffsetOnAxis(ap=row_ids[:, k:k + 1], axis=0),
                                         compute_op=ALU.add).then_inc(done, 16)

            def experts(r, d, m):
                c, k = m // 4, m % 4
                if k % 2 == 1 and c < CH:
                    half, i = k // 2, 2 * c + k // 2
                    pool.wait_ge(s_gx, r.count(2 * CH, d, i + 1))
                    pool.wait_ge(s_cb, r.count(CH, d, c + 1))
                    g.tensor_tensor(hid[:, half, :], hid[:, half, :], cb[:, c % 2, :], ALU.mult).then_inc(s_g, 1)
                cc, half = (c, 0) if k == 2 else (c - 1, 1)
                if k % 2 == 0 and 0 <= cc < CH:
                    i = 2 * cc + half
                    pool.wait_ge(s_gh, r.count(2 * CH, d, i + 1))
                    g.tensor_tensor(a_l[:, half, :], hid[:, half, :], a_h[:, half, :].bitcast(F32), ALU.subtract).then_inc(s_gl, 1)

            def power(r, d, chain, pooled):
                pool.wait_ge(chain, r.count(N_OPS, d, 3))
                g.tensor_tensor(rstd[:], var_eps[:], minus_half[:], ALU.pow).then_inc(pooled, 1)

            def body(r):
                for s in range(4):
                    for i in range(STEPS):
                        d, m = moe_step(s, i)
                        if s == 0 and i == 1 and r.att:
                            projected, used = r.held(pool, TB, 0, TB), r.held(pool, HG * NR, 0, 0)
                            pool.wait_ge(go, 1)
                            pool.wait_ge(s_vn, projected)
                            pool.wait_ge(s_pv, used)
                            g.tensor_copy(v_aug[:, :, :, 0:DK], v_new[:].rearrange("p k (h w) -> p k h w", h=H)).then_inc(s_v, 1)
                        if r.has[d] and 0 <= m <= MOE_LAST:
                            experts(r, d, m)
                        if s == 0 and i == 2 and r.nxt:
                            gather(r, 1, h_in, s_tab, s_idx, idx, s_gat)
                        if r.att and i in (3, 7, 11):
                            rd = i // HH
                            written = r.held(pool, HG * STEPS, 0, STEPS * s + i + 1)
                            pool.wait_ge(go, 1)
                            pool.wait_ge(s_exp, written)
                            if rd == 2:
                                blk = probs0[:, :, 0:T].rearrange("p h (a c) -> p h a c", a=2)[:, :, :, 0:P]
                                op = g.affine_select(out=blk, in_=blk, compare_op=ALU.is_ge, fill=0.0, base=0,
                                                     pattern=[[0, HH], [0, 2], [1, P]], channel_multiplier=-1)
                            else:
                                blk = (probs1 if rd else probs0)[:, :, 0:P]
                                op = g.affine_select(out=blk, in_=blk, compare_op=ALU.is_ge, fill=0.0, base=0,
                                                     pattern=[[0, HH], [1, P]], channel_multiplier=-1)
                            op.then_inc(s_mask, 1)
                        if s == 0 and i == 5 and r.nxt:
                            power(r, 1, s_n1, s_n1p)
                        if s == 0 and i == 9 and r.epi:
                            power(r, -1, s_n2, s_n2p)
                        k = {(0, 10): 0, (1, 0): 1, (1, 1): 2, (1, 2): 3}.get((s, i))
                        if k is not None and r.nxt:
                            pool.wait_ge(s_qk, r.count(TB, 1, k + 1))
                            pool.wait_ge(s_qt, r.count(TB, 1, k))
                            pool.wait_ge(s_g, r.count(2 * CH, -2, 2 * CH))
                            g.tensor_tensor(cb[:, 0, :].rearrange("p (h w) -> p h w", w=HALF),
                                            hid[:, 0, :].rearrange("p (h w) -> p h w", w=HALF),
                                            cos_sb[:, k:k + 1, :].broadcast_to([P, 4 * H, HALF]), ALU.mult).then_inc(s_rc, 1)
                        if s == 2 and i == 4 and r.att:
                            gather(r, 0, res, s_tabr, s_idxr, idx_res, s_gatr)

            rounds(pool, body)


N_OPS = 4
CW_OPS = 17
CW_READ = 1
FIRST_PIECES = 5


def tables():
    import numpy as np
    f = np.float32
    pos = np.arange(T, dtype=f)[:, None]
    i = np.arange(D // 2, dtype=f)[None, :]
    ang = (pos / np.power(f(10000.0), f(2.0) * i / f(D))).astype(f)
    pe = np.zeros((T, D), f)
    pe[:, 0::2], pe[:, 1::2] = np.sin(ang), np.cos(ang)
    freq = f(1.0) / np.power(f(10000.0), f(2.0) * np.arange(HALF, dtype=f) / f(DK))
    rot = (pos * freq[None, :]).astype(f)
    return pe, np.cos(rot).astype(f), np.concatenate([-np.sin(rot), np.sin(rot)], 1).astype(f)


def kernel(**inputs):
    import numpy as np
    import concourse.bacc as bacc
    from concourse.bass_utils import run_bass_kernel_spmd as run

    a = {k: np.asarray(v) for k, v in inputs.items()}
    pe, cos, sin2 = tables()
    layout = {
        "x": a["x"].reshape(NB, TB, P).transpose(0, 2, 1),
        "table": a["L0_tok_W"],
        "pe": pe, "cos": cos, "sin2": sin2,
        "wqkv": np.concatenate([a["L0_attn_WQ_w"].T, a["L0_attn_WK_w"].T, a["L0_attn_WV_w"].T], axis=1),
        "bqkv": np.concatenate([a["L0_attn_WQ_b"], a["L0_attn_WK_b"], a["L0_attn_WV_b"]]),
        "wo": a["L0_attn_Wo_w"].T,
        "bo": a["L0_attn_Wo_b"],
        "wr": np.concatenate([a["L0_ffn_router_w"], a["L0_ffn_shared_gate_w"], np.zeros((D, 1), np.float32)], axis=1),
        "w1": a["L0_ffn_w1"], "w2": a["L0_ffn_w2"],
        "wgu": a["L0_ffn_shared_gate_up"], "wdn": a["L0_ffn_shared_down"],
    }
    nc = bacc.Bacc("TRN2", target_bir_lowering=False, num_devices=1)
    arrays, args = {}, []
    for name, value in layout.items():
        value = np.ascontiguousarray(value)
        arrays["in_" + name] = value
        args.append(nc.dram_tensor("in_" + name, value.shape, mybir.dt.from_np(value.dtype), kind="ExternalInput").ap())
    out = nc.dram_tensor("out_0", (NB, T, D), F32, kind="ExternalOutput").ap()
    lm_block_kernel(nc, *args, out, loop=LOOP)
    r = run(nc, [arrays], core_ids=[0])
    return r.results[0]["out_0"]


LOOP = True
```

```python
from contextlib import ExitStack

import concourse.bass as bass
from concourse import mybir

F32 = mybir.dt.float32
F32R = mybir.dt.float32r
BF16 = mybir.dt.bfloat16
I32 = mybir.dt.int32
U32 = mybir.dt.uint32
ALU = mybir.AluOpType
ACT = mybir.ActivationFunctionType
AX = mybir.AxisListType

P = 128
NB, T, D = 8, 512, 256
H, DK = 16, 16
E, F = 8, 256
TB, DC = T // P, D // P
HH = 4
HG = H // HH
CH = E + 1
STEPS = 12
LOOP_FIRST = 2
HALF = DK // 2
TERMS_Q = (0, 0, 1, 0, 2, 1)
TERMS_K = (0, 1, 0, 2, 0, 1)
NT = len(TERMS_Q)
KS = NT * DK
KM = KS + 3
STORES = 16 * TB // 2
LOADS = 2 * NT * 16
EPS = 1e-5
NEG = -3.0e38
SCALE = 1.0 / DK ** 0.5
MAX_FILLS = ((3,), (2,), (0, 1))
NF = HH * len(MAX_FILLS)
ROUND_KEYS = ((0,), (1,), (2, 3))
NR = len(ROUND_KEYS)
MOE_LAST = 4 * CH + 1


def max_fills(i):
    if i >= 8:
        return []
    return [3 * (i // 2) + 2] if i % 2 else [3 * (i // 2), 3 * (i // 2) + 1]


def moe_step(s, i):
    return (-2, STEPS * 3 + i - 3) if s == 0 else (-1, STEPS * (s - 1) + i - 3)


def ring_uses():
    uses = []
    for s in range(4):
        for i in range(STEPS):
            d, m = moe_step(s, i)
            plain = [("plain", 1 if s == 3 else 0, NF * ((s + 1) % HG) + f) for f in max_fills(i)]
            if len(plain) == 2:
                uses.append(plain.pop(0))
            if m == 2:
                uses.append(("spread", d, 0))
            if i % 2:
                uses += plain
            if s and m >= 0 and m % 4 == 3 and m // 4 + 1 < CH:
                uses.append(("spread", d, m // 4 + 1))
            if i % 2 == 0:
                uses += plain
            if i == 3:
                uses.append(("heads", -1 if s == 0 else 0, (s - 1) % 4))
            if i == 9:
                uses.append(("maxima", 1 if s == 3 else 0, (s + 1) % 4))
            if s == 1 and i == 1:
                uses.append(("router", -1, 0))
            if s == 1 and i == 4:
                uses.append(("weights", -1, 0))
    if len(uses) % 2:
        uses.append(("nobody", 0, 0))
    return uses


class Round:

    def __init__(self, t, fixed=None):
        self.t = t
        n = t if fixed is None else fixed
        self.n = n
        self.early = 0 <= n + 2 < NB
        self.nxt = 0 <= n + 1 < NB
        self.att = 0 <= n < NB
        self.epi = 0 <= n - 1 < NB
        self.tail = 0 <= n - 2 < NB
        self.has = {2: self.early, 1: self.nxt, 0: self.att, -1: self.epi, -2: self.tail}

    def count(self, per, d, k):
        if isinstance(self.t, int):
            return min(max((self.t + d) * per + k, 0), NB * per)
        assert (LOOP_FIRST + d) * per + k > 0
        return self.t * per + (d * per + k)

    def held(self, eng, per, d, k):
        value = self.count(per, d, k)
        return value if isinstance(value, int) else eng.snap(eng.to_reg(value))


def lm_block_kernel(nc, x, table, pe, cos, sin2, wqkv, bqkv, wo, bo, wr, w1, w2, wgu, wdn, out, loop):
    ctx = ExitStack()
    with ctx:
        def sb(name, shape, dt=F32):
            return ctx.enter_context(nc.sbuf_tensor(name, shape, dt))

        def bank(name, n=1):
            return ctx.enter_context(nc.psum_tensor(name, [P, n, 512], F32))

        def sem(name):
            return ctx.enter_context(nc.semaphore(name))

        parts_dram = nc.dram_tensor("qk_parts", (3, 4, P, T), BF16, kind="Internal").ap()
        base_dram = nc.dram_tensor("pe_plus_bias", (T, D), F32, kind="Internal").ap()

        ident = sb("ident", [P, P])
        identb = sb("identb", [P, P], BF16)
        causal = sb("causal", [P, T], BF16)
        cos_sb = sb("cos_sb", [P, TB, HALF])
        sin_sb = sb("sin_sb", [P, TB, DK])
        bias = sb("bias", [P, 3 * D])
        spread = sb("spread", [P, CH, P], BF16)
        iota8 = sb("iota8", [P, E])
        minus_half = sb("minus_half", [P, TB])
        wqkv_h, wqkv_l = sb("wqkv_h", [P, DC, 3 * D], F32R), sb("wqkv_l", [P, DC, 3 * D], F32R)
        wo_h, wo_l = sb("wo_h", [P, DC, D], F32R), sb("wo_l", [P, DC, D], F32R)
        wr_h, wr_l = sb("wr_h", [P, DC, E + 2], F32R), sb("wr_l", [P, DC, E + 2], F32R)
        w1_h, w1_l = sb("w1_h", [P, DC, E, F], F32R), sb("w1_l", [P, DC, E, F], F32R)
        w2_h, w2_l = sb("w2_h", [P, DC, E, D], F32R), sb("w2_l", [P, DC, E, D], F32R)
        wgu_h, wgu_l = sb("wgu_h", [P, DC, 2 * F], F32R), sb("wgu_l", [P, DC, 2 * F], F32R)
        wdn_h, wdn_l = sb("wdn_h", [P, DC, D], F32R), sb("wdn_l", [P, DC, D], F32R)
        idx, idx_res = sb("idx", [P, TB], I32), sb("idx_res", [P, TB], I32)
        h_in = sb("h_in", [P, TB, D])
        res = sb("res", [P, TB, D])
        h1 = sb("h1", [P, TB, D])
        o_tok = sb("o_tok", [P, TB, D])
        v_new = sb("v_new", [P, TB, D])
        v_aug = sb("v_aug", [P, TB, H, DK + 1])
        stats = sb("stats", [P, TB, 6])
        mv = sb("mv", [P, TB, 2])
        var_eps = sb("var_eps", [P, TB])
        rstd = sb("rstd", [P, TB])
        a_h, a_l = sb("a_h", [P, DC, T], F32R), sb("a_l", [P, DC, T], F32R)
        x2_h, x2_l = sb("x2_h", [P, DC, T], F32R), sb("x2_l", [P, DC, T], F32R)
        split = h_in[:].rearrange("p (b k) d -> p b (k d)", b=2)
        hid = sb("hid", [P, 2, T])
        cb = sb("cb", [P, 2, T])
        parts = sb("parts", [P, 3, 4, 2 * P], BF16)
        q_terms = sb("q_terms", [P, HG, HH, T], BF16)
        k_terms = sb("k_terms", [P, HG, HH, T], BF16)
        probs0 = sb("probs0", [P, HH, T])
        probs1 = sb("probs1", [P, HH, 3 * P])
        heads_t = sb("heads_t", [P, T])
        rec = sb("rec", [P, TB, HH])
        row_max = sb("row_max", [P, TB, HH])
        max_rest = sb("max_rest", [P, TB, HH])
        max_parts = sb("max_parts", [P, TB, 3, HH], BF16)
        max_rows = sb("max_rows", [3 * HH, T], BF16)
        nmax = sb("nmax", [P, TB])
        logit = sb("logit", [P, TB, CH])
        ex = sb("ex", [P, TB, CH])
        esum = sb("esum", [P, TB])
        erec = sb("erec", [P, TB])
        pr = sb("pr", [P, TB, E])
        top8 = sb("top8", [P, TB, 8])
        top_i = sb("top_i", [P, TB, 8], U32)
        top_f = sb("top_f", [P, TB, 2])
        pick = sb("pick", [P, TB, E])
        pick2 = sb("pick2", [P, TB, E])
        den = sb("den", [P, TB])
        cw = sb("cw", [P, TB, CH])
        cw_rest = sb("cw_rest", [P, TB, CH])
        cw_parts = sb("cw_parts", [P, TB, P], BF16)
        cw_rows = sb("cw_rows", [P, T], BF16)

        ring = bank("ring", 2)
        bank_s = bank("bank_s")
        bank_o = bank("bank_o")
        bank_fg = bank("bank_fg", 2)
        bank_y = bank("bank_y", 2)

        go = sem("go")
        s_ld = sem("s_ld"); s_cd = sem("s_cd"); s_cp = sem("s_cp"); s_cv = sem("s_cv"); s_cq = sem("s_cq")
        s_wd = [sem("s_wd0"), sem("s_wd1")]
        s_we = [sem("s_we0"), sem("s_we1")]
        s_wh = sem("s_wh"); s_wl = sem("s_wl"); s_ea = sem("s_ea"); s_base = sem("s_base")
        s_tab = sem("s_tab"); s_idx = sem("s_idx"); s_gat = sem("s_gat")
        s_tabr = sem("s_tabr"); s_idxr = sem("s_idxr"); s_gatr = sem("s_gatr")
        s_n1 = sem("s_n1"); s_n1p = sem("s_n1p"); s_n2 = sem("s_n2"); s_n2p = sem("s_n2p")
        s_xt = sem("s_xt"); s_xh = sem("s_xh"); s_xl = sem("s_xl")
        s_qkv = sem("s_qkv"); s_qk = sem("s_qk"); s_vn = sem("s_vn"); s_v = sem("s_v")
        s_rc = sem("s_rc"); s_rs = sem("s_rs"); s_rot = sem("s_rot")
        s_qt = sem("s_qt"); s_ph = sem("s_ph"); s_pc = sem("s_pc"); s_pr = sem("s_pr"); s_pm = sem("s_pm"); s_pl = sem("s_pl")
        s_pw = [sem("s_pw0"), sem("s_pw1")]; s_terms = [sem(f"s_terms{g}") for g in range(HG)]
        s_mf = sem("s_mf"); s_mr = sem("s_mr"); s_mc = sem("s_mc"); s_mt = sem("s_mt"); s_me = sem("s_me")
        s_mrow = [sem(f"s_mrow{g}") for g in range(HG)]
        s_sf = sem("s_sf"); s_exp = sem("s_exp"); s_mask = sem("s_mask"); s_pv = sem("s_pv")
        s_oe = sem("s_oe"); s_ot = sem("s_ot"); s_or = sem("s_or"); s_on = sem("s_on")
        s_ott = sem("s_ott"); s_oh = sem("s_oh"); s_ol = sem("s_ol"); s_op = sem("s_op"); s_h1 = sem("s_h1")
        s_x2t = sem("s_x2t"); s_x2h = sem("s_x2h"); s_x2l = sem("s_x2l")
        s_rt = sem("s_rt"); s_lg = sem("s_lg"); s_ex = sem("s_ex"); s_cw = sem("s_cw"); s_ct = sem("s_ct")
        s_ce = sem("s_ce"); s_sp = sem("s_sp"); s_cb = sem("s_cb")
        s_up = sem("s_up"); s_th = sem("s_th"); s_gx = sem("s_gx"); s_gs = sem("s_gs"); s_g = sem("s_g"); s_gh = sem("s_gh")
        s_gl = sem("s_gl"); s_dn = sem("s_dn")
        s_ye = sem("s_ye"); s_yt = sem("s_yt"); s_fin = sem("s_fin"); s_out = sem("s_out")

        READ = {"plain": (s_mr, HG * NF), "router": (s_lg, 3), "heads": (s_on, HG), "weights": (s_ce, 1),
                "spread": (s_cb, CH), "maxima": (s_me, HG)}
        USES = ring_uses()

        def ring_bank(use):
            return USES.index(use) % 2

        def ring_free(r, use):
            at = USES.index(use) - 2
            back = 0
            while True:
                if at < 0:
                    at += len(USES)
                    back += 1
                kind, d, k = USES[at]
                if r.n - back < -1:
                    return go, 1
                if 0 <= r.n - back + d < NB and kind in READ:
                    s, per = READ[kind]
                    return s, r.count(per, d - back, 3 if kind == "router" else k + 1)
                at -= 2

        def rounds(eng, body):
            for n in range(-2, LOOP_FIRST):
                body(Round(n))
            if loop:
                with eng.Fori(LOOP_FIRST, NB - 2) as t:
                    body(Round(t, fixed=3))
            else:
                for n in range(LOOP_FIRST, NB - 2):
                    body(Round(n))
            for n in range(NB - 2, NB + 2):
                body(Round(n))

        def seq(ap, r, d):
            if isinstance(r.t, int):
                return ap[r.t + d:r.t + d + 1]
            return ap[bass.ds(r.t + d, 1)]

        def weight_pieces():
            cut = []
            def rows(w):
                return w.rearrange("(c p) n -> p c n", p=P)
            for c in range(DC):
                cut.append((rows(wqkv)[:, c, 0:512], wqkv_h[:, c, 0:512], wqkv_l[:, c, 0:512], 512))
            cut.append((rows(wqkv)[:, :, 512:768], wqkv_h[:, :, 512:768], wqkv_l[:, :, 512:768], 512))
            cut.append((rows(wo), wo_h[:], wo_l[:], 512))
            cut.append((rows(wr), wr_h[:], wr_l[:], DC * (E + 2)))
            for c in range(DC):
                cut.append((rows(wgu)[:, c, :], wgu_h[:, c, :], wgu_l[:, c, :], 512))
            cut.append((rows(wdn), wdn_h[:], wdn_l[:], 512))
            for e in range(E):
                cut.append((rows(w1[e]), w1_h[:, :, e, :], w1_l[:, :, e, :], 512))
                cut.append((rows(w2[e]), w2_h[:, :, e, :], w2_l[:, :, e, :], 512))
            return cut

        def stage(n, width):
            flat = h1[:].rearrange("p k d -> p (k d)")[:, 512 * (n % 2):512 * (n % 2) + width]
            return flat if width == 512 and weight_shape(n) == 1 else flat.rearrange("p (c n) -> p c n", c=DC)

        def weight_shape(n):
            return 1 if len(weight_pieces()[n][1].shape) == 2 else 2

        block = ctx.enter_context(nc.Block())

        @block.sync
        def _(sp):
            sp.dma_start(cos_sb[:], cos.rearrange("(k p) c -> p k c", p=P)).then_inc(s_ld, 16)
            sp.dma_start(sin_sb[:], sin2.rearrange("(k p) c -> p k c", p=P)).then_inc(s_ld, 16)
            sp.dma_start(bias[:], bqkv.rearrange("(a n) -> a n", a=1).broadcast_to([P, 3 * D])).then_inc(s_ld, 16)
            sp.dma_start(res[:], pe.rearrange("(k p) d -> p k d", p=P)).then_inc(s_cd, 16)
            sp.dma_start(v_new[:, 0, :], bo.rearrange("(a n) -> a n", a=1).broadcast_to([P, D])).then_inc(s_cd, 16)
            pieces = weight_pieces()
            for n, (src, _, _, width) in enumerate(pieces[:FIRST_PIECES]):
                if n >= 2:
                    sp.wait_ge(s_wl, n - 1)
                sp.dma_start(stage(n, width), src).then_inc(s_wd[n % 2], 16)
            sp.wait_ge(s_base, 1)
            sp.dma_start(base_dram.rearrange("(k p) d -> p k d", p=P), res[:]).then_inc(s_cd, 16)
            sp.wait_ge(s_cd, 48)

            def body(r):
                if r.att:
                    load_terms(r, 0, 3)
                if r.tail:
                    sp.wait_ge(s_fin, r.count(1, -2, 1))
                    sp.dma_start(seq(out, r, -2).rearrange("a (k p) d -> p (a k) d", p=P), o_tok[:]).then_inc(s_out, 16)
                if r.att:
                    load_maxima(r, 0, 1)
                if r.nxt:
                    for k in range(TB):
                        sp.wait_ge(s_pl, r.count(TB, 1, k + 1))
                        sp.wait_ge(s_pm, r.count(TB, 1, k + 1))
                        sp.wait_ge(s_ph, r.count(TB, 1, k + 1))
                        sp.wait_ge(s_terms[3], r.count(LOADS, 0, LOADS))
                        cols = slice((k % 2) * P, (k % 2 + 1) * P)
                        sp.dma_start(parts_dram[:, :, :, k * P:(k + 1) * P].rearrange("a c p t -> p (a c) t"),
                                     parts[:, :, :, cols].rearrange("p a c t -> p (a c) t")).then_inc(s_pw[k % 2], 16)
                    load_terms(r, 1, 0)
                if r.att:
                    load_maxima(r, 0, 2)
                if r.nxt:
                    load_terms(r, 1, 1)
                if r.early:
                    x_read, x2_read, divided = r.held(sp, 1, 2, 0), r.held(sp, 1, -1, 1), r.held(sp, TB, 2, 0)
                    sp.wait_ge(s_xt, x_read)
                    sp.wait_ge(s_x2t, x2_read)
                    sp.wait_ge(s_pl, divided)
                    sp.dma_start(h_in[:], pe.rearrange("(k p) d -> p k d", p=P)).then_inc(s_tab, 16)
                    sp.wait_ge(s_gat, r.count(64, 2, 0))
                    sp.dma_start(idx[:], seq(x, r, 2).rearrange("a p k -> (a p) k")).then_inc(s_idx, 16)
                if r.att:
                    sp.wait_ge(s_h1, r.count(1, 0, 0))
                    sp.dma_start(res[:], base_dram.rearrange("(k p) d -> p k d", p=P)).then_inc(s_tabr, 16)
                    sp.wait_ge(s_gatr, r.count(64, 0, 0))
                    sp.dma_start(idx_res[:], seq(x, r, 0).rearrange("a p k -> (a p) k")).then_inc(s_idxr, 16)
                    load_maxima(r, 0, 3)
                if r.nxt:
                    load_terms(r, 1, 2)
                    load_maxima(r, 1, 0)

            def load_maxima(r, d, g):
                turned, scored = r.held(sp, HG, d, g + 1), r.held(sp, HG * STEPS, d - 1, STEPS * (g + 1))
                sp.wait_ge(s_me, turned)
                sp.wait_ge(s_sf, scored)
                for a in range(3):
                    sp.dma_start(q_terms[KS + a:KS + a + 1, g, :, :], max_rows[HH * a:HH * (a + 1), :]).then_inc(s_mrow[g], 16)

            def load_terms(r, d, g):
                stored, scored = r.held(sp, STORES, d, STORES), r.held(sp, HG * STEPS, d - 1, STEPS * (g + 1))
                sp.wait_ge(s_pw[0], stored)
                sp.wait_ge(s_pw[1], stored)
                sp.wait_ge(s_sf, scored)
                rows = slice((g % 2) * 64, (g % 2) * 64 + 64)
                for j in range(NT):
                    for c, terms, dst in ((0, TERMS_Q, q_terms), (2, TERMS_K, k_terms)):
                        sp.dma_start(dst[DK * j:DK * (j + 1), g, :, :],
                                     parts_dram[terms[j], c + g // 2, rows, :].rearrange("(h i) t -> i h t", i=DK))\
                            .then_inc(s_terms[g], 16)

            rounds(sp, body)
            sp.wait_ge(s_out, 16 * NB)

        @block.tensor
        def _(pe_eng):
            t_eng = pe_eng

            def product(dst, lh, ll, rh, rl, first, last):
                t_eng.matmul(dst, lh, rh, start=first, stop=False, skip_group_check=True)
                t_eng.matmul(dst, lh, rl, start=False, stop=False, skip_group_check=True)
                return t_eng.matmul(dst, ll, rh, start=False, stop=last, skip_group_check=True)

            def plain_scores(r, d, g, f):
                head = f // len(MAX_FILLS)
                use = ("plain", d, NF * g + f)
                t_eng.wait_ge(s_terms[g], r.count(LOADS, d, LOADS))
                t_eng.wait_ge(*ring_free(r, use))
                off = 0
                for qb in MAX_FILLS[f % len(MAX_FILLS)]:
                    last = t_eng.matmul(ring[:, ring_bank(use), off:off + (qb + 1) * P], q_terms[0:KS, g, head, qb * P:(qb + 1) * P],
                                        k_terms[0:KS, g, head, 0:(qb + 1) * P], start=True, stop=True)
                    off += (qb + 1) * P
                last.then_inc(s_mf, 1)

            def scores(r, g, i):
                t_eng.wait_ge(s_mrow[g], r.count(48, 0, 48))
                t_eng.wait_ge(s_exp, r.count(HG * STEPS, 0, STEPS * g + i))
                off = 0
                for kb in ROUND_KEYS[i // HH]:
                    n = T - kb * P
                    last = t_eng.matmul(bank_s[:, 0, off:off + n], k_terms[0:KM, g, i % HH, kb * P:(kb + 1) * P],
                                        q_terms[0:KM, g, i % HH, kb * P:T], start=True, stop=True)
                    off += n
                last.then_inc(s_sf, 1)

            def probs_v(r, d, g, rd):
                t_eng.wait_ge(s_mask, r.count(HG * STEPS, d, STEPS * g + HH * rd + HH))
                t_eng.wait_ge(s_exp, r.count(HG * STEPS, d, STEPS * g + HH * rd + HH))
                t_eng.wait_ge(s_v, r.count(1, d, 1))
                if rd == 0:
                    t_eng.wait_ge(s_oe, r.count(HG, d, g))
                buf = probs1 if rd == 1 else probs0
                off = 0
                for kb in ROUND_KEYS[rd]:
                    n = T - kb * P
                    for hh in range(HH):
                        last = t_eng.matmul(bank_o[32 * hh:32 * hh + DK + 1, 0, kb * P:T], v_aug[:, kb, HH * g + hh, :],
                                            buf[:, hh, off:off + n], start=(kb == 0), stop=(kb == TB - 1),
                                            skip_group_check=True)
                    off += n
                last.then_inc(s_pv, 1)

            def turn(dst, src, last_sem):
                for c in range(DC):
                    for k in range(TB):
                        last = t_eng.transpose(dst[:, c, k * P:(k + 1) * P], src[:, k, c * P:(c + 1) * P], ident[:])
                last.then_inc(last_sem, 1)

            def qkv(r, k):
                n = TB
                t_eng.wait_ge(s_xh, r.count(2, 1, 2))
                t_eng.wait_ge(s_xl, r.count(2, 1, 2))
                if r.n < 0:
                    t_eng.wait_ge(s_wl, 3)
                t_eng.wait_ge(s_h1, r.count(1, -1, 1))
                t_eng.wait_ge(s_gx, r.count(2 * CH, -2, 2 * CH))
                t_eng.wait_ge(s_qk, r.count(n, 1, k))
                t_eng.wait_ge(s_vn, r.count(n, 1, k))
                for b, cols in ((0, slice(0, 512)), (1, slice(512, 768))):
                    dst = bank_fg[:, b, 0:cols.stop - cols.start]
                    for c in range(DC):
                        rows = slice(k * P, (k + 1) * P)
                        last = product(dst, a_h[:, c, rows], a_l[:, c, rows], wqkv_h[:, c, cols], wqkv_l[:, c, cols],
                                       c == 0, c == DC - 1)
                last.then_inc(s_qkv, 1)

            def turn_qk(r, k):
                if k >= 2:
                    t_eng.wait_ge(s_pc, r.count(TB, 1, k - 1))
                    t_eng.wait_ge(s_ph, r.count(TB, 1, k - 1))
                else:
                    t_eng.wait_ge(s_x2h, r.count(2, -1, 2))
                    t_eng.wait_ge(s_x2l, r.count(2, -1, 2))
                    t_eng.wait_ge(s_xh, r.count(2, 1, 2))
                    t_eng.wait_ge(s_xl, r.count(2, 1, 2))
                t_eng.wait_ge(s_rot, r.count(TB, 1, k + 1))
                for c in range(4):
                    last = t_eng.transpose(bank_y[:, k % 2, c * P:(c + 1) * P], cb[:, 0, c * P:(c + 1) * P], ident[:])
                last.then_inc(s_qt, 1)

            def experts(r, d, m, part):
                c, k = m // 4, m % 4
                half = k // 2
                if part == 0 and m == 2:
                    spread_weights(r, d, 0)
                if k % 2 == 0 and c < CH:
                    i = 2 * c + half
                    if part == 0:
                        free = i if c == 0 or (c == 1 and half == 0) else i - 1
                        t_eng.wait_ge(s_gx, r.count(2 * CH, d, free))
                    if part == 0 and i == 0:
                        t_eng.wait_ge(s_x2h, r.count(2, d, 2))
                        t_eng.wait_ge(s_x2l, r.count(2, d, 2))
                        t_eng.wait_ge(s_qk, r.count(TB, d + 2, TB))
                        t_eng.wait_ge(s_vn, r.count(TB, d + 2, TB))
                        t_eng.wait_ge(s_h1, r.count(1, d, 1))
                        if r.n <= 1:
                            t_eng.wait_ge(s_wl, len(weight_pieces()))
                    cols = slice(half * P, half * P + P)
                    dc = part
                    if c == 0:
                        product(bank_fg[:, 0, :], wgu_h[:, dc, cols], wgu_l[:, dc, cols], x2_h[:, dc, :], x2_l[:, dc, :],
                                dc == 0, dc == DC - 1)
                        up = slice(F + half * P, F + half * P + P)
                        last = product(bank_fg[:, 1, :], wgu_h[:, dc, up], wgu_l[:, dc, up], x2_h[:, dc, :], x2_l[:, dc, :],
                                       dc == 0, dc == DC - 1)
                    else:
                        last = product(bank_fg[:, half, :], w1_h[:, dc, c - 1, cols], w1_l[:, dc, c - 1, cols],
                                       x2_h[:, dc, :], x2_l[:, dc, :], dc == 0, dc == DC - 1)
                    if part == 1:
                        last.then_inc(s_up, 1)
                if k % 2 == 1:
                    cc, half = (c - 1, 1) if k == 1 else (c, 0)
                    if 0 <= cc < CH:
                        i = 2 * cc + half
                        if part == 0:
                            t_eng.wait_ge(s_gl, r.count(2 * CH, d, i + 1))
                        if part == 0 and i == 0:
                            t_eng.wait_ge(s_pc, r.count(TB, d + 2, TB))
                            t_eng.wait_ge(s_ph, r.count(TB, d + 2, TB))
                        dd = part
                        cols = slice(dd * P, dd * P + P)
                        wh, wl = (wdn_h[:, half, cols], wdn_l[:, half, cols]) if cc == 0 else \
                                 (w2_h[:, half, cc - 1, cols], w2_l[:, half, cc - 1, cols])
                        last = product(bank_y[:, dd, :], wh, wl, a_h[:, half, :], a_l[:, half, :], i == 0, i == 2 * CH - 1)
                        if part == 1:
                            last.then_inc(s_dn, 1)
                if part == 1 and k == 3 and c + 1 < CH:
                    spread_weights(r, d, c + 1)

            def spread_weights(r, d, c):
                t_eng.wait_ge(s_ce, r.count(1, d, 1))
                t_eng.wait_ge(*ring_free(r, ("spread", d, c)))
                t_eng.matmul(ring[:, ring_bank(("spread", d, c)), :], spread[:, (c + CH - 1) % CH, :], cw_rows[:], start=True, stop=True)\
                    .then_inc(s_sp, 1)

            def body(r):
                for s in range(4):
                    for i in range(STEPS):
                        d, m = moe_step(s, i)
                        plain_d = 1 if s == 3 else 0
                        fills = max_fills(i) if r.has[plain_d] else []
                        moe = r.has[d] and 0 <= m <= MOE_LAST
                        if len(fills) == 2:
                            plain_scores(r, plain_d, (s + 1) % HG, fills[0])
                        if moe:
                            experts(r, d, m, 0)
                        if i == 0 and r.has[-1 if s == 0 else 0]:
                            probs_v(r, -1 if s == 0 else 0, (s - 1) % HG, 2)
                        if r.att and i in (5, 9):
                            probs_v(r, 0, s, (i - 5) // 4)
                        if r.att:
                            scores(r, s, i)
                        if len(fills) == 1:
                            plain_scores(r, plain_d, (s + 1) % HG, fills[0])
                        if moe:
                            experts(r, d, m, 1)
                        if len(fills) == 2:
                            plain_scores(r, plain_d, (s + 1) % HG, fills[1])
                        if i == 3 and r.has[-1 if s == 0 else 0]:
                            hd, g = (-1, 3) if s == 0 else (0, s - 1)
                            t_eng.wait_ge(s_oe, r.count(HG, hd, g + 1))
                            t_eng.wait_ge(*ring_free(r, ("heads", hd, g)))
                            for k in range(TB):
                                last = t_eng.transpose(ring[:, ring_bank(("heads", hd, g)), k * P:(k + 1) * P], heads_t[:, k * P:(k + 1) * P], ident[:])
                            last.then_inc(s_ot, 1)
                        if i == 9 and r.has[plain_d]:
                            g = (s + 1) % HG
                            t_eng.wait_ge(s_mc, r.count(4 * HG, plain_d, 4 * g + 4))
                            t_eng.wait_ge(*ring_free(r, ("maxima", plain_d, g)))
                            turned = ring[:, ring_bank(("maxima", plain_d, g)), :].bitcast(BF16)
                            for k in range(TB):
                                last = t_eng.transpose(turned[0:3 * HH, k * P:(k + 1) * P],
                                                       max_parts[:, k, :, :].rearrange("p a h -> p (a h)"), identb[:])
                            last.then_inc(s_mt, 1)
                        if s == 0 and i == 5 and r.epi:
                            t_eng.wait_ge(s_on, r.count(HG, -1, HG))
                            t_eng.wait_ge(s_gx, r.count(2 * CH, -2, 2 * CH))
                            t_eng.wait_ge(s_qk, r.count(TB, 0, TB))
                            t_eng.wait_ge(s_vn, r.count(TB, 0, TB))
                            turn(bank_fg, o_tok, s_ott)
                        if s == 0 and i == 6 and r.tail:
                            t_eng.wait_ge(s_ye, r.count(1, -2, 1))
                            for k in range(TB):
                                for dd in range(DC):
                                    off = (k % 2) * D + dd * P
                                    last = t_eng.transpose(bank_y[:, k // 2, off:off + P], hid[:, dd, k * P:(k + 1) * P], ident[:])
                            last.then_inc(s_yt, 1)
                        if s == 0 and i == 7 and r.epi:
                            t_eng.wait_ge(s_oh, r.count(2, -1, 2))
                            t_eng.wait_ge(s_ol, r.count(2, -1, 2))
                            if r.n <= 1:
                                t_eng.wait_ge(s_wl, 4)
                            for k in range(TB):
                                for c in range(DC):
                                    rows = slice(k * P, (k + 1) * P)
                                    last = product(bank_fg[:, k // 2, (k % 2) * D:(k % 2 + 1) * D], a_h[:, c, rows], a_l[:, c, rows],
                                                   wo_h[:, c, :], wo_l[:, c, :], c == 0, c == DC - 1)
                            last.then_inc(s_op, 1)
                        if s == 0 and i == 8 and r.nxt:
                            t_eng.wait_ge(s_n1, r.count(N_OPS, 1, N_OPS))
                            t_eng.wait_ge(s_fin, r.count(1, -2, 1))
                            t_eng.wait_ge(s_pc, r.count(TB, 0, TB))
                            t_eng.wait_ge(s_ph, r.count(TB, 0, TB))
                            t_eng.wait_ge(s_x2h, r.count(2, -2, 2))
                            turn(bank_y, h_in, s_xt)
                        if s == 0 and i == 10 and r.nxt:
                            qkv(r, 0)
                        if s == 0 and i == 11 and r.epi:
                            t_eng.wait_ge(s_n2, r.count(N_OPS, -1, N_OPS))
                            t_eng.wait_ge(s_xh, r.count(2, 1, 2))
                            t_eng.wait_ge(s_xl, r.count(2, 1, 2))
                            t_eng.wait_ge(s_fin, r.count(1, -2, 1))
                            t_eng.wait_ge(s_pc, r.count(TB, 0, TB))
                            t_eng.wait_ge(s_ph, r.count(TB, 0, TB))
                            turn(bank_y, h_in, s_x2t)
                        if s == 1 and i < TB and r.nxt:
                            if i + 1 < TB:
                                qkv(r, i + 1)
                            turn_qk(r, i)
                        if s == 1 and i == 1 and r.epi:
                            t_eng.wait_ge(s_x2h, r.count(2, -1, 2))
                            t_eng.wait_ge(s_x2l, r.count(2, -1, 2))
                            if r.n <= 1:
                                t_eng.wait_ge(s_wl, 5)
                            t_eng.wait_ge(*ring_free(r, ("router", -1, 0)))
                            for k in range(TB):
                                for c in range(DC):
                                    rows = slice(k * P, (k + 1) * P)
                                    last = product(ring[:, ring_bank(("router", -1, 0)), k * (E + 2):(k + 1) * (E + 2)], x2_h[:, c, rows], x2_l[:, c, rows],
                                                   wr_h[:, c, :], wr_l[:, c, :], c == 0, c == DC - 1)
                            last.then_inc(s_rt, 1)
                        if s == 1 and i == 4 and r.epi:
                            t_eng.wait_ge(s_cw, r.count(CW_OPS, -1, CW_OPS))
                            t_eng.wait_ge(*ring_free(r, ("weights", -1, 0)))
                            turned = ring[:, ring_bank(("weights", -1, 0)), :].bitcast(BF16)
                            for k in range(TB):
                                last = t_eng.transpose(turned[:, k * P:(k + 1) * P], cw_parts[:, k, :], identb[:])
                            last.then_inc(s_ct, 1)

            t_eng.wait_ge(go, 1)
            rounds(t_eng, body)

        @block.scalar
        def _(act):
            def split_weight(n):
                _, hi, _, width = weight_pieces()[n]
                if n < FIRST_PIECES:
                    act.wait_ge(s_wd[n % 2], 16 * (n // 2 + 1))
                else:
                    act.wait_ge(s_we[n % 2], 16 * ((n - FIRST_PIECES) // 2 + 1))
                nc.scalar.activation(hi, stage(n, width), ACT.Copy).then_inc(s_wh, 1)

            for n in range(FIRST_PIECES):
                split_weight(n)

            def experts(r, d, m):
                c, k = m // 4, m % 4
                i = 2 * c + k // 2
                if k % 2 == 1 and c < CH:
                    act.wait_ge(s_up, r.count(2 * CH, d, i + 1))
                    act.wait_ge(s_gl, r.count(2 * CH, d, i - 1))
                    if i < 2:
                        act.wait_ge(s_gl, r.count(2 * CH, d - 1, 2 * CH))
                    if i < 2:
                        act.wait_ge(s_rot, r.count(TB, d + 2, TB))
                    if i < 2:
                        act.wait_ge(s_yt, r.count(1, d - 1, 1))
                    nc.scalar.activation(hid[:, k // 2, :], bank_fg[:, 0 if c == 0 else k // 2, :], ACT.Tanh, scale=0.5)\
                        .then_inc(s_th, 1)

            def experts_high(r, d, m):
                c, k = m // 4, m % 4
                cc, half = (c, 0) if k == 2 else (c - 1, 1)
                if k % 2 == 0 and 0 <= cc < CH:
                    i = 2 * cc + half
                    act.wait_ge(s_g, r.count(2 * CH, d, i + 1))
                    act.wait_ge(s_dn, r.count(2 * CH, d, i - 1))
                    if i < 2:
                        act.wait_ge(s_qkv, r.count(TB, d + 2, TB))
                    if i < 2:
                        act.wait_ge(s_op, r.count(1, d, 1))
                    nc.scalar.activation(a_h[:, half, :], hid[:, half, :], ACT.Copy).then_inc(s_gh, 1)

            def weights_out(r, d, c):
                act.wait_ge(s_sp, r.count(CH, d, c + 1))
                if c >= 2:
                    act.wait_ge(s_g, r.count(2 * CH, d, 2 * (c - 1)))
                if c < 2:
                    act.wait_ge(s_qt, r.count(TB, d + 2, TB))
                if c < 2:
                    act.wait_ge(s_g, r.count(2 * CH, d - 1, 2 * CH))
                nc.scalar.activation(cb[:, c % 2, :], ring[:, ring_bank(("spread", d, c)), :], ACT.Copy).then_inc(s_cb, 1)

            def high(src, dst, sem_out):
                for c in range(DC):
                    nc.scalar.activation(dst[:, c, :], src[:, c, :], ACT.Copy).then_inc(sem_out, 1)

            def body(r):
                for s in range(4):
                    for i in range(STEPS):
                        d, m = moe_step(s, i)
                        moe = r.has[d] and 0 <= m <= MOE_LAST
                        if moe:
                            experts(r, d, m)
                            if m == 2:
                                weights_out(r, d, 0)
                            experts_high(r, d, m)
                        if r.att:
                            buf, rd = (probs1 if i // HH == 1 else probs0), i // HH
                            g3 = NR * s
                            free = {0: g3, 1: g3 - 1, 2: g3 + 1}[rd]
                            act.wait_ge(s_sf, r.count(HG * STEPS, 0, STEPS * s + i + 1))
                            act.wait_ge(s_pv, r.count(HG * NR, 0, free))
                            n = T if rd == 0 else 3 * P
                            nc.scalar.activation(buf[:, i % HH, 0:n], bank_s[:, 0, 0:n], ACT.Exp, scale=SCALE).then_inc(s_exp, 1)
                        if moe and m % 4 == 3 and m // 4 + 1 < CH:
                            weights_out(r, d, m // 4 + 1)
                        hd, hg = (-1, 3) if s == 0 else (0, s - 1)
                        if i == 0 and r.has[hd]:
                            act.wait_ge(s_pv, r.count(HG * NR, hd, NR * (hg + 1)))
                            act.wait_ge(s_ot, r.count(HG, hd, hg))
                            nc.scalar.activation(heads_t[:], bank_o[:, 0, :], ACT.Copy).then_inc(s_oe, 1)
                        pd = 1 if s == 3 else 0
                        if i == 9 and r.has[pd]:
                            g = (s + 1) % HG
                            act.wait_ge(s_mt, r.count(HG, pd, g + 1))
                            act.wait_ge(s_mrow[(g - 1) % HG], r.count(48, pd - (g == 0), 48))
                            turned = ring[:, ring_bank(("maxima", pd, g)), :].bitcast(BF16)
                            nc.scalar.activation(max_rows[:], turned[0:3 * HH, 0:T], ACT.Copy).then_inc(s_me, 1)
                        if s == 0 and i == 5 and r.tail:
                            act.wait_ge(s_dn, r.count(2 * CH, -2, 2 * CH))
                            for dd in range(DC):
                                y = nc.scalar.activation(hid[:, dd, :], bank_y[:, dd, :], ACT.Copy)
                            y.then_inc(s_ye, 1)
                        if s == 0 and i == 5 and r.epi:
                            act.wait_ge(s_ott, r.count(1, -1, 1))
                            act.wait_ge(s_dn, r.count(2 * CH, -2, 2 * CH))
                            act.wait_ge(s_qkv, r.count(TB, 0, TB))
                            high(bank_fg, a_h, s_oh)
                        if s == 0 and i == 8 and r.nxt:
                            act.wait_ge(s_xt, r.count(1, 1, 1))
                            act.wait_ge(s_op, r.count(1, -1, 1))
                            act.wait_ge(s_qkv, r.count(TB, 0, TB))
                            high(bank_y, a_h, s_xh)
                        if s == 0 and i == 11 and r.epi:
                            act.wait_ge(s_x2t, r.count(1, -1, 1))
                            act.wait_ge(s_up, r.count(2 * CH, -2, 2 * CH))
                            act.wait_ge(s_rt, r.count(1, -2, 1))
                            high(bank_y, x2_h, s_x2h)
                        if s == 1 and i == 2 and r.epi:
                            act.wait_ge(s_lg, r.count(3, -1, 3))
                            act.wait_ge(s_cw, r.count(CW_OPS, -2, CW_OPS))
                            nc.scalar.activation(ex[:], logit[:], ACT.Exp).then_inc(s_ex, 1)
                        if s == 1 and i == 4 and r.epi:
                            act.wait_ge(s_ct, r.count(1, -1, 1))
                            act.wait_ge(s_sp, r.count(CH, -2, CH))
                            turned = ring[:, ring_bank(("weights", -1, 0)), :].bitcast(BF16)
                            nc.scalar.activation(cw_rows[:], turned[:, 0:T], ACT.Copy).then_inc(s_ce, 1)
                        if s == 1 and 1 <= i <= TB and r.nxt:
                            k = i - 1
                            cols = slice((k % 2) * P, (k % 2 + 1) * P)
                            act.wait_ge(s_pr, r.count(TB, 1, k + 1))
                            act.wait_ge(s_pw[k % 2], r.count(STORES, 1, 16 * (k // 2)))
                            nc.scalar.activation(parts[:, 1, :, cols], split[:, k % 2, :].rearrange("p (c t) -> p c t", c=4),
                                                 ACT.Copy).then_inc(s_pm, 1)
                        if s == 1 and i < TB and r.nxt:
                            k = i
                            cols = slice((k % 2) * P, (k % 2 + 1) * P)
                            turned = bank_y[:, k % 2, :]
                            act.wait_ge(s_qt, r.count(TB, 1, k + 1))
                            act.wait_ge(s_pl, r.count(TB, 1, k - 1))
                            nc.scalar.activation(split[:, k % 2, :], turned, ACT.Copy).then_inc(s_pc, 1)
                            act.wait_ge(s_pw[k % 2], r.count(STORES, 1, 16 * (k // 2)))
                            nc.scalar.activation(parts[:, 0, :, cols], turned.rearrange("p (c t) -> p c t", c=4),
                                                 ACT.Copy).then_inc(s_ph, 1)
                        n = FIRST_PIECES + STEPS * (s - 1) + i
                        if r.n == 0 and FIRST_PIECES <= n + 1 < len(weight_pieces()):
                            src, _, _, width = weight_pieces()[n + 1]
                            act.wait_ge(s_wl, n)
                            act.dma_start(stage(n + 1, width), src).then_inc(s_we[(n + 1) % 2], 16)
                        if r.n == 0 and FIRST_PIECES <= n < len(weight_pieces()):
                            split_weight(n)

            act.wait_ge(go, 1)
            rounds(act, body)

        @block.vector
        def _(dve):
            v = nc.vector
            v.memset(causal[:], 0.0).then_inc(s_cv, 1)
            v.memset(v_aug[:], 1.0).then_inc(s_cv, 1)
            v.memset(cw_parts[:], 0.0).then_inc(s_cv, 1)
            v.memset(bank_o[:, 0, :], 0.0).then_inc(s_cv, 1)
            v.memset(k_terms[KS:P, :, :, :].rearrange("p g h t -> p (g h t)"), 1.0).then_inc(s_cv, 1)
            dve.wait_ge(s_cp, 6)
            v.tensor_copy(identb[:], ident[:]).then_inc(s_cv, 1)
            dve.wait_ge(s_cv, 6)
            dve.wait_ge(s_ld, 48)
            v.memset(minus_half[:], -0.5).then_inc(go, 1)
            dve.wait_ge(s_cd, 32)
            v.tensor_tensor(res[:], res[:], v_new[:, 0:1, :].broadcast_to([P, TB, D]), ALU.add).then_inc(s_base, 1)

            def low_weight(n):
                _, hi, lo, width = weight_pieces()[n]
                dve.wait_ge(s_wh, n + 1)
                v.tensor_tensor(lo, stage(n, width), hi.bitcast(F32), ALU.subtract).then_inc(s_wl, 1)

            for n in range(FIRST_PIECES):
                low_weight(n)

            def statistics(r, d, src, chain):
                for k in range(TB):
                    last = v.bn_stats(stats[:, k, :], src[:, k, :])
                last.then_inc(chain, 1)
                summed = r.held(dve, N_OPS, d, 1)
                dve.wait_ge(go, 1)
                dve.wait_ge(chain, summed)
                for k in range(TB):
                    last = v.bn_aggr(mv[:, k, :], stats[:, k, :])
                last.then_inc(chain, 1)
                dve.wait_ge(chain, r.count(N_OPS, d, 2))
                v.tensor_scalar(var_eps[:], mv[:, :, 1], EPS, None, ALU.add).then_inc(chain, 1)

            def normalise(src, chain):
                for k in range(TB):
                    last = v.tensor_scalar(h_in[:, k, :], src[:, k, :], mv[:, k, 0:1], rstd[:, k:k + 1], ALU.subtract, ALU.mult)
                last.then_inc(chain, 1)

            def low(r, d, src, hi, lo, filled, sem_out):
                for c in range(DC):
                    dve.wait_ge(filled, r.count(2, d, c + 1))
                    v.tensor_tensor(lo[:, c, :], src[:, c, :], hi[:, c, :].bitcast(F32), ALU.subtract).then_inc(sem_out, 1)

            def maxima(r, d, g, f):
                filled = r.held(dve, HG * NF, d, NF * g + f + 1)
                dve.wait_ge(go, 1)
                dve.wait_ge(s_mf, filled)
                b, off = ring_bank(("plain", d, NF * g + f)), 0
                for qb in MAX_FILLS[f % len(MAX_FILLS)]:
                    n = (qb + 1) * P
                    last = v.tensor_tensor_reduce(ring[:, b, off:off + n], ring[:, b, off:off + n], causal[:, T - n:T], 1.0, NEG,
                                                  ALU.add, ALU.max, row_max[:, qb, f // len(MAX_FILLS):f // len(MAX_FILLS) + 1])
                    off += n
                last.then_inc(s_mr, 1)

            def experts(r, d, m):
                c, k = m // 4, m % 4
                if k % 2 == 1 and c < CH:
                    half, i = k // 2, 2 * c + k // 2
                    dve.wait_ge(s_th, r.count(2 * CH, d, i + 1))
                    op = v.scalar_tensor_tensor(out=hid[:, half, :], in0=hid[:, half, :], scalar=1.0,
                                                in1=bank_fg[:, 0 if c == 0 else half, :], op0=ALU.add, op1=ALU.mult)
                    if c == 0:
                        op.then_inc(s_gs, 1)
                        dve.wait_ge(s_gs, r.count(2, d, half + 1))
                        op = v.tensor_tensor(hid[:, half, :], hid[:, half, :], bank_fg[:, 1, :], ALU.mult)
                    op.then_inc(s_gx, 1)
                    if i > 0:
                        weigh(r, d, i)
                if m == 2:
                    weigh(r, d, 0)
                cc, half = (c, 0) if k == 2 else (c - 1, 1)
                if k % 2 == 0 and 0 <= cc < CH:
                    i = 2 * cc + half
                    dve.wait_ge(s_gh, r.count(2 * CH, d, i + 1))
                    v.tensor_tensor(a_l[:, half, :], hid[:, half, :], a_h[:, half, :].bitcast(F32), ALU.subtract).then_inc(s_gl, 1)

            def weigh(r, d, i):
                dve.wait_ge(s_gx, r.count(2 * CH, d, i + 1))
                dve.wait_ge(s_cb, r.count(CH, d, i // 2 + 1))
                v.tensor_tensor(hid[:, i % 2, :], hid[:, i % 2, :], cb[:, i // 2 % 2, :], ALU.mult).then_inc(s_g, 1)

            def shift_logits(r):
                lg = ring[:, ring_bank(("router", -1, 0)), 0:TB * (E + 2)].rearrange("p (k e) -> p k e", k=TB)
                dve.wait_ge(s_rt, r.count(1, -1, 1))
                v.tensor_reduce(nmax[:], lg[:, :, 0:E], AX.X, ALU.max).then_inc(s_lg, 1)
                dve.wait_ge(s_lg, r.count(3, -1, 1))
                dve.wait_ge(s_ex, r.count(1, -2, 1))
                v.tensor_tensor(logit[:, :, 0:E], lg[:, :, 0:E], nmax[:, :].unsqueeze(2).broadcast_to([P, TB, E]), ALU.subtract)\
                    .then_inc(s_lg, 1)
                v.tensor_scalar(logit[:, :, E:CH], lg[:, :, E:CH], -1.0, None, ALU.mult).then_inc(s_lg, 1)

            def route(r):
                base = -1
                done = [0]

                def link(op):
                    done[0] += 1
                    op.then_inc(s_cw, 1)

                def linked():
                    dve.wait_ge(s_cw, r.count(CW_OPS, base, done[0]))

                def linked_alone():
                    so_far = r.held(dve, CW_OPS, base, done[0])
                    dve.wait_ge(go, 1)
                    dve.wait_ge(s_cw, so_far)

                dve.wait_ge(s_ex, r.count(1, -1, 1))
                dve.wait_ge(s_lg, r.count(3, -1, 3))
                link(v.tensor_reduce(esum[:], ex[:, :, 0:E], AX.X, ALU.add))
                linked()
                link(v.reciprocal(erec[:], esum[:]))
                linked()
                link(v.tensor_tensor(pr[:], ex[:, :, 0:E], erec[:, :].unsqueeze(2).broadcast_to([P, TB, E]), ALU.mult))
                linked_alone()
                for k in range(TB):
                    op = v.max(top8[:, k, :], pr[:, k, :])
                link(op)
                linked_alone()
                for k in range(TB):
                    op = v.max_index(top_i[:, k, :], top8[:, k, :], pr[:, k, :])
                link(op)
                linked()
                link(v.tensor_copy(top_f[:], top_i[:, :, 0:2]))
                linked()
                for dst, j in ((pick, 0), (pick2, 1)):
                    link(v.tensor_tensor(dst[:], iota8[:, :].unsqueeze(1).broadcast_to([P, TB, E]),
                                         top_f[:, :, j:j + 1].broadcast_to([P, TB, E]), ALU.is_equal))
                linked()
                link(v.tensor_tensor(pick[:], pick[:], pick2[:], ALU.add))
                linked()
                link(v.scalar_tensor_tensor(out=cw[:, :, 0:E], in0=pick[:], scalar=0.5, in1=pr[:], op0=ALU.mult, op1=ALU.mult))
                link(v.tensor_scalar(den[:], ex[:, :, E], 1.0, None, ALU.add))
                linked()
                link(v.reciprocal(den[:], den[:]))
                linked()
                link(v.tensor_scalar(cw[:, :, E], den[:], 0.5, None, ALU.mult))
                linked()
                dve.wait_ge(s_ct, r.count(1, -2, 1))
                link(v.tensor_copy(cw_parts[:, :, 0:CH], cw[:]))
                linked()
                link(v.tensor_tensor(cw_rest[:], cw[:], cw_parts[:, :, 0:CH], ALU.subtract))
                linked()
                link(v.tensor_copy(cw_parts[:, :, CH:2 * CH], cw_rest[:]))
                linked()
                link(v.tensor_tensor(cw_parts[:, :, 2 * CH:3 * CH], cw_rest[:], cw_parts[:, :, CH:2 * CH], ALU.subtract))
                assert done[0] == CW_OPS

            def body(r):
                for s in range(4):
                    for i in range(STEPS):
                        d, m = moe_step(s, i)
                        pd, pg = (1 if s == 3 else 0), (s + 1) % HG
                        fills = max_fills(i) if r.has[pd] else []
                        if len(fills) == 2:
                            maxima(r, pd, pg, fills[0])
                        if r.has[d] and 0 <= m <= MOE_LAST:
                            experts(r, d, m)
                        if fills:
                            maxima(r, pd, pg, fills[-1])
                        if i == 8 and r.has[pd]:
                            n = 4 * HG
                            dve.wait_ge(s_mr, r.count(HG * NF, pd, NF * (pg + 1)))
                            dve.wait_ge(s_mt, r.count(HG, pd, pg))
                            v.tensor_scalar(max_parts[:, :, 0, :], row_max[:], -1.0, None, ALU.mult).then_inc(s_mc, 1)
                            dve.wait_ge(s_mc, r.count(n, pd, 4 * pg + 1))
                            v.scalar_tensor_tensor(out=max_rest[:], in0=row_max[:], scalar=-1.0, in1=max_parts[:, :, 0, :],
                                                   op0=ALU.mult, op1=ALU.subtract).then_inc(s_mc, 1)
                            dve.wait_ge(s_mc, r.count(n, pd, 4 * pg + 2))
                            v.tensor_copy(max_parts[:, :, 1, :], max_rest[:]).then_inc(s_mc, 1)
                            dve.wait_ge(s_mc, r.count(n, pd, 4 * pg + 3))
                            v.tensor_tensor(max_parts[:, :, 2, :], max_rest[:], max_parts[:, :, 1, :], ALU.subtract).then_inc(s_mc, 1)
                        hd, hg = (-1, 3) if s == 0 else (0, s - 1)
                        if i == 3 and r.has[hd]:
                            ht = ring[:, ring_bank(("heads", hd, hg)), :].rearrange("p (k h w) -> p k h w", k=TB, h=HH)
                            dve.wait_ge(s_ot, r.count(HG, hd, hg + 1))
                            v.reciprocal(rec[:], ht[:, :, :, DK]).then_inc(s_or, 1)
                            dve.wait_ge(s_or, r.count(HG, hd, hg + 1))
                            dve.wait_ge(s_ott, r.count(1, hd, 0))
                            if s == 1:
                                dve.wait_ge(s_out, r.count(16, -2, 16))
                            v.tensor_tensor(o_tok[:, :, hg * HH * DK:(hg + 1) * HH * DK].rearrange("p k (h w) -> p k h w", h=HH),
                                            ht[:, :, :, 0:DK], rec[:].unsqueeze(3).broadcast_to([P, TB, HH, DK]), ALU.mult)\
                                .then_inc(s_on, 1)
                        if s == 3 and i == 8 and r.early:
                            dve.wait_ge(s_gat, r.count(64, 2, 64))
                            statistics(r, 2, h_in, s_n1)
                        if s == 3 and i == 10 and r.early:
                            dve.wait_ge(s_n1p, r.count(1, 2, 1))
                            normalise(h_in, s_n1)
                        if s == 0 and i == 5 and r.epi:
                            low(r, -1, bank_fg, a_h, a_l, s_oh, s_ol)
                        if s == 0 and i == 6 and r.tail:
                            dve.wait_ge(s_yt, r.count(1, -2, 1))
                            dve.wait_ge(s_ott, r.count(1, -1, 1))
                            dve.wait_ge(s_h1, r.count(1, -2, 1))
                            if not r.epi:
                                dve.wait_ge(s_out, r.count(16, -2, 0))
                            for half in range(2):
                                op = v.tensor_tensor(o_tok[:, 2 * half:2 * half + 2, :], bank_y[:, half, :].rearrange("p (k d) -> p k d", k=2),
                                                     h1[:, 2 * half:2 * half + 2, :], ALU.add)
                            op.then_inc(s_fin, 1)
                        if s == 0 and i == 7 and r.epi:
                            dve.wait_ge(s_op, r.count(1, -1, 1))
                            dve.wait_ge(s_gatr, r.count(64, -1, 64))
                            dve.wait_ge(s_fin, r.count(1, -2, 1))
                            if r.n <= 1:
                                dve.wait_ge(s_wl, len(weight_pieces()))
                            for half in range(2):
                                op = v.tensor_tensor(h1[:, 2 * half:2 * half + 2, :], bank_fg[:, half, :].rearrange("p (k d) -> p k d", k=2),
                                                     res[:, 2 * half:2 * half + 2, :], ALU.add)
                            op.then_inc(s_h1, 1)
                        if s == 0 and i == 8 and r.epi:
                            dve.wait_ge(s_h1, r.count(1, -1, 1))
                            statistics(r, -1, h1, s_n2)
                        if s == 0 and i == 8 and r.nxt:
                            low(r, 1, bank_y, a_h, a_l, s_xh, s_xl)
                        if s == 0 and i == 9 and r.epi:
                            dve.wait_ge(s_n2p, r.count(1, -1, 1))
                            dve.wait_ge(s_xt, r.count(1, 1, 1))
                            normalise(h1, s_n2)
                        if s == 0 and i == 11 and r.epi:
                            low(r, -1, bank_y, x2_h, x2_l, s_x2h, s_x2l)
                        if s == 0 and i == 10 and r.nxt:
                            biased(r, 0)
                        if s == 1 and i < TB and r.nxt:
                            rotated(r, i)
                            if i + 1 < TB:
                                biased(r, i + 1)
                        if s == 1 and i == 1 and r.epi:
                            shift_logits(r)
                        if s == 1 and i == 2 and r.epi:
                            route(r)
                        if r.n == 0 and s >= 1:
                            n = FIRST_PIECES + STEPS * (s - 1) + i
                            if n < len(weight_pieces()):
                                low_weight(n)

            def biased(r, k):
                dve.wait_ge(s_qkv, r.count(TB, 1, k + 1))
                dve.wait_ge(s_yt, r.count(1, -2, 1))
                dve.wait_ge(s_rot, r.count(TB, 1, k))
                dve.wait_ge(s_gl, r.count(2 * CH, -2, 2 * CH))
                v.tensor_tensor(hid[:, 0, :], bank_fg[:, 0, :], bias[:, 0:2 * D], ALU.add).then_inc(s_qk, 1)
                dve.wait_ge(s_v, r.count(1, 1, 0))
                if r.n < 0:
                    dve.wait_ge(s_base, 1)
                v.tensor_tensor(v_new[:, k, :], bank_fg[:, 1, 0:D], bias[:, 2 * D:3 * D], ALU.add).then_inc(s_vn, 1)
                dve.wait_ge(s_qk, r.count(TB, 1, k + 1))
                x = hid[:, 0, :].rearrange("p (h a w) -> p h a w", a=2, w=HALF)
                y = hid[:, 1, :].rearrange("p (h a w) -> p h a w", a=2, w=HALF)
                for a in range(2):
                    sn = sin_sb[:, k:k + 1, a * HALF:(a + 1) * HALF].broadcast_to([P, 2 * H, HALF])
                    op = v.tensor_tensor(y[:, :, a, :], x[:, :, 1 - a, :], sn, ALU.mult)
                op.then_inc(s_rs, 1)

            def rotated(r, k):
                dve.wait_ge(s_rs, r.count(TB, 1, k + 1))
                dve.wait_ge(s_rc, r.count(TB, 1, k + 1))
                v.tensor_tensor(cb[:, 0, :], cb[:, 0, :], hid[:, 1, :], ALU.add).then_inc(s_rot, 1)

            rounds(dve, body)

        @block.gpsimd
        def _(pool):
            g = nc.gpsimd
            g.memset(ident[:], 0.0).then_inc(s_cq, 1)
            g.memset(spread[:], 0.0).then_inc(s_cq, 1)
            pool.wait_ge(s_cq, 2)
            g.affine_select(out=ident[:], in_=ident[:], compare_op=ALU.not_equal, fill=1.0, base=0,
                            pattern=[[-1, P]], channel_multiplier=1).then_inc(s_cp, 1)
            for a in range(3):
                g.affine_select(out=spread[:], in_=spread[:], compare_op=ALU.not_equal, fill=1.0, base=-CH * a,
                                pattern=[[-1, CH], [0, P]], channel_multiplier=1).then_inc(s_cp, 1)
                pool.wait_ge(s_cp, a + 2)
            g.iota(iota8[:], pattern=[[1, E]], base=0, channel_multiplier=0,
                   allow_small_or_imprecise_dtypes=True).then_inc(s_cp, 1)
            pool.wait_ge(s_cv, 1)
            last = causal[:, T - P:T]
            g.affine_select(out=last, in_=last, compare_op=ALU.is_ge, fill=NEG, base=0,
                            pattern=[[-1, P]], channel_multiplier=1).then_inc(s_cp, 1)
            pool.wait_ge(go, 1)

            def gather(r, d, dst, tab, ids, row_ids, done):
                here = r.held(pool, 16, d, 16)
                pool.wait_ge(go, 1)
                pool.wait_ge(tab, here)
                pool.wait_ge(ids, here)
                for k in range(TB):
                    g.indirect_dma_start(out=dst[:, k, :], out_offset=None, in_=table,
                                         in_offset=bass.IndirectOffsetOnAxis(ap=row_ids[:, k:k + 1], axis=0),
                                         compute_op=ALU.add).then_inc(done, 16)

            def power(r, d, chain, pooled):
                pool.wait_ge(chain, r.count(N_OPS, d, 3))
                g.tensor_tensor(rstd[:], var_eps[:], minus_half[:], ALU.pow).then_inc(pooled, 1)

            def body(r):
                for s in range(4):
                    for i in range(STEPS):
                        d, m = moe_step(s, i)
                        if s == 0 and i == 1 and r.att:
                            projected, used = r.held(pool, TB, 0, TB), r.held(pool, HG * NR, 0, 0)
                            pool.wait_ge(go, 1)
                            pool.wait_ge(s_vn, projected)
                            pool.wait_ge(s_pv, used)
                            g.tensor_copy(v_aug[:, :, :, 0:DK], v_new[:].rearrange("p k (h w) -> p k h w", h=H)).then_inc(s_v, 1)
                        if s == 2 and i == 8 and r.early:
                            gather(r, 2, h_in, s_tab, s_idx, idx, s_gat)
                        if r.att:
                            rd, head = i // HH, i % HH
                            buf = probs1 if rd == 1 else probs0
                            written = r.held(pool, HG * STEPS, 0, STEPS * s + i + 1)
                            pool.wait_ge(go, 1)
                            pool.wait_ge(s_exp, written)
                            if rd == 2:
                                blk = buf[:, head, 0:T].rearrange("p (a c) -> p a c", a=2)[:, :, 0:P]
                                pattern = [[0, 2], [1, P]]
                            else:
                                blk = buf[:, head, 0:P]
                                pattern = [[1, P]]
                            g.affine_select(out=blk, in_=blk, compare_op=ALU.is_ge, fill=0.0, base=0,
                                            pattern=pattern, channel_multiplier=-1).then_inc(s_mask, 1)
                        if s == 3 and i == 8 and r.early:
                            power(r, 2, s_n1, s_n1p)
                        if s == 0 and i == 9 and r.epi:
                            power(r, -1, s_n2, s_n2p)
                        if s == 1 and 1 <= i <= TB and r.nxt:
                            k = i - 1
                            cols = slice((k % 2) * P, (k % 2 + 1) * P)
                            pool.wait_ge(s_pm, r.count(TB, 1, k + 1))
                            g.tensor_tensor(parts[:, 2, :, cols], split[:, k % 2, :].rearrange("p (c t) -> p c t", c=4),
                                            parts[:, 1, :, cols], ALU.subtract).then_inc(s_pl, 1)
                        k = {(0, 10): 0, (1, 0): 1, (1, 1): 2, (1, 2): 3}.get((s, i))
                        if k is not None and r.nxt:
                            pool.wait_ge(s_qk, r.count(TB, 1, k + 1))
                            pool.wait_ge(s_qt, r.count(TB, 1, k))
                            pool.wait_ge(s_g, r.count(2 * CH, -2, 2 * CH))
                            g.tensor_tensor(cb[:, 0, :].rearrange("p (h w) -> p h w", w=HALF),
                                            hid[:, 0, :].rearrange("p (h w) -> p h w", w=HALF),
                                            cos_sb[:, k:k + 1, :].broadcast_to([P, 4 * H, HALF]), ALU.mult).then_inc(s_rc, 1)
                        if s == 1 and i < TB and r.nxt:
                            k = i
                            cols = slice((k % 2) * P, (k % 2 + 1) * P)
                            rest = split[:, k % 2, :].rearrange("p (c t) -> p c t", c=4)
                            pool.wait_ge(s_pc, r.count(TB, 1, k + 1))
                            pool.wait_ge(s_ph, r.count(TB, 1, k + 1))
                            g.tensor_tensor(rest, rest, parts[:, 0, :, cols], ALU.subtract).then_inc(s_pr, 1)
                        if s == 2 and i == 4 and r.att:
                            gather(r, 0, res, s_tabr, s_idxr, idx_res, s_gatr)

            rounds(pool, body)


N_OPS = 4
CW_OPS = 17
FIRST_PIECES = 5


def tables():
    import numpy as np
    f = np.float32
    pos = np.arange(T, dtype=f)[:, None]
    i = np.arange(D // 2, dtype=f)[None, :]
    ang = (pos / np.power(f(10000.0), f(2.0) * i / f(D))).astype(f)
    pe = np.zeros((T, D), f)
    pe[:, 0::2], pe[:, 1::2] = np.sin(ang), np.cos(ang)
    freq = f(1.0) / np.power(f(10000.0), f(2.0) * np.arange(HALF, dtype=f) / f(DK))
    rot = (pos * freq[None, :]).astype(f)
    return pe, np.cos(rot).astype(f), np.concatenate([-np.sin(rot), np.sin(rot)], 1).astype(f)


def kernel(**inputs):
    import numpy as np
    import concourse.bacc as bacc
    from concourse.bass_utils import run_bass_kernel_spmd as run

    a = {k: np.asarray(v) for k, v in inputs.items()}
    pe, cos, sin2 = tables()
    layout = {
        "x": a["x"].reshape(NB, TB, P).transpose(0, 2, 1),
        "table": a["L0_tok_W"],
        "pe": pe, "cos": cos, "sin2": sin2,
        "wqkv": np.concatenate([a["L0_attn_WQ_w"].T, a["L0_attn_WK_w"].T, a["L0_attn_WV_w"].T], axis=1),
        "bqkv": np.concatenate([a["L0_attn_WQ_b"], a["L0_attn_WK_b"], a["L0_attn_WV_b"]]),
        "wo": a["L0_attn_Wo_w"].T,
        "bo": a["L0_attn_Wo_b"],
        "wr": np.concatenate([a["L0_ffn_router_w"], a["L0_ffn_shared_gate_w"], np.zeros((D, 1), np.float32)], axis=1),
        "w1": a["L0_ffn_w1"], "w2": a["L0_ffn_w2"],
        "wgu": a["L0_ffn_shared_gate_up"], "wdn": a["L0_ffn_shared_down"],
    }
    nc = bacc.Bacc("TRN2", target_bir_lowering=False, num_devices=1)
    arrays, args = {}, []
    for name, value in layout.items():
        value = np.ascontiguousarray(value)
        arrays["in_" + name] = value
        args.append(nc.dram_tensor("in_" + name, value.shape, mybir.dt.from_np(value.dtype), kind="ExternalInput").ap())
    out = nc.dram_tensor("out_0", (NB, T, D), F32, kind="ExternalOutput").ap()
    lm_block_kernel(nc, *args, out, loop=LOOP)
    r = run(nc, [arrays], core_ids=[0])
    return r.results[0]["out_0"]


LOOP = True
```

```python
from contextlib import ExitStack

import concourse.bass as bass
from concourse import mybir

F32 = mybir.dt.float32
F32R = mybir.dt.float32r
BF16 = mybir.dt.bfloat16
I32 = mybir.dt.int32
U32 = mybir.dt.uint32
ALU = mybir.AluOpType
ACT = mybir.ActivationFunctionType
AX = mybir.AxisListType

P = 128
NB, T, D = 8, 512, 256
H, DK = 16, 16
E, F = 8, 256
TB, DC = T // P, D // P
HH = 4
HG = H // HH
CH = E + 1
STEPS = 12
HEADS_STEP = (2, 4, 3, 3)
ROTATE_ON_DVE = 0
LOOP_FIRST = 2
HALF = DK // 2
TERMS = ((3, 0), (2, 1), (1, 2))
NT = sum(n for n, _ in TERMS)
KS = NT * DK
KM = KS + 3
STORES = 16 * TB // 2
LOADS = 2 * 16 * len(TERMS)
EPS = 1e-5
NEG = -3.0e38
SCALE = 1.0 / DK ** 0.5
MAX_FILLS = ((3,), (2,), (0, 1))
NF = HH * len(MAX_FILLS)
ROUND_KEYS = ((0,), (1,), (2, 3))
NR = len(ROUND_KEYS)
MOE_LAST = 4 * CH + 1


def max_fills(i):
    if i >= 8:
        return []
    return [3 * (i // 2) + 2] if i % 2 else [3 * (i // 2), 3 * (i // 2) + 1]


def moe_step(s, i):
    return (-2, STEPS * 3 + i - 3) if s == 0 else (-1, STEPS * (s - 1) + i - 3)


def ring_uses():
    uses = []
    for s in range(4):
        for i in range(STEPS):
            d, m = moe_step(s, i)
            plain = [("plain", 1 if s == 3 else 0, NF * ((s + 1) % HG) + f) for f in max_fills(i)]
            if len(plain) == 2:
                uses.append(plain.pop(0))
            if i % 2:
                uses += plain
            if m == 2:
                uses.append(("spread", d, 0))
            if s and m >= 0 and m % 4 == 3 and m // 4 + 1 < CH:
                uses.append(("spread", d, m // 4 + 1))
            if i % 2 == 0:
                uses += plain
            if i == HEADS_STEP[s]:
                uses.append(("heads", -1 if s == 0 else 0, (s - 1) % 4))
            if i == 9:
                uses.append(("maxima", 1 if s == 3 else 0, (s + 1) % 4))
            if s == 1 and i == 1:
                uses.append(("router", -1, 0))
            if s == 1 and i == 4:
                uses.append(("weights", -1, 0))
    if len(uses) % 2:
        uses.append(("nobody", 0, 0))
    return uses


class Round:

    def __init__(self, t, fixed=None):
        self.t = t
        n = t if fixed is None else fixed
        self.n = n
        self.early = 0 <= n + 2 < NB
        self.nxt = 0 <= n + 1 < NB
        self.att = 0 <= n < NB
        self.epi = 0 <= n - 1 < NB
        self.tail = 0 <= n - 2 < NB
        self.has = {2: self.early, 1: self.nxt, 0: self.att, -1: self.epi, -2: self.tail}

    def count(self, per, d, k):
        if isinstance(self.t, int):
            return min(max((self.t + d) * per + k, 0), NB * per)
        assert (LOOP_FIRST + d) * per + k > 0
        return self.t * per + (d * per + k)

    def held(self, eng, per, d, k):
        value = self.count(per, d, k)
        return value if isinstance(value, int) else eng.snap(eng.to_reg(value))


def lm_block_kernel(nc, x, table, pe, cos, sin2, wqkv, bqkv, wo, bo, wr, w1, w2, wgu, wdn, out):
    ctx = ExitStack()
    with ctx:
        def sb(name, shape, dt=F32):
            return ctx.enter_context(nc.sbuf_tensor(name, shape, dt))

        def bank(name, n=1):
            return ctx.enter_context(nc.psum_tensor(name, [P, n, 512], F32))

        def sem(name):
            return ctx.enter_context(nc.semaphore(name))

        parts_dram = nc.dram_tensor("qk_parts", (3, 4, DK, P // DK, T), BF16, kind="Internal").ap()
        base_dram = nc.dram_tensor("pe_plus_bias", (T, D), F32, kind="Internal").ap()

        ident = sb("ident", [P, P])
        identb = sb("identb", [P, P], BF16)
        causal = sb("causal", [P, T], BF16)
        cos_sb = sb("cos_sb", [P, TB, HALF])
        sin_sb = sb("sin_sb", [P, TB, DK])
        bias = sb("bias", [P, 3 * D])
        spread = sb("spread", [P, CH, P], BF16)
        iota8 = sb("iota8", [P, E])
        minus_half = sb("minus_half", [P, TB])
        wqkv_h, wqkv_l = sb("wqkv_h", [P, DC, 3 * D], F32R), sb("wqkv_l", [P, DC, 3 * D], F32R)
        wo_h, wo_l = sb("wo_h", [P, DC, D], F32R), sb("wo_l", [P, DC, D], F32R)
        wr_hl = sb("wr_hl", [P, DC, 2, E + 2], F32R)
        w1_h, w1_l = sb("w1_h", [P, DC, E, F], F32R), sb("w1_l", [P, DC, E, F], F32R)
        w2_h, w2_l = sb("w2_h", [P, DC, E, D], F32R), sb("w2_l", [P, DC, E, D], F32R)
        wgu_h, wgu_l = sb("wgu_h", [P, DC, 2 * F], F32R), sb("wgu_l", [P, DC, 2 * F], F32R)
        wdn_h, wdn_l = sb("wdn_h", [P, DC, D], F32R), sb("wdn_l", [P, DC, D], F32R)
        idx, idx_res = sb("idx", [P, TB], I32), sb("idx_res", [P, TB], I32)
        h_in = sb("h_in", [P, TB, D])
        res = sb("res", [P, TB, D])
        h1 = sb("h1", [P, TB, D])
        o_tok = sb("o_tok", [P, TB, D])
        v_new = sb("v_new", [P, TB, D])
        v_aug = sb("v_aug", [P, TB, H, DK + 1])
        stats = sb("stats", [P, TB, 6])
        mv = sb("mv", [P, TB, 2])
        var_eps = sb("var_eps", [P, TB])
        rstd = sb("rstd", [P, TB])
        a_h, a_l = sb("a_h", [P, DC, T], F32R), sb("a_l", [P, DC, T], F32R)
        x2_h, x2_l = sb("x2_h", [P, DC, T], F32R), sb("x2_l", [P, DC, T], F32R)
        split = h_in[:].rearrange("p (b k) d -> p b (k d)", b=2)
        hid = sb("hid", [P, 2, T])
        cb = sb("cb", [P, 2, T])
        parts = sb("parts", [P, 3, 4, 2 * P], BF16)
        q_terms = sb("q_terms", [P, HG, HH, T], BF16)
        k_terms = sb("k_terms", [P, HG, HH, T], BF16)
        probs0 = sb("probs0", [P, HH, T])
        probs1 = sb("probs1", [P, HH, 3 * P])
        heads_t = sb("heads_t", [P, T])
        rec = sb("rec", [P, TB, HH])
        row_max = sb("row_max", [P, TB, HH])
        max_rest = sb("max_rest", [P, TB, HH])
        max_parts = sb("max_parts", [P, TB, 3, HH], BF16)
        max_rows = sb("max_rows", [3 * HH, T], BF16)
        nmax = sb("nmax", [P, TB])
        logit_sum = sb("logit_sum", [P, TB, E + 2])
        logit = sb("logit", [P, TB, CH])
        ex = sb("ex", [P, TB, CH])
        esum = sb("esum", [P, TB])
        erec = sb("erec", [P, TB])
        pr = sb("pr", [P, TB, E])
        top8 = sb("top8", [P, TB, 8])
        top_i = sb("top_i", [P, TB, 8], U32)
        top_f = sb("top_f", [P, TB, 2])
        pick = sb("pick", [P, TB, 2, E])
        den = sb("den", [P, TB])
        cw = sb("cw", [P, TB, CH])
        cw_rest = sb("cw_rest", [P, TB, CH])
        cw_parts = sb("cw_parts", [P, TB, P], BF16)
        cw_rows = sb("cw_rows", [P, T], BF16)

        ring = bank("ring", 2)
        bank_s = bank("bank_s")
        bank_o = bank("bank_o")
        bank_fg = bank("bank_fg", 2)
        bank_y = bank("bank_y", 2)

        constants_ready = sem("constants_ready")
        tables_loaded = sem("tables_loaded")
        base_loaded = sem("base_loaded")
        pool_constants = sem("pool_constants")
        dve_constants = sem("dve_constants")
        base_stored = sem("base_stored")
        pool_filled = sem("pool_filled")
        weight_loaded = [sem(f"weight_loaded{n}") for n in range(STAGES)]
        attn_constants = sem("attn_constants")
        weight_high = sem("weight_high")
        weight_low = sem("weight_low")
        base_summed = sem("base_summed")
        x_table_loaded = sem("x_table_loaded")
        x_ids_loaded = sem("x_ids_loaded")
        x_gathered = sem("x_gathered")
        res_table_loaded = sem("res_table_loaded")
        res_ids_loaded = sem("res_ids_loaded")
        res_gathered = sem("res_gathered")
        norm1_links = sem("norm1_links")
        norm1_power = sem("norm1_power")
        norm2_links = sem("norm2_links")
        norm2_power = sem("norm2_power")
        x_turned = sem("x_turned")
        x_high = sem("x_high")
        x_low = sem("x_low")
        qkv_projected = sem("qkv_projected")
        qk_biased = sem("qk_biased")
        v_copied = sem("v_copied")
        v_ready = sem("v_ready")
        cosine_term = sem("cosine_term")
        sine_term = sem("sine_term")
        qk_rotated = sem("qk_rotated")
        qk_turned = sem("qk_turned")
        part_high = sem("part_high")
        qk_copied = sem("qk_copied")
        part_rest = sem("part_rest")
        part_middle = sem("part_middle")
        part_low = sem("part_low")
        parts_stored = [sem("parts_stored0"), sem("parts_stored1")]
        terms_loaded = [sem(f"terms_loaded{g}") for g in range(HG)]
        plain_scored = sem("plain_scored")
        maxima_taken = sem("maxima_taken")
        maxima_links = sem("maxima_links")
        maxima_turned = sem("maxima_turned")
        maxima_rows = sem("maxima_rows")
        maxima_loaded = [sem(f"maxima_loaded{g}") for g in range(HG)]
        scores_ready = sem("scores_ready")
        probs_ready = sem("probs_ready")
        probs_masked = sem("probs_masked")
        values_summed = sem("values_summed")
        heads_copied = sem("heads_copied")
        heads_turned = sem("heads_turned")
        sums_inverted = sem("sums_inverted")
        heads_divided = sem("heads_divided")
        o_turned = sem("o_turned")
        o_high = sem("o_high")
        o_low = sem("o_low")
        o_projected = sem("o_projected")
        residual_summed = sem("residual_summed")
        x2_turned = sem("x2_turned")
        x2_high = sem("x2_high")
        x2_low = sem("x2_low")
        router_scored = sem("router_scored")
        logit_links = sem("logit_links")
        router_exps = sem("router_exps")
        router_links = sem("router_links")
        router_turned = sem("router_turned")
        router_rows = sem("router_rows")
        router_spread = sem("router_spread")
        router_weights = sem("router_weights")
        up_done = sem("up_done")
        tanh_done = sem("tanh_done")
        silu_done = sem("silu_done")
        gate_done = sem("gate_done")
        hidden_weighed = sem("hidden_weighed")
        hidden_high = sem("hidden_high")
        hidden_low = sem("hidden_low")
        down_done = sem("down_done")
        y_copied = sem("y_copied")
        y_turned = sem("y_turned")
        y_rows = sem("y_rows")
        block_summed = sem("block_summed")
        out_stored = sem("out_stored")

        READ = {"plain": (maxima_taken, HG * NF), "router": (logit_links, 4), "heads": (heads_divided, HG), "weights": (router_rows, 1),
                "spread": (router_weights, CH), "maxima": (maxima_rows, HG)}
        USES = ring_uses()

        def ring_bank(use):
            return USES.index(use) % 2

        def ring_free(r, use):
            at = USES.index(use) - 2
            back = 0
            while True:
                if at < 0:
                    at += len(USES)
                    back += 1
                kind, d, k = USES[at]
                if r.n - back < -1:
                    return constants_ready, 1
                if 0 <= r.n - back + d < NB and kind in READ:
                    s, per = READ[kind]
                    return s, r.count(per, d - back, k + 1)
                at -= 2

        def rounds(eng, body):
            for n in range(-2, LOOP_FIRST):
                body(Round(n))
            with eng.Fori(LOOP_FIRST, NB - 2) as t:
                body(Round(t, fixed=LOOP_FIRST + 1))
            for n in range(NB - 2, NB + 2):
                body(Round(n))

        def seq(ap, r, d):
            if isinstance(r.t, int):
                return ap[r.t + d:r.t + d + 1]
            return ap[bass.ds(r.t + d, 1)]

        def weight_pieces():
            cut = []
            def rows(w):
                return w.rearrange("(c p) n -> p c n", p=P)
            for c in range(DC):
                cut.append((rows(wqkv)[:, c, 0:512], wqkv_h[:, c, 0:512], wqkv_l[:, c, 0:512], 512))
            cut.append((rows(wqkv)[:, :, 512:768], wqkv_h[:, :, 512:768], wqkv_l[:, :, 512:768], 512))
            cut.append((rows(wo), wo_h[:], wo_l[:], 512))
            cut.append((rows(wr), wr_hl[:, :, 0, :], wr_hl[:, :, 1, :], DC * (E + 2)))
            for c in range(DC):
                cut.append((rows(wgu)[:, c, :], wgu_h[:, c, :], wgu_l[:, c, :], 512))
            cut.append((rows(wdn), wdn_h[:], wdn_l[:], 512))
            for e in range(E):
                cut.append((rows(w1[e]), w1_h[:, :, e, :], w1_l[:, :, e, :], 512))
                cut.append((rows(w2[e]), w2_h[:, :, e, :], w2_l[:, :, e, :], 512))
            return cut

        def stage(n, width):
            home = (h1, o_tok)[n // 2 % 2]
            flat = home[:].rearrange("p k d -> p (k d)")[:, 512 * (n % 2):512 * (n % 2) + width]
            return flat if width == 512 and weight_shape(n) == 1 else flat.rearrange("p (c n) -> p c n", c=DC)

        def weight_shape(n):
            return 1 if len(weight_pieces()[n][1].shape) == 2 else 2

        block = ctx.enter_context(nc.Block())

        def cosines(r, k, engine, eng):
            eng.wait_ge(qk_biased, r.count(TB, 1, k + 1))
            eng.wait_ge(qk_turned, r.count(TB, 1, k))
            eng.wait_ge(hidden_weighed, r.count(2 * CH, -2, 2 * CH))
            cs = cos_sb[:, k, :].unsqueeze(1).unsqueeze(3).broadcast_to([P, 4 * 2, HALF, P // DK])
            engine.tensor_tensor(cb[:, 0, :].rearrange("p (c w h) -> p c w h", w=HALF, h=P // DK),
                                 hid[:, 0, :].rearrange("p (c w h) -> p c w h", w=HALF, h=P // DK), cs, ALU.mult).then_inc(cosine_term, 1)

        @block.sync
        def _(sp):
            def load_constants():
                sp.dma_start(cos_sb[:], cos.rearrange("(k p) c -> p k c", p=P)).then_inc(tables_loaded, 16)
                sp.dma_start(sin_sb[:], sin2.rearrange("(k p) c -> p k c", p=P)).then_inc(tables_loaded, 16)
                sp.dma_start(bias[:], bqkv.rearrange("(a n) -> a n", a=1).broadcast_to([P, 3 * D])).then_inc(tables_loaded, 16)
                sp.dma_start(res[:], pe.rearrange("(k p) d -> p k d", p=P)).then_inc(base_loaded, 16)
                sp.dma_start(v_new[:, 0, :], bo.rearrange("(a n) -> a n", a=1).broadcast_to([P, D])).then_inc(base_loaded, 16)
                sp.wait_ge(base_summed, 1)
                sp.dma_start(base_dram.rearrange("(k p) d -> p k d", p=P), res[:]).then_inc(base_stored, 16)

            def body(r):
                if r.att:
                    load_terms(r, 0, 3)
                if r.tail:
                    sp.wait_ge(block_summed, r.count(2, -2, 2))
                    sp.dma_start(seq(out, r, -2).rearrange("a (k p) d -> p (a k) d", p=P), o_tok[:]).then_inc(out_stored, 16)
                if r.att:
                    load_maxima(r, 0, 1)
                if r.nxt:
                    for k in range(TB):
                        sp.wait_ge(part_low, r.count(TB, 1, k + 1))
                        sp.wait_ge(part_middle, r.count(TB, 1, k + 1))
                        sp.wait_ge(part_high, r.count(TB, 1, k + 1))
                        sp.wait_ge(terms_loaded[3], r.count(LOADS, 0, LOADS))
                        cols = slice((k % 2) * P, (k % 2 + 1) * P)
                        sp.dma_start(parts_dram[:, :, :, :, k * P:(k + 1) * P].rearrange("a c i h t -> (i h) (a c) t"),
                                     parts[:, :, :, cols].rearrange("p a c t -> p (a c) t")).then_inc(parts_stored[k % 2], 16)
                    load_terms(r, 1, 0)
                if r.att:
                    load_maxima(r, 0, 2)
                if r.nxt:
                    load_terms(r, 1, 1)
                if r.early:
                    x_read, x2_read, divided = r.held(sp, 1, 2, 0), r.held(sp, 1, -1, 1), r.held(sp, TB, 2, 0)
                    sp.wait_ge(x_turned, x_read)
                    sp.wait_ge(x2_turned, x2_read)
                    sp.wait_ge(part_low, divided)
                    sp.dma_start(h_in[:], pe.rearrange("(k p) d -> p k d", p=P)).then_inc(x_table_loaded, 16)
                    sp.wait_ge(x_gathered, r.count(64, 2, 0))
                    sp.dma_start(idx[:], seq(x, r, 2).rearrange("a p k -> (a p) k")).then_inc(x_ids_loaded, 16)
                if r.n == -2:
                    load_constants()
                if r.att:
                    sp.wait_ge(residual_summed, r.count(2, 0, 0))
                    if r.n == 0:
                        sp.wait_ge(base_stored, 16)
                    sp.dma_start(res[:], base_dram.rearrange("(k p) d -> p k d", p=P)).then_inc(res_table_loaded, 16)
                    sp.wait_ge(res_gathered, r.count(64, 0, 0))
                    sp.dma_start(idx_res[:], seq(x, r, 0).rearrange("a p k -> (a p) k")).then_inc(res_ids_loaded, 16)
                    load_maxima(r, 0, 3)
                if r.nxt:
                    load_terms(r, 1, 2)
                    load_maxima(r, 1, 0)

            def load_maxima(r, d, g):
                turned, scored = r.held(sp, HG, d, g + 1), r.held(sp, HG * STEPS, d - 1, STEPS * (g + 1))
                sp.wait_ge(maxima_rows, turned)
                sp.wait_ge(scores_ready, scored)
                for a in range(3):
                    sp.dma_start(q_terms[KS + a:KS + a + 1, g, :, :], max_rows[HH * a:HH * (a + 1), :]).then_inc(maxima_loaded[g], 16)

            def load_terms(r, d, g):
                stored, scored = r.held(sp, STORES, d, STORES), r.held(sp, HG * STEPS, d - 1, STEPS * (g + 1))
                sp.wait_ge(parts_stored[0], stored)
                sp.wait_ge(parts_stored[1], stored)
                sp.wait_ge(scores_ready, scored)
                heads = slice((g % 2) * HH, (g % 2 + 1) * HH)
                j = 0
                for n, part in TERMS:
                    of_q = parts_dram[part:part + 1, g // 2, :, heads, :].broadcast_to([n, DK, HH, T])
                    of_k = parts_dram[0:n, 2 + g // 2, :, heads, :]
                    for terms, dst in ((of_q, q_terms), (of_k, k_terms)):
                        sp.dma_start(dst[DK * j:DK * (j + n), g, :, :].rearrange("p h t -> p (h t)"),
                                     terms.rearrange("a i h t -> a i (h t)")).then_inc(terms_loaded[g], 16)
                    j += n

            rounds(sp, body)
            sp.wait_ge(out_stored, 16 * NB)

        @block.tensor
        def _(pe_eng):
            t_eng = pe_eng

            def product(dst, lh, ll, rh, rl, first, last):
                t_eng.matmul(dst, lh, rh, start=first, stop=False, skip_group_check=True)
                t_eng.matmul(dst, lh, rl, start=False, stop=False, skip_group_check=True)
                return t_eng.matmul(dst, ll, rh, start=False, stop=last, skip_group_check=True)

            def high_product(dst, lh, rh, rl, first):
                t_eng.matmul(dst, lh, rh, start=first, stop=False, skip_group_check=True)
                t_eng.matmul(dst, lh, rl, start=False, stop=False, skip_group_check=True)

            def low_product(dst, ll, rh, last):
                return t_eng.matmul(dst, ll, rh, start=False, stop=last, skip_group_check=True)

            def plain_scores(r, d, g, f):
                head = f // len(MAX_FILLS)
                use = ("plain", d, NF * g + f)
                t_eng.wait_ge(terms_loaded[g], r.count(LOADS, d, LOADS))
                t_eng.wait_ge(*ring_free(r, use))
                off = 0
                for qb in MAX_FILLS[f % len(MAX_FILLS)]:
                    last = t_eng.matmul(ring[:, ring_bank(use), off:off + (qb + 1) * P], q_terms[0:KS, g, head, qb * P:(qb + 1) * P],
                                        k_terms[0:KS, g, head, 0:(qb + 1) * P], start=True, stop=True)
                    off += (qb + 1) * P
                last.then_inc(plain_scored, 1)

            def scores(r, g, i):
                t_eng.wait_ge(maxima_loaded[g], r.count(48, 0, 48))
                t_eng.wait_ge(probs_ready, r.count(HG * STEPS, 0, STEPS * g + i))
                off = 0
                for kb in ROUND_KEYS[i // HH]:
                    n = T - kb * P
                    last = t_eng.matmul(bank_s[:, 0, off:off + n], k_terms[0:KM, g, i % HH, kb * P:(kb + 1) * P],
                                        q_terms[0:KM, g, i % HH, kb * P:T], start=True, stop=True)
                    off += n
                last.then_inc(scores_ready, 1)

            def probs_v(r, d, g, rd):
                t_eng.wait_ge(probs_masked, r.count(HG * STEPS, d, STEPS * g + HH * rd + HH))
                t_eng.wait_ge(probs_ready, r.count(HG * STEPS, d, STEPS * g + HH * rd + HH))
                t_eng.wait_ge(v_ready, r.count(1, d, 1))
                if rd == 0:
                    t_eng.wait_ge(heads_copied, r.count(HG, d, g))
                buf = probs1 if rd == 1 else probs0
                off = 0
                for kb in ROUND_KEYS[rd]:
                    n = T - kb * P
                    for hh in range(HH):
                        last = t_eng.matmul(bank_o[32 * hh:32 * hh + DK + 1, 0, kb * P:T], v_aug[:, kb, HH * g + hh, :],
                                            buf[:, hh, off:off + n], start=(kb == 0), stop=(kb == TB - 1),
                                            skip_group_check=True)
                    off += n
                last.then_inc(values_summed, 1)

            def turn(dst, src, last_sem):
                for c in range(DC):
                    for k in range(TB):
                        last = t_eng.transpose(dst[:, c, k * P:(k + 1) * P], src[:, k, c * P:(c + 1) * P], ident[:])
                last.then_inc(last_sem, 1)

            def qkv(r, k):
                n = TB
                t_eng.wait_ge(x_high, r.count(2, 1, 2))
                if r.n < 0:
                    t_eng.wait_ge(weight_low, 3)
                t_eng.wait_ge(residual_summed, r.count(2, -1, 2))
                t_eng.wait_ge(silu_done, r.count(2 * CH, -2, 2 * CH))
                t_eng.wait_ge(qk_biased, r.count(n, 1, k))
                t_eng.wait_ge(v_copied, r.count(n, 1, k))
                rows = slice(k * P, (k + 1) * P)
                outs = [(bank_fg[:, 0, :], slice(0, 512)), (bank_fg[:, 1, 0:256], slice(512, 768))]
                for dst, cols in outs:
                    for c in range(DC):
                        high_product(dst, a_h[:, c, rows], wqkv_h[:, c, cols], wqkv_l[:, c, cols], c == 0)
                t_eng.wait_ge(x_low, r.count(2, 1, 2))
                for dst, cols in outs:
                    for c in range(DC):
                        last = low_product(dst, a_l[:, c, rows], wqkv_h[:, c, cols], c == DC - 1)
                last.then_inc(qkv_projected, 1)

            def turn_qk(r, k):
                if k >= 2:
                    t_eng.wait_ge(qk_copied, r.count(TB, 1, k - 1))
                    t_eng.wait_ge(part_high, r.count(TB, 1, k - 1))
                else:
                    t_eng.wait_ge(x2_high, r.count(2, -1, 2))
                    t_eng.wait_ge(x2_low, r.count(2, -1, 2))
                    t_eng.wait_ge(x_high, r.count(2, 1, 2))
                    t_eng.wait_ge(x_low, r.count(2, 1, 2))
                t_eng.wait_ge(qk_rotated, r.count(TB, 1, k + 1))
                for c in range(4):
                    last = t_eng.transpose(bank_y[:, k % 2, c * P:(c + 1) * P], cb[:, 0, c * P:(c + 1) * P], ident[:])
                last.then_inc(qk_turned, 1)

            def experts(r, d, m, part):
                c, k = m // 4, m % 4
                half = k // 2
                if part == 1 and m == 2:
                    spread_weights(r, d, 0)
                if k % 2 == 0 and c < CH:
                    i = 2 * c + half
                    if part == 0:
                        free = i if c == 0 or (c == 1 and half == 0) else i - 1
                        t_eng.wait_ge(silu_done, r.count(2 * CH, d, free))
                    if part == 0 and i == 0:
                        t_eng.wait_ge(x2_high, r.count(2, d, 2))
                        t_eng.wait_ge(x2_low, r.count(2, d, 2))
                        t_eng.wait_ge(qk_biased, r.count(TB, d + 2, TB))
                        t_eng.wait_ge(v_copied, r.count(TB, d + 2, TB))
                        t_eng.wait_ge(residual_summed, r.count(2, d, 2))
                        if r.n <= 1:
                            t_eng.wait_ge(weight_low, len(weight_pieces()))
                    cols = slice(half * P, half * P + P)
                    dc = part
                    if c == 0:
                        product(bank_fg[:, 0, :], wgu_h[:, dc, cols], wgu_l[:, dc, cols], x2_h[:, dc, :], x2_l[:, dc, :],
                                dc == 0, dc == DC - 1)
                        up = slice(F + half * P, F + half * P + P)
                        last = product(bank_fg[:, 1, :], wgu_h[:, dc, up], wgu_l[:, dc, up], x2_h[:, dc, :], x2_l[:, dc, :],
                                       dc == 0, dc == DC - 1)
                    else:
                        last = product(bank_fg[:, half, :], w1_h[:, dc, c - 1, cols], w1_l[:, dc, c - 1, cols],
                                       x2_h[:, dc, :], x2_l[:, dc, :], dc == 0, dc == DC - 1)
                    if part == 1:
                        last.then_inc(up_done, 1)
                if k % 2 == 1:
                    cc, half = (c - 1, 1) if k == 1 else (c, 0)
                    if 0 <= cc < CH:
                        i = 2 * cc + half
                        if part == 0:
                            t_eng.wait_ge(hidden_high, r.count(2 * CH, d, i + 1))
                        if part == 0 and i == 0:
                            t_eng.wait_ge(qk_copied, r.count(TB, d + 2, TB))
                            t_eng.wait_ge(part_high, r.count(TB, d + 2, TB))
                        dd = part
                        cols = slice(dd * P, dd * P + P)
                        wh, wl = (wdn_h[:, half, cols], wdn_l[:, half, cols]) if cc == 0 else \
                                 (w2_h[:, half, cc - 1, cols], w2_l[:, half, cc - 1, cols])
                        t_eng.matmul(bank_y[:, dd, :], wh, a_h[:, half, :], start=(i == 0), stop=False, skip_group_check=True)
                        t_eng.matmul(bank_y[:, dd, :], wl, a_h[:, half, :], start=False, stop=False, skip_group_check=True)
                        if part == 0:
                            t_eng.wait_ge(hidden_low, r.count(2 * CH, d, i + 1))
                        last = t_eng.matmul(bank_y[:, dd, :], wh, a_l[:, half, :], start=False, stop=(i == 2 * CH - 1),
                                            skip_group_check=True)
                        if part == 1:
                            last.then_inc(down_done, 1)
                if part == 1 and k == 3 and c + 1 < CH:
                    spread_weights(r, d, c + 1)

            def spread_weights(r, d, c):
                t_eng.wait_ge(router_rows, r.count(1, d, 1))
                t_eng.wait_ge(*ring_free(r, ("spread", d, c)))
                t_eng.matmul(ring[:, ring_bank(("spread", d, c)), :], spread[:, (c + CH - 1) % CH, :], cw_rows[:], start=True, stop=True)\
                    .then_inc(router_spread, 1)

            def body(r):
                if r.n == 0:
                    t_eng.wait_ge(attn_constants, 7)
                for s in range(4):
                    for i in range(STEPS):
                        d, m = moe_step(s, i)
                        plain_d = 1 if s == 3 else 0
                        fills = max_fills(i) if r.has[plain_d] else []
                        moe = r.has[d] and 0 <= m <= MOE_LAST
                        if len(fills) == 2:
                            plain_scores(r, plain_d, (s + 1) % HG, fills[0])
                        if moe:
                            experts(r, d, m, 0)
                        if i == 0 and r.has[-1 if s == 0 else 0]:
                            probs_v(r, -1 if s == 0 else 0, (s - 1) % HG, 2)
                        if r.att and i in (5, 9):
                            probs_v(r, 0, s, (i - 5) // 4)
                        if r.att:
                            scores(r, s, i)
                        if len(fills) == 1:
                            plain_scores(r, plain_d, (s + 1) % HG, fills[0])
                        if moe:
                            experts(r, d, m, 1)
                        if len(fills) == 2:
                            plain_scores(r, plain_d, (s + 1) % HG, fills[1])
                        if i == HEADS_STEP[s] and r.has[-1 if s == 0 else 0]:
                            hd, g = (-1, 3) if s == 0 else (0, s - 1)
                            t_eng.wait_ge(heads_copied, r.count(HG, hd, g + 1))
                            t_eng.wait_ge(*ring_free(r, ("heads", hd, g)))
                            for k in range(TB):
                                last = t_eng.transpose(ring[:, ring_bank(("heads", hd, g)), k * P:(k + 1) * P], heads_t[:, k * P:(k + 1) * P], ident[:])
                            last.then_inc(heads_turned, 1)
                        if i == 9 and r.has[plain_d]:
                            g = (s + 1) % HG
                            t_eng.wait_ge(maxima_links, r.count(4 * HG, plain_d, 4 * g + 4))
                            t_eng.wait_ge(*ring_free(r, ("maxima", plain_d, g)))
                            turned = ring[:, ring_bank(("maxima", plain_d, g)), :].bitcast(BF16)
                            for k in range(TB):
                                last = t_eng.transpose(turned[0:3 * HH, k * P:(k + 1) * P],
                                                       max_parts[:, k, :, :].rearrange("p a h -> p (a h)"), identb[:])
                            last.then_inc(maxima_turned, 1)
                        if s == 0 and i == 5 and r.epi:
                            t_eng.wait_ge(heads_divided, r.count(HG, -1, HG))
                            t_eng.wait_ge(silu_done, r.count(2 * CH, -2, 2 * CH))
                            t_eng.wait_ge(qk_biased, r.count(TB, 0, TB))
                            t_eng.wait_ge(v_copied, r.count(TB, 0, TB))
                            turn(bank_fg, o_tok, o_turned)
                        if s == 0 and i == 6 and r.tail:
                            t_eng.wait_ge(y_copied, r.count(1, -2, 1))
                            for k in range(TB):
                                for dd in range(DC):
                                    off = (k % 2) * D + dd * P
                                    last = t_eng.transpose(bank_y[:, k // 2, off:off + P], hid[:, dd, k * P:(k + 1) * P], ident[:])
                            last.then_inc(y_turned, 1)
                        if s == 0 and i == 7 and r.epi:
                            t_eng.wait_ge(o_high, r.count(2, -1, 2))
                            t_eng.wait_ge(o_low, r.count(2, -1, 2))
                            if r.n <= 1:
                                t_eng.wait_ge(weight_low, 4)
                            for k in range(TB):
                                dst = bank_fg[:, k // 2, (k % 2) * D:(k % 2 + 1) * D]
                                rows = slice(k * P, (k + 1) * P)
                                for c in range(DC):
                                    high_product(dst, a_h[:, c, rows], wo_h[:, c, :], wo_l[:, c, :], c == 0)
                                for c in range(DC):
                                    last = low_product(dst, a_l[:, c, rows], wo_h[:, c, :], c == DC - 1)
                                if k % 2:
                                    last.then_inc(o_projected, 1)
                        if s == 0 and i == 7 and r.nxt:
                            t_eng.wait_ge(norm1_links, r.count(N_OPS, 1, N_OPS))
                            t_eng.wait_ge(y_rows, r.count(1, -2, 1))
                            t_eng.wait_ge(qk_copied, r.count(TB, 0, TB))
                            t_eng.wait_ge(part_high, r.count(TB, 0, TB))
                            t_eng.wait_ge(x2_high, r.count(2, -2, 2))
                            turn(bank_y, h_in, x_turned)
                        if s == 0 and i == 10 and r.nxt:
                            qkv(r, 0)
                        if s == 0 and i == 11 and r.epi:
                            t_eng.wait_ge(norm2_links, r.count(N_OPS, -1, N_OPS))
                            t_eng.wait_ge(x_high, r.count(2, 1, 2))
                            t_eng.wait_ge(x_low, r.count(2, 1, 2))
                            t_eng.wait_ge(y_rows, r.count(1, -2, 1))
                            t_eng.wait_ge(qk_copied, r.count(TB, 0, TB))
                            t_eng.wait_ge(part_high, r.count(TB, 0, TB))
                            turn(bank_y, h_in, x2_turned)
                        if s == 1 and i < TB and r.nxt:
                            if i + 1 < TB:
                                qkv(r, i + 1)
                            turn_qk(r, i)
                        if s == 1 and i == 1 and r.epi:
                            t_eng.wait_ge(x2_high, r.count(2, -1, 2))
                            t_eng.wait_ge(x2_low, r.count(2, -1, 2))
                            if r.n <= 1:
                                t_eng.wait_ge(weight_low, 5)
                            t_eng.wait_ge(*ring_free(r, ("router", -1, 0)))
                            bank, width = ring_bank(("router", -1, 0)), 2 * (E + 2)
                            for k in range(TB):
                                rows = slice(k * P, (k + 1) * P)
                                for c in range(DC):
                                    t_eng.matmul(ring[:, bank, k * width:(k + 1) * width], x2_h[:, c, rows],
                                                 wr_hl[:, c, :, :].rearrange("p a e -> p (a e)"), start=(c == 0), stop=False,
                                                 skip_group_check=True)
                                for c in range(DC):
                                    last = t_eng.matmul(ring[:, bank, k * width:k * width + E + 2], x2_l[:, c, rows],
                                                        wr_hl[:, c, 0, :], start=False, stop=(c == DC - 1), skip_group_check=True)
                            last.then_inc(router_scored, 1)
                        if s == 1 and i == 4 and r.epi:
                            t_eng.wait_ge(router_links, r.count(CW_OPS, -1, CW_OPS))
                            t_eng.wait_ge(*ring_free(r, ("weights", -1, 0)))
                            turned = ring[:, ring_bank(("weights", -1, 0)), :].bitcast(BF16)
                            for k in range(TB):
                                last = t_eng.transpose(turned[:, k * P:(k + 1) * P], cw_parts[:, k, :], identb[:])
                            last.then_inc(router_turned, 1)

            t_eng.wait_ge(constants_ready, 1)
            rounds(t_eng, body)

        @block.scalar
        def _(act):
            def load_weight(n):
                if n >= len(weight_pieces()):
                    return
                piece, _, _, width = weight_pieces()[n]
                if n >= STAGES:
                    act.wait_ge(weight_low, n - STAGES + 1)
                act.dma_start(stage(n, width), piece).then_inc(weight_loaded[n % STAGES], 16)

            def split_weight(n):
                _, hi, _, width = weight_pieces()[n]
                act.wait_ge(weight_loaded[n % STAGES], 16 * (n // STAGES + 1))
                nc.scalar.activation(hi, stage(n, width), ACT.Copy).then_inc(weight_high, 1)
                load_weight(n + STAGES - 1)

            for n in range(STAGES - 1):
                load_weight(n)
            for n in range(FIRST_PIECES):
                split_weight(n)

            def experts(r, d, m):
                c, k = m // 4, m % 4
                i = 2 * c + k // 2
                if k % 2 == 1 and c < CH:
                    act.wait_ge(up_done, r.count(2 * CH, d, i + 1))
                    act.wait_ge(hidden_low, r.count(2 * CH, d, i - 1))
                    if i < 2:
                        act.wait_ge(hidden_low, r.count(2 * CH, d - 1, 2 * CH))
                    if i < 2:
                        act.wait_ge(qk_rotated, r.count(TB, d + 2, TB))
                    if i < 2:
                        act.wait_ge(y_turned, r.count(1, d - 1, 1))
                    nc.scalar.activation(hid[:, k // 2, :], bank_fg[:, 0 if c == 0 else k // 2, :], ACT.Tanh, scale=0.5)\
                        .then_inc(tanh_done, 1)

            def experts_high(r, d, m):
                c, k = m // 4, m % 4
                cc, half = (c, 0) if k == 2 else (c - 1, 1)
                if k % 2 == 0 and 0 <= cc < CH:
                    i = 2 * cc + half
                    act.wait_ge(hidden_weighed, r.count(2 * CH, d, i + 1))
                    act.wait_ge(down_done, r.count(2 * CH, d, i - 1))
                    if i < 2:
                        act.wait_ge(qkv_projected, r.count(TB, d + 2, TB))
                    if i < 2:
                        act.wait_ge(o_projected, r.count(2, d, 2))
                    nc.scalar.activation(a_h[:, half, :], hid[:, half, :], ACT.Copy).then_inc(hidden_high, 1)

            def weights_out(r, d, c):
                act.wait_ge(router_spread, r.count(CH, d, c + 1))
                if c >= 2:
                    act.wait_ge(hidden_weighed, r.count(2 * CH, d, 2 * (c - 1)))
                if c < 2:
                    act.wait_ge(qk_turned, r.count(TB, d + 2, TB))
                if c < 2:
                    act.wait_ge(hidden_weighed, r.count(2 * CH, d - 1, 2 * CH))
                nc.scalar.activation(cb[:, c % 2, :], ring[:, ring_bank(("spread", d, c)), :], ACT.Copy).then_inc(router_weights, 1)

            def high(src, dst, sem_out, blocks=range(DC)):
                for c in blocks:
                    nc.scalar.activation(dst[:, c, :], src[:, c, :], ACT.Copy).then_inc(sem_out, 1)

            def values(r, k):
                act.wait_ge(qkv_projected, r.count(TB, 1, k + 1))
                act.wait_ge(v_ready, r.count(1, 1, 0))
                if r.n < 0:
                    act.wait_ge(base_summed, 1)
                nc.scalar.activation(v_new[:, k, :], bank_fg[:, 1, 0:D], ACT.Copy).then_inc(v_copied, 1)

            def body(r):
                for s in range(4):
                    for i in range(STEPS):
                        d, m = moe_step(s, i)
                        moe = r.has[d] and 0 <= m <= MOE_LAST
                        if moe:
                            experts(r, d, m)
                        if moe and m != 2:
                            experts_high(r, d, m)
                        if s == 0 and i == 8 and r.nxt:
                            act.wait_ge(x_turned, r.count(1, 1, 1))
                            act.wait_ge(o_projected, r.count(2, -1, 2))
                            act.wait_ge(qkv_projected, r.count(TB, 0, TB))
                            high(bank_y, a_h, x_high, (0,))
                        if r.att:
                            buf, rd = (probs1 if i // HH == 1 else probs0), i // HH
                            g3 = NR * s
                            free = {0: g3, 1: g3 - 1, 2: g3 + 1}[rd]
                            act.wait_ge(scores_ready, r.count(HG * STEPS, 0, STEPS * s + i + 1))
                            act.wait_ge(values_summed, r.count(HG * NR, 0, free))
                            n = T if rd == 0 else 3 * P
                            nc.scalar.activation(buf[:, i % HH, 0:n], bank_s[:, 0, 0:n], ACT.Exp, scale=SCALE).then_inc(probs_ready, 1)
                        if moe and m == 2:
                            weights_out(r, d, 0)
                            experts_high(r, d, m)
                        if moe and m % 4 == 3 and m // 4 + 1 < CH:
                            weights_out(r, d, m // 4 + 1)
                        hd, hg = (-1, 3) if s == 0 else (0, s - 1)
                        if i == 0 and r.has[hd]:
                            act.wait_ge(values_summed, r.count(HG * NR, hd, NR * (hg + 1)))
                            act.wait_ge(heads_turned, r.count(HG, hd, hg))
                            nc.scalar.activation(heads_t[:], bank_o[:, 0, :], ACT.Copy).then_inc(heads_copied, 1)
                        pd = 1 if s == 3 else 0
                        if i == 9 and r.has[pd]:
                            g = (s + 1) % HG
                            act.wait_ge(maxima_turned, r.count(HG, pd, g + 1))
                            act.wait_ge(maxima_loaded[(g - 1) % HG], r.count(48, pd - (g == 0), 48))
                            turned = ring[:, ring_bank(("maxima", pd, g)), :].bitcast(BF16)
                            nc.scalar.activation(max_rows[:], turned[0:3 * HH, 0:T], ACT.Copy).then_inc(maxima_rows, 1)
                        if s == 0 and i == 5 and r.tail:
                            act.wait_ge(down_done, r.count(2 * CH, -2, 2 * CH))
                            for dd in range(DC):
                                y = nc.scalar.activation(hid[:, dd, :], bank_y[:, dd, :], ACT.Copy)
                            y.then_inc(y_copied, 1)
                        if s == 0 and i == 6 and r.tail:
                            act.wait_ge(y_turned, r.count(1, -2, 1))
                            act.wait_ge(o_turned, r.count(1, -1, 1))
                            if not r.epi:
                                act.wait_ge(out_stored, r.count(16, -2, 0))
                            for half in range(2):
                                y = nc.scalar.activation(o_tok[:, 2 * half:2 * half + 2, :],
                                                         bank_y[:, half, :].rearrange("p (k d) -> p k d", k=2), ACT.Copy)
                            y.then_inc(y_rows, 1)
                        if s == 0 and i == 5 and r.epi:
                            act.wait_ge(o_turned, r.count(1, -1, 1))
                            act.wait_ge(down_done, r.count(2 * CH, -2, 2 * CH))
                            act.wait_ge(qkv_projected, r.count(TB, 0, TB))
                            high(bank_fg, a_h, o_high)
                        if s == 0 and i == 8 and r.nxt:
                            high(bank_y, a_h, x_high, (1,))
                        if s == 0 and i == 11 and r.epi:
                            act.wait_ge(x2_turned, r.count(1, -1, 1))
                            act.wait_ge(up_done, r.count(2 * CH, -2, 2 * CH))
                            act.wait_ge(router_scored, r.count(1, -2, 1))
                            high(bank_y, x2_h, x2_high)
                        if s == 1 and i == 2 and r.epi:
                            act.wait_ge(logit_links, r.count(4, -1, 4))
                            act.wait_ge(router_links, r.count(CW_OPS, -2, CW_OPS))
                            nc.scalar.activation(ex[:], logit[:], ACT.Exp).then_inc(router_exps, 1)
                        if s == 1 and i == 4 and r.epi:
                            act.wait_ge(router_turned, r.count(1, -1, 1))
                            act.wait_ge(router_spread, r.count(CH, -2, CH))
                            turned = ring[:, ring_bank(("weights", -1, 0)), :].bitcast(BF16)
                            nc.scalar.activation(cw_rows[:], turned[:, 0:T], ACT.Copy).then_inc(router_rows, 1)
                        if s == 1 and 1 <= i <= TB and r.nxt:
                            k = i - 1
                            cols = slice((k % 2) * P, (k % 2 + 1) * P)
                            act.wait_ge(part_rest, r.count(TB, 1, k + 1))
                            act.wait_ge(parts_stored[k % 2], r.count(STORES, 1, 16 * (k // 2)))
                            nc.scalar.activation(parts[:, 1, :, cols], split[:, k % 2, :].rearrange("p (c t) -> p c t", c=4),
                                                 ACT.Copy).then_inc(part_middle, 1)
                        if s == 0 and i == 10 and r.nxt:
                            values(r, 0)
                        if s == 1 and i + 1 < TB and r.nxt:
                            values(r, i + 1)
                        if s == 1 and i < TB and r.nxt:
                            k = i
                            cols = slice((k % 2) * P, (k % 2 + 1) * P)
                            turned = bank_y[:, k % 2, :]
                            act.wait_ge(qk_turned, r.count(TB, 1, k + 1))
                            act.wait_ge(part_low, r.count(TB, 1, k - 1))
                            nc.scalar.activation(split[:, k % 2, :], turned, ACT.Copy).then_inc(qk_copied, 1)
                            act.wait_ge(parts_stored[k % 2], r.count(STORES, 1, 16 * (k // 2)))
                            nc.scalar.activation(parts[:, 0, :, cols], turned.rearrange("p (c t) -> p c t", c=4),
                                                 ACT.Copy).then_inc(part_high, 1)
                        n = FIRST_PIECES + STEPS * (s - 2) + i
                        if r.n == -1 and s >= 2 and n < len(weight_pieces()):
                            split_weight(n)

            act.wait_ge(constants_ready, 1)
            rounds(act, body)

        @block.vector
        def _(dve):
            v = nc.vector
            v.memset(causal[:], 0.0).then_inc(dve_constants, 1)
            v.memset(bank_o[:, 0, :], 0.0).then_inc(dve_constants, 1)
            dve.wait_ge(pool_constants, 3)
            dve.wait_ge(dve_constants, 2)
            dve.wait_ge(tables_loaded, 48)
            v.tensor_copy(identb[:], ident[:]).then_inc(constants_ready, 1)

            def low_weight(n):
                _, hi, lo, width = weight_pieces()[n]
                dve.wait_ge(weight_high, n + 1)
                v.tensor_tensor(lo, stage(n, width), hi.bitcast(F32), ALU.subtract).then_inc(weight_low, 1)

            for n in range(FIRST_PIECES):
                low_weight(n)

            def row_statistics(src, ks):
                for k in ks:
                    last = v.bn_stats(stats[:, k, :], src[:, k, :])
                return last

            def variances(r, d, chain):
                summed = r.held(dve, N_OPS, d, 1)
                dve.wait_ge(constants_ready, 1)
                dve.wait_ge(chain, summed)
                for k in range(TB):
                    last = v.bn_aggr(mv[:, k, :], stats[:, k, :])
                last.then_inc(chain, 1)
                dve.wait_ge(chain, r.count(N_OPS, d, 2))
                v.tensor_scalar(var_eps[:], mv[:, :, 1], EPS, None, ALU.add).then_inc(chain, 1)

            def normalise(src, chain):
                for k in range(TB):
                    last = v.tensor_scalar(h_in[:, k, :], src[:, k, :], mv[:, k, 0:1], rstd[:, k:k + 1], ALU.subtract, ALU.mult)
                last.then_inc(chain, 1)

            def low(r, d, src, hi, lo, filled, sem_out):
                for c in range(DC):
                    dve.wait_ge(filled, r.count(2, d, c + 1))
                    v.tensor_tensor(lo[:, c, :], src[:, c, :], hi[:, c, :].bitcast(F32), ALU.subtract).then_inc(sem_out, 1)

            def maxima(r, d, g, f):
                filled = r.held(dve, HG * NF, d, NF * g + f + 1)
                dve.wait_ge(constants_ready, 1)
                dve.wait_ge(plain_scored, filled)
                b, off = ring_bank(("plain", d, NF * g + f)), 0
                for qb in MAX_FILLS[f % len(MAX_FILLS)]:
                    n = (qb + 1) * P
                    last = v.tensor_tensor_reduce(ring[:, b, off:off + n], ring[:, b, off:off + n], causal[:, T - n:T], 1.0, NEG,
                                                  ALU.add, ALU.max, row_max[:, qb, f // len(MAX_FILLS):f // len(MAX_FILLS) + 1])
                    off += n
                last.then_inc(maxima_taken, 1)

            def experts(r, d, m):
                c, k = m // 4, m % 4
                if k % 2 == 1 and c < CH:
                    half, i = k // 2, 2 * c + k // 2
                    dve.wait_ge(tanh_done, r.count(2 * CH, d, i + 1))
                    op = v.scalar_tensor_tensor(out=hid[:, half, :], in0=hid[:, half, :], scalar=1.0,
                                                in1=bank_fg[:, 0 if c == 0 else half, :], op0=ALU.add, op1=ALU.mult)
                    if c == 0:
                        op.then_inc(gate_done, 1)
                        dve.wait_ge(gate_done, r.count(2, d, half + 1))
                        op = v.tensor_tensor(hid[:, half, :], hid[:, half, :], bank_fg[:, 1, :], ALU.mult)
                    op.then_inc(silu_done, 1)
                    if i > 0:
                        weigh(r, d, i)
                if m == 2:
                    weigh(r, d, 0)
                cc, half = (c, 0) if k == 2 else (c - 1, 1)
                if k % 2 == 0 and 0 <= cc < CH:
                    i = 2 * cc + half
                    dve.wait_ge(hidden_high, r.count(2 * CH, d, i + 1))
                    v.tensor_tensor(a_l[:, half, :], hid[:, half, :], a_h[:, half, :].bitcast(F32), ALU.subtract).then_inc(hidden_low, 1)

            def weigh(r, d, i):
                dve.wait_ge(silu_done, r.count(2 * CH, d, i + 1))
                dve.wait_ge(router_weights, r.count(CH, d, i // 2 + 1))
                v.tensor_tensor(hid[:, i % 2, :], hid[:, i % 2, :], cb[:, i // 2 % 2, :], ALU.mult).then_inc(hidden_weighed, 1)

            def shift_logits(r):
                both = ring[:, ring_bank(("router", -1, 0)), 0:TB * 2 * (E + 2)].rearrange("p (k a e) -> p k a e", k=TB, a=2)
                dve.wait_ge(router_scored, r.count(1, -1, 1))
                v.tensor_reduce(logit_sum[:], both.rearrange("p k a e -> p k e a"), AX.X, ALU.add).then_inc(logit_links, 1)
                dve.wait_ge(logit_links, r.count(4, -1, 1))
                v.tensor_reduce(nmax[:], logit_sum[:, :, 0:E], AX.X, ALU.max).then_inc(logit_links, 1)
                dve.wait_ge(logit_links, r.count(4, -1, 2))
                dve.wait_ge(router_exps, r.count(1, -2, 1))
                v.tensor_tensor(logit[:, :, 0:E], logit_sum[:, :, 0:E], nmax[:, :].unsqueeze(2).broadcast_to([P, TB, E]), ALU.subtract)\
                    .then_inc(logit_links, 1)
                v.tensor_scalar(logit[:, :, E:CH], logit_sum[:, :, E:CH], -1.0, None, ALU.mult).then_inc(logit_links, 1)

            def route(r, part):
                done = [0 if part == 0 else CW_FIRST]

                def link(op):
                    done[0] += 1
                    op.then_inc(router_links, 1)

                def linked():
                    dve.wait_ge(router_links, r.count(CW_OPS, -1, done[0]))

                def linked_alone():
                    so_far = r.held(dve, CW_OPS, -1, done[0])
                    dve.wait_ge(constants_ready, 1)
                    dve.wait_ge(router_links, so_far)

                if part == 0:
                    dve.wait_ge(router_exps, r.count(1, -1, 1))
                    dve.wait_ge(logit_links, r.count(4, -1, 4))
                    link(v.tensor_reduce(esum[:], ex[:, :, 0:E], AX.X, ALU.add))
                    link(v.tensor_scalar(den[:], ex[:, :, E], 1.0, None, ALU.add))
                    linked()
                    link(v.reciprocal(erec[:], esum[:]))
                    link(v.reciprocal(den[:], den[:]))
                    linked()
                    link(v.tensor_tensor(pr[:], ex[:, :, 0:E], erec[:, :].unsqueeze(2).broadcast_to([P, TB, E]), ALU.mult))
                    link(v.tensor_scalar(cw[:, :, E], den[:], 0.5, None, ALU.mult))
                    linked_alone()
                    for k in range(TB):
                        op = v.max(top8[:, k, :], pr[:, k, :])
                    link(op)
                    linked_alone()
                    for k in range(TB):
                        op = v.max_index(top_i[:, k, :], top8[:, k, :], pr[:, k, :])
                    link(op)
                    assert done[0] == CW_FIRST
                    return
                linked()
                link(v.tensor_copy(top_f[:], top_i[:, :, 0:2]))
                linked()
                link(v.tensor_tensor(pick[:], iota8[:, :].unsqueeze(1).unsqueeze(1).broadcast_to([P, TB, 2, E]),
                                     top_f[:, :, :].unsqueeze(3).broadcast_to([P, TB, 2, E]), ALU.is_equal))
                linked()
                link(v.tensor_tensor(pick[:, :, 0, :], pick[:, :, 0, :], pick[:, :, 1, :], ALU.add))
                linked()
                link(v.scalar_tensor_tensor(out=cw[:, :, 0:E], in0=pick[:, :, 0, :], scalar=0.5, in1=pr[:], op0=ALU.mult, op1=ALU.mult))
                linked()
                dve.wait_ge(router_turned, r.count(1, -2, 1))
                if r.n <= 1:
                    dve.wait_ge(attn_constants, 7)
                link(v.tensor_copy(cw_parts[:, :, 0:CH], cw[:]))
                linked()
                link(v.tensor_tensor(cw_rest[:], cw[:], cw_parts[:, :, 0:CH], ALU.subtract))
                linked()
                link(v.tensor_copy(cw_parts[:, :, CH:2 * CH], cw_rest[:]))
                linked()
                link(v.tensor_tensor(cw_parts[:, :, 2 * CH:3 * CH], cw_rest[:], cw_parts[:, :, CH:2 * CH], ALU.subtract))
                assert done[0] == CW_OPS

            def body(r):
                for s in range(4):
                    for i in range(STEPS):
                        d, m = moe_step(s, i)
                        pd, pg = (1 if s == 3 else 0), (s + 1) % HG
                        fills = max_fills(i) if r.has[pd] else []
                        if len(fills) == 2:
                            maxima(r, pd, pg, fills[0])
                        moe = r.has[d] and 0 <= m <= MOE_LAST
                        if s == 0 and i == 6 and r.epi:
                            low(r, -1, bank_fg, a_h, a_l, o_high, o_low)
                        if moe and m != 2:
                            experts(r, d, m)
                        if fills:
                            maxima(r, pd, pg, fills[-1])
                        if moe and m == 2:
                            experts(r, d, m)
                        if s == 1 and i < TB and r.nxt:
                            rotated(r, i)
                            if i + 1 < TB:
                                biased(r, i + 1)
                        if s == 1 and i == 1 and r.epi:
                            shift_logits(r)
                        if s == 1 and i == 2 and r.epi:
                            route(r, 0)
                        if s == 1 and i == 3 and r.epi:
                            route(r, 1)
                        if i == 7 and r.has[pd]:
                            n = 4 * HG
                            dve.wait_ge(maxima_taken, r.count(HG * NF, pd, NF * (pg + 1)))
                            dve.wait_ge(maxima_turned, r.count(HG, pd, pg))
                            v.tensor_scalar(max_parts[:, :, 0, :], row_max[:], -1.0, None, ALU.mult).then_inc(maxima_links, 1)
                            dve.wait_ge(maxima_links, r.count(n, pd, 4 * pg + 1))
                            v.scalar_tensor_tensor(out=max_rest[:], in0=row_max[:], scalar=-1.0, in1=max_parts[:, :, 0, :],
                                                   op0=ALU.mult, op1=ALU.subtract).then_inc(maxima_links, 1)
                            dve.wait_ge(maxima_links, r.count(n, pd, 4 * pg + 2))
                            v.tensor_copy(max_parts[:, :, 1, :], max_rest[:]).then_inc(maxima_links, 1)
                            dve.wait_ge(maxima_links, r.count(n, pd, 4 * pg + 3))
                            v.tensor_tensor(max_parts[:, :, 2, :], max_rest[:], max_parts[:, :, 1, :], ALU.subtract).then_inc(maxima_links, 1)
                        hd, hg = (-1, 3) if s == 0 else (0, s - 1)
                        if i == HEADS_STEP[s] and r.has[hd]:
                            ht = ring[:, ring_bank(("heads", hd, hg)), :].rearrange("p (k h w) -> p k h w", k=TB, h=HH)
                            dve.wait_ge(heads_turned, r.count(HG, hd, hg + 1))
                            v.reciprocal(rec[:], ht[:, :, :, DK]).then_inc(sums_inverted, 1)
                            dve.wait_ge(sums_inverted, r.count(HG, hd, hg + 1))
                            dve.wait_ge(o_turned, r.count(1, hd, 0))
                            if s == 1:
                                dve.wait_ge(out_stored, r.count(16, -2, 16))
                            if r.n == 0:
                                dve.wait_ge(weight_low, len(weight_pieces()))
                            v.tensor_tensor(o_tok[:, :, hg * HH * DK:(hg + 1) * HH * DK].rearrange("p k (h w) -> p k h w", h=HH),
                                            ht[:, :, :, 0:DK], rec[:].unsqueeze(3).broadcast_to([P, TB, HH, DK]), ALU.mult)\
                                .then_inc(heads_divided, 1)
                        if s == 3 and i == 8 and r.early:
                            dve.wait_ge(x_gathered, r.count(64, 2, 64))
                            row_statistics(h_in, range(TB)).then_inc(norm1_links, 1)
                            variances(r, 2, norm1_links)
                        if s == 3 and i == 10 and r.early:
                            dve.wait_ge(norm1_power, r.count(1, 2, 1))
                            normalise(h_in, norm1_links)
                        if s == 0 and i == 7 and r.epi:
                            dve.wait_ge(res_gathered, r.count(64, -1, 64))
                            if r.n <= 1:
                                dve.wait_ge(weight_low, len(weight_pieces()))
                            for half in range(2):
                                ks = slice(2 * half, 2 * half + 2)
                                dve.wait_ge(o_projected, r.count(2, -1, half + 1))
                                dve.wait_ge(block_summed, r.count(2, -2, half + 1))
                                v.tensor_tensor(h1[:, ks, :], bank_fg[:, half, :].rearrange("p (k d) -> p k d", k=2),
                                                res[:, ks, :], ALU.add).then_inc(residual_summed, 1)
                                dve.wait_ge(residual_summed, r.count(2, -1, half + 1))
                                last = row_statistics(h1, (2 * half, 2 * half + 1))
                            last.then_inc(norm2_links, 1)
                            variances(r, -1, norm2_links)
                        if s == 0 and i == 8 and r.nxt:
                            low(r, 1, bank_y, a_h, a_l, x_high, x_low)
                        if s == 0 and i == 9 and r.epi:
                            dve.wait_ge(norm2_power, r.count(1, -1, 1))
                            dve.wait_ge(x_turned, r.count(1, 1, 1))
                            normalise(h1, norm2_links)
                        if s == 0 and i == 11 and r.epi:
                            low(r, -1, bank_y, x2_h, x2_l, x2_high, x2_low)
                        if s == 0 and i == 10 and r.nxt:
                            biased(r, 0)
                        if r.n == -2 and s == 3 and i == 11:
                            dve.wait_ge(base_loaded, 32)
                            v.tensor_tensor(res[:], res[:], v_new[:, 0:1, :].broadcast_to([P, TB, D]), ALU.add).then_inc(base_summed, 1)
                        n = FIRST_PIECES + STEPS * (s - 2) + i
                        if r.n == -1 and s >= 2 and n < len(weight_pieces()):
                            low_weight(n)

            def biased(r, k):
                dve.wait_ge(qkv_projected, r.count(TB, 1, k + 1))
                dve.wait_ge(y_turned, r.count(1, -2, 1))
                dve.wait_ge(qk_rotated, r.count(TB, 1, k))
                dve.wait_ge(hidden_low, r.count(2 * CH, -2, 2 * CH))
                v.tensor_tensor(hid[:, 0, :], bank_fg[:, 0, :], bias[:, 0:2 * D], ALU.add).then_inc(qk_biased, 1)
                dve.wait_ge(qk_biased, r.count(TB, 1, k + 1))
                x = hid[:, 0, :].rearrange("p (c a w h) -> p c a w h", c=4, a=2, w=HALF)
                y = hid[:, 1, :].rearrange("p (c a w h) -> p c a w h", c=4, a=2, w=HALF)
                for a in range(2):
                    sn = sin_sb[:, k, a * HALF:(a + 1) * HALF].unsqueeze(1).unsqueeze(3)
                    op = v.tensor_tensor(y[:, :, a], x[:, :, 1 - a], sn.broadcast_to([P, 4, HALF, P // DK]), ALU.mult)
                op.then_inc(sine_term, 1)
                if r.n <= ROTATE_ON_DVE:
                    cosines(r, k, v, dve)

            def rotated(r, k):
                dve.wait_ge(sine_term, r.count(TB, 1, k + 1))
                dve.wait_ge(cosine_term, r.count(TB, 1, k + 1))
                v.tensor_tensor(cb[:, 0, :], cb[:, 0, :], hid[:, 1, :], ALU.add).then_inc(qk_rotated, 1)

            rounds(dve, body)

        @block.gpsimd
        def _(pool):
            g = nc.gpsimd
            g.memset(ident[:], 0.0).then_inc(pool_filled, 1)
            g.memset(minus_half[:], -0.5).then_inc(pool_filled, 1)
            pool.wait_ge(pool_filled, 2)
            g.affine_select(out=ident[:], in_=ident[:], compare_op=ALU.not_equal, fill=1.0, base=0,
                            pattern=[[-1, P]], channel_multiplier=1).then_inc(pool_constants, 1)
            g.iota(iota8[:], pattern=[[1, E]], base=0, channel_multiplier=0,
                   allow_small_or_imprecise_dtypes=True).then_inc(pool_constants, 1)
            pool.wait_ge(dve_constants, 1)
            last = causal[:, T - P:T]
            g.affine_select(out=last, in_=last, compare_op=ALU.is_ge, fill=NEG, base=0,
                            pattern=[[-1, P]], channel_multiplier=1).then_inc(pool_constants, 1)

            def attention_constants():
                g.memset(spread[:], 0.0).then_inc(attn_constants, 1)
                g.memset(v_aug[:], 1.0).then_inc(attn_constants, 1)
                g.memset(cw_parts[:], 0.0).then_inc(attn_constants, 1)
                pool.wait_ge(attn_constants, 3)
                g.memset(k_terms[KS:P, :, :, :].rearrange("p g h t -> p (g h t)"), 1.0).then_inc(attn_constants, 1)
                for a in range(3):
                    pool.wait_ge(attn_constants, 4 + a)
                    g.affine_select(out=spread[:], in_=spread[:], compare_op=ALU.not_equal, fill=1.0, base=-CH * a,
                                    pattern=[[-1, CH], [0, P]], channel_multiplier=1).then_inc(attn_constants, 1)

            def gather(r, d, dst, tab, ids, row_ids, done):
                here = r.held(pool, 16, d, 16)
                if r.n > -2:
                    pool.wait_ge(constants_ready, 1)
                pool.wait_ge(tab, here)
                pool.wait_ge(ids, here)
                for k in range(TB):
                    g.indirect_dma_start(out=dst[:, k, :], out_offset=None, in_=table,
                                         in_offset=bass.IndirectOffsetOnAxis(ap=row_ids[:, k:k + 1], axis=0),
                                         compute_op=ALU.add).then_inc(done, 16)

            def power(r, d, chain, pooled):
                pool.wait_ge(chain, r.count(N_OPS, d, 3))
                g.tensor_tensor(rstd[:], var_eps[:], minus_half[:], ALU.pow).then_inc(pooled, 1)

            def body(r):
                if r.n == -1:
                    pool.wait_ge(constants_ready, 1)
                for s in range(4):
                    for i in range(STEPS):
                        if s == 0 and i == 1 and r.att:
                            projected, used = r.held(pool, TB, 0, TB), r.held(pool, HG * NR, 0, 0)
                            pool.wait_ge(constants_ready, 1)
                            pool.wait_ge(v_copied, projected)
                            pool.wait_ge(values_summed, used)
                            if r.n == 0:
                                pool.wait_ge(attn_constants, 7)
                            v_bias = bias[:, 2 * D:3 * D].rearrange("p (h w) -> p h w", h=H).unsqueeze(1)
                            g.tensor_tensor(v_aug[:, :, :, 0:DK], v_new[:].rearrange("p k (h w) -> p k h w", h=H),
                                            v_bias.broadcast_to([P, TB, H, DK]), ALU.add).then_inc(v_ready, 1)
                        if s == 0 and i == 6 and r.tail:
                            pool.wait_ge(y_rows, r.count(1, -2, 1))
                            pool.wait_ge(residual_summed, r.count(2, -2, 2))
                            for half in range(2):
                                ks = slice(2 * half, 2 * half + 2)
                                g.tensor_tensor(o_tok[:, ks, :], o_tok[:, ks, :], h1[:, ks, :], ALU.add).then_inc(block_summed, 1)
                        if s == 2 and i == 8 and r.early:
                            gather(r, 2, h_in, x_table_loaded, x_ids_loaded, idx, x_gathered)
                        if r.att:
                            rd, head = i // HH, i % HH
                            buf = probs1 if rd == 1 else probs0
                            written = r.held(pool, HG * STEPS, 0, STEPS * s + i + 1)
                            pool.wait_ge(constants_ready, 1)
                            pool.wait_ge(probs_ready, written)
                            if rd == 2:
                                blk = buf[:, head, 0:T].rearrange("p (a c) -> p a c", a=2)[:, :, 0:P]
                                pattern = [[0, 2], [1, P]]
                            else:
                                blk = buf[:, head, 0:P]
                                pattern = [[1, P]]
                            g.affine_select(out=blk, in_=blk, compare_op=ALU.is_ge, fill=0.0, base=0,
                                            pattern=pattern, channel_multiplier=-1).then_inc(probs_masked, 1)
                        if s == 3 and i == 8 and r.early:
                            power(r, 2, norm1_links, norm1_power)
                        if r.n == -2 and s == 3 and i == 11:
                            attention_constants()
                        if s == 0 and i == 7 and r.epi:
                            power(r, -1, norm2_links, norm2_power)
                        if s == 1 and 1 <= i <= TB and r.nxt:
                            k = i - 1
                            cols = slice((k % 2) * P, (k % 2 + 1) * P)
                            pool.wait_ge(part_middle, r.count(TB, 1, k + 1))
                            g.tensor_tensor(parts[:, 2, :, cols], split[:, k % 2, :].rearrange("p (c t) -> p c t", c=4),
                                            parts[:, 1, :, cols], ALU.subtract).then_inc(part_low, 1)
                        k = {(0, 11): 0, (1, 0): 1, (1, 1): 2, (1, 2): 3}.get((s, i))
                        if k is not None and r.nxt and r.n > ROTATE_ON_DVE:
                            cosines(r, k, g, pool)
                        if s == 1 and i < TB and r.nxt:
                            k = i
                            cols = slice((k % 2) * P, (k % 2 + 1) * P)
                            rest = split[:, k % 2, :].rearrange("p (c t) -> p c t", c=4)
                            pool.wait_ge(qk_copied, r.count(TB, 1, k + 1))
                            pool.wait_ge(part_high, r.count(TB, 1, k + 1))
                            g.tensor_tensor(rest, rest, parts[:, 0, :, cols], ALU.subtract).then_inc(part_rest, 1)
                        if s == 2 and i == 4 and r.att:
                            gather(r, 0, res, res_table_loaded, res_ids_loaded, idx_res, res_gathered)

            rounds(pool, body)


N_OPS = 4
CW_OPS, CW_FIRST = 16, 8
FIRST_PIECES = 3
STAGES = 4


def tables():
    import numpy as np
    f = np.float32
    pos = np.arange(T, dtype=f)[:, None]
    i = np.arange(D // 2, dtype=f)[None, :]
    ang = (pos / np.power(f(10000.0), f(2.0) * i / f(D))).astype(f)
    pe = np.zeros((T, D), f)
    pe[:, 0::2], pe[:, 1::2] = np.sin(ang), np.cos(ang)
    freq = f(1.0) / np.power(f(10000.0), f(2.0) * np.arange(HALF, dtype=f) / f(DK))
    rot = (pos * freq[None, :]).astype(f)
    return pe, np.cos(rot).astype(f), np.concatenate([-np.sin(rot), np.sin(rot)], 1).astype(f)


def kernel(**inputs):
    import numpy as np
    import concourse.bacc as bacc
    from concourse.bass_utils import run_bass_kernel_spmd as run

    a = {k: np.asarray(v) for k, v in inputs.items()}
    pe, cos, sin2 = tables()

    def by_width(w):
        return w.reshape(-1, D // P, P // DK, DK).transpose(0, 1, 3, 2).reshape(w.shape)
    layout = {
        "x": a["x"].reshape(NB, TB, P).transpose(0, 2, 1),
        "table": a["L0_tok_W"],
        "pe": pe, "cos": cos, "sin2": sin2,
        "wqkv": np.concatenate([by_width(a["L0_attn_WQ_w"].T), by_width(a["L0_attn_WK_w"].T), a["L0_attn_WV_w"].T], axis=1),
        "bqkv": np.concatenate([by_width(a["L0_attn_WQ_b"]), by_width(a["L0_attn_WK_b"]), a["L0_attn_WV_b"]]),
        "wo": a["L0_attn_Wo_w"].T,
        "bo": a["L0_attn_Wo_b"],
        "wr": np.concatenate([a["L0_ffn_router_w"], a["L0_ffn_shared_gate_w"], np.zeros((D, 1), np.float32)], axis=1),
        "w1": a["L0_ffn_w1"], "w2": a["L0_ffn_w2"],
        "wgu": a["L0_ffn_shared_gate_up"], "wdn": a["L0_ffn_shared_down"],
    }
    nc = bacc.Bacc("TRN2", target_bir_lowering=False, num_devices=1)
    arrays, args = {}, []
    for name, value in layout.items():
        value = np.ascontiguousarray(value)
        arrays["in_" + name] = value
        args.append(nc.dram_tensor("in_" + name, value.shape, mybir.dt.from_np(value.dtype), kind="ExternalInput").ap())
    out = nc.dram_tensor("out_0", (NB, T, D), F32, kind="ExternalOutput").ap()
    lm_block_kernel(nc, *args, out)
    r = run(nc, [arrays], core_ids=[0])
    return r.results[0]["out_0"]
```
